# Optimizing a Trainium2 kernel written in Bass

```python
import numpy as np
import jax
import jax.numpy as jnp

def _softmax(x, axis=-1):
    return jax.nn.softmax(x, axis=axis)

def _gelu(x):
    return jax.nn.gelu(x, approximate=True)

def _silu(x):
    return jax.nn.silu(x)

def _sigmoid(x):
    return jax.nn.sigmoid(x)

def _layernorm(x, axis=-1, eps=1e-05):
    m = jnp.mean(x, axis=axis, keepdims=True)
    v = jnp.var(x, axis=axis, keepdims=True)
    return (x - m) / jnp.sqrt(v + eps)

def _scatter_add(tgt, idx, src, axis=0):
    return tgt.at[idx].add(src)

def _segment_sum(src, seg, n):
    return jax.ops.segment_sum(src, seg, n)
kernel_name = 'mk_perceiver_d2_seqx_r4_209206'

def setup_inputs(seed: int=0):
    np.random.seed(seed)
    _w = jnp.asarray

    def _rec_inputs():
        import jax
        import jax.numpy as jnp
        _rk = jax.random.key(seed)
        x = 7.22e-05 + 1 * jax.random.normal(jax.random.fold_in(_rk, 1), (128, 32, 256), jnp.float32)
        _lenS = 32 - jax.random.randint(jax.random.fold_in(_rk, 7), (128,), 0, max(1, 32 // 4) + 1, jnp.int32)
        _lenS2 = 257 - jax.random.randint(jax.random.fold_in(_rk, 8), (128,), 0, max(1, 257 // 4) + 1, jnp.int32)
        _ctx_1024P = jax.random.normal(jax.random.fold_in(_rk, 11), (128, 16, 256), jnp.float32)
        _ctx_1024c = jax.random.dirichlet(jax.random.fold_in(_rk, 511), 0.3 * jnp.ones((16,), jnp.float32), (128, 257))
        _ctx_1024t = jnp.einsum('bsk,bkd->bsd', _ctx_1024c, _ctx_1024P)
        _ctx_1024t = _ctx_1024t * jax.lax.rsqrt(jnp.mean(jnp.square(_ctx_1024t)) + 1e-12) * 0.953939
        ctx_1024 = -1.52775e-05 + 0.999936 * (_ctx_1024t + 0.3 * jax.random.normal(jax.random.fold_in(_rk, 611), (128, 257, 256), jnp.float32))
        return (x, ctx_1024)
    x, ctx_1024 = _rec_inputs()

    def _L0_xattn_setup():
        import math
        import jax, jax.numpy as jnp
        import numpy as np
        B, TQ, TK, D = (4, 512, 2048, 256)
        N_HEAD = 16
        STRIDE = 16
        key = jax.random.key(seed)
        ks = jax.random.split(key, 7)
        w_scale = 0.02
        return {'q': jax.random.normal(ks[0], (B, TQ, D), jnp.float32), 'k': jax.random.normal(ks[1], (B, TK, D), jnp.float32), 'v': jax.random.normal(ks[2], (B, TK, D), jnp.float32), 'Wq': jax.random.normal(ks[3], (D, D), jnp.float32) * w_scale, 'bq': jnp.zeros((D,), jnp.float32), 'Wk': jax.random.normal(ks[4], (D, D), jnp.float32) * w_scale, 'bk': jnp.zeros((D,), jnp.float32), 'Wv': jax.random.normal(ks[5], (D, D), jnp.float32) * w_scale, 'bv': jnp.zeros((D,), jnp.float32), 'Wo': jax.random.normal(ks[6], (D, D), jnp.float32) * w_scale, 'bo': jnp.zeros((D,), jnp.float32)}
    _L0_xattn_all = _L0_xattn_setup()
    _L0_xattn_in = {k: v for k, v in _L0_xattn_all.items() if k in ('Wq', 'bq', 'Wk', 'bk', 'Wv', 'bv', 'Wo', 'bo')}
    del _L0_xattn_all

    def _L0_attn_setup():
        import jax, jax.numpy as jnp
        import numpy as np
        H = 16

        def _pairwise_l2(pos):
            sq = jnp.sum((pos[:, :, None, :] - pos[:, None, :, :]) ** 2, axis=-1)
            safe = jnp.where(sq > 0, sq, 1.0)
            return jnp.where(sq > 0, jnp.sqrt(safe), 0.0)
        key = jax.random.key(seed)
        ks = jax.random.split(key, 12)
        B, S, D = (2, 512, 256)
        init = lambda k, shape: jax.random.normal(k, shape, dtype=jnp.float32) * 0.02
        return {'x': jax.random.normal(ks[0], (B, S, D), dtype=jnp.float32), 'wq': init(ks[1], (D, D)), 'bq': init(ks[2], (D,)), 'wk': init(ks[3], (D, D)), 'bk': init(ks[4], (D,)), 'wv': init(ks[5], (D, D)), 'bv': init(ks[6], (D,)), 'wo': init(ks[7], (D, D)), 'bo': init(ks[8], (D,)), 'w3d': init(ks[9], (3, D)), 'b3d': init(ks[10], (3,))}
    _L0_attn_all = _L0_attn_setup()
    _L0_attn_in = {k: v for k, v in _L0_attn_all.items() if k in ('wq', 'bq', 'wk', 'bk', 'wv', 'bv', 'wo', 'bo', 'w3d', 'b3d')}
    del _L0_attn_all

    def _L0_ffn_setup():
        import jax, jax.numpy as jnp
        import numpy as np
        D, H, O, E, K = (256, 512, 256, 8, 2)
        B, S = (4, 256)
        key = jax.random.key(seed)
        ks = jax.random.split(key, 8)
        scale = 0.02
        return {'hidden_states': jax.random.normal(ks[0], (B, S, D), jnp.float32), 'router_w': jax.random.normal(ks[1], (E, D), jnp.float32) * scale, 'sg': jax.random.normal(ks[2], (H, D), jnp.float32) * scale, 'su': jax.random.normal(ks[3], (H, D), jnp.float32) * scale, 'sd': jax.random.normal(ks[4], (O, H), jnp.float32) * scale, 'eg': jax.random.normal(ks[5], (E, H, D), jnp.float32) * scale, 'eu': jax.random.normal(ks[6], (E, H, D), jnp.float32) * scale, 'ed': jax.random.normal(ks[7], (E, O, H), jnp.float32) * scale}
    _L0_ffn_all = _L0_ffn_setup()
    _L0_ffn_in = {k: v for k, v in _L0_ffn_all.items() if k in ('router_w', 'sg', 'su', 'sd', 'eg', 'eu', 'ed')}
    del _L0_ffn_all

    def _L1_xattn_setup():
        import jax, jax.numpy as jnp
        import numpy as np
        B, S, D, DFF = (4, 512, 256, 1024)
        EPS = 1e-05

        def layernorm(x, gamma, beta):
            mu = jnp.mean(x, axis=-1, keepdims=True)
            var = jnp.var(x, axis=-1, keepdims=True)
            return (x - mu) * jax.lax.rsqrt(var + EPS) * gamma + beta

        def attention(Q, K, V, causal):
            d_k = Q.shape[-1]
            scores = jnp.einsum('bqd,bkd->bqk', Q, K) / jnp.sqrt(jnp.asarray(d_k, Q.dtype))
            if causal:
                q_len, k_len = (scores.shape[-2], scores.shape[-1])
                mask = jnp.tril(jnp.ones((q_len, k_len), dtype=bool))
                scores = jnp.where(mask[None], scores, jnp.asarray(-jnp.inf, scores.dtype))
            w = jax.nn.softmax(scores, axis=-1)
            return jnp.einsum('bqk,bkd->bqd', w, V)
        key = jax.random.key(seed)
        ks = jax.random.split(key, 12)
        sd = 0.02
        return {'y': jax.random.normal(ks[0], (B, S, D), jnp.float32), 'Z': jax.random.normal(ks[1], (B, S, D), jnp.float32), 'w1': jax.random.normal(ks[2], (D, DFF), jnp.float32) * sd, 'b1': jnp.zeros((DFF,), jnp.float32), 'w2': jax.random.normal(ks[3], (DFF, D), jnp.float32) * sd, 'b2': jnp.zeros((D,), jnp.float32), 'g1': jnp.ones((D,), jnp.float32), 'beta1': jnp.zeros((D,), jnp.float32), 'g2': jnp.ones((D,), jnp.float32), 'beta2': jnp.zeros((D,), jnp.float32), 'g3': jnp.ones((D,), jnp.float32), 'beta3': jnp.zeros((D,), jnp.float32)}
    _L1_xattn_all = _L1_xattn_setup()
    _L1_xattn_in = {k: v for k, v in _L1_xattn_all.items() if k in ('w1', 'b1', 'w2', 'b2', 'g1', 'beta1', 'g2', 'beta2', 'g3', 'beta3')}
    del _L1_xattn_all

    def _L1_attn_setup():
        import jax, jax.numpy as jnp
        import numpy as np
        B, N, DM, H, FF = (8, 512, 256, 16, 1024)
        D = DM // H // 2
        LAMBDA_INIT = 0.8 - 0.6 * float(np.exp(-0.3 * 1.0))

        def _layernorm(x, g, b, eps=1e-05):
            mu = jnp.mean(x, axis=-1, keepdims=True)
            var = jnp.mean(jnp.square(x - mu), axis=-1, keepdims=True)
            return (x - mu) * jax.lax.rsqrt(var + eps) * g + b

        def _rmsnorm(x, eps=1e-05):
            return x * jax.lax.rsqrt(jnp.mean(x * x, axis=-1, keepdims=True) + eps)

        def _diff_attn(x, Wq, Wk, Wv, lq1, lq2, lk1, lk2, Wo, bo):
            b, n, d = x.shape
            scale = D ** (-0.5)
            q = (x @ Wq.T).reshape(b, n, H, D, 2).transpose(0, 1, 4, 2, 3).reshape(b, n, 2 * H, D) * scale
            k = (x @ Wk.T).reshape(b, n, H, D, 2).transpose(0, 1, 4, 2, 3).reshape(b, n, 2 * H, D)
            v = (x @ Wv.T).reshape(b, n, H, 2 * D).transpose(0, 2, 1, 3)
            att = jnp.einsum('bnqd,bnkd->bnqk', q, k)
            att = jnp.nan_to_num(att)
            att = jax.nn.softmax(att.astype(jnp.float32), axis=-1)
            lam = jnp.exp(jnp.sum(lq1 * lk1)) - jnp.exp(jnp.sum(lq2 * lk2)) + LAMBDA_INIT
            att6 = att.reshape(b, n, 2, H, 2, H)
            att2 = att6[:, :, 0, :, 0, :] - lam * att6[:, :, 1, :, 1, :]
            out = jnp.einsum('bnah,bhnd->bnad', att2, v)
            out = _rmsnorm(out) * (1.0 - LAMBDA_INIT)
            out = out.reshape(b, n, d)
            return out @ Wo.T + bo
        key = jax.random.key(seed)
        ks = jax.random.split(key, 12)
        p = lambda k, sh, s=0.02: jax.random.normal(k, sh, jnp.float32) * s
        return {'x': jax.random.normal(ks[0], (B, N, DM), jnp.float32), 'Wq': p(ks[1], (DM, DM)), 'Wk': p(ks[2], (DM, DM)), 'Wv': p(ks[3], (DM, DM)), 'lq1': p(ks[4], (D,), 0.1), 'lq2': p(ks[5], (D,), 0.1), 'lk1': p(ks[6], (D,), 0.1), 'lk2': p(ks[7], (D,), 0.1), 'Wo': p(ks[8], (DM, DM)), 'bo': jnp.zeros((DM,), jnp.float32), 'ln1_g': jnp.ones((DM,), jnp.float32), 'ln1_b': jnp.zeros((DM,), jnp.float32), 'ln2_g': jnp.ones((DM,), jnp.float32), 'ln2_b': jnp.zeros((DM,), jnp.float32), 'W1': p(ks[9], (FF, DM)), 'b1': jnp.zeros((FF,), jnp.float32), 'W2': p(ks[10], (DM, FF)), 'b2': jnp.zeros((DM,), jnp.float32)}
    _L1_attn_all = _L1_attn_setup()
    _L1_attn_in = {k: v for k, v in _L1_attn_all.items() if k in ('Wq', 'Wk', 'Wv', 'lq1', 'lq2', 'lk1', 'lk2', 'Wo', 'bo', 'ln1_g', 'ln1_b', 'ln2_g', 'ln2_b', 'W1', 'b1', 'W2', 'b2')}
    del _L1_attn_all

    def _L1_ffn_setup():
        import jax, jax.numpy as jnp
        import numpy as np
        HEADS = 8
        DIM = 256
        DIM_KEY = 128
        NUM_KEYS = 64
        TOPK = 16
        key = jax.random.key(seed)
        k1, k2, k3, k4, k5 = jax.random.split(key, 5)
        b, n = (4, 512)
        x = jax.random.normal(k1, (b, n, DIM), dtype=jnp.float32)
        Wq = jax.random.normal(k2, (2 * HEADS * DIM_KEY, DIM), dtype=jnp.float32) * 0.02
        keys = jax.random.normal(k3, (HEADS, NUM_KEYS, 2, DIM_KEY), dtype=jnp.float32)
        W_down = jax.random.normal(k4, (16384, DIM), dtype=jnp.float32)
        W_up = jax.random.normal(k5, (16384, DIM), dtype=jnp.float32)
        return {'x': x, 'Wq': Wq, 'keys': keys, 'W_down': W_down, 'W_up': W_up}
    _L1_ffn_all = _L1_ffn_setup()
    _L1_ffn_in = {k: v for k, v in _L1_ffn_all.items() if k in ('Wq', 'keys', 'W_down', 'W_up')}
    del _L1_ffn_all
    return {'x': x, 'ctx_1024': ctx_1024, 'L0_xattn_Wq': _L0_xattn_in['Wq'], 'L0_xattn_bq': _L0_xattn_in['bq'], 'L0_xattn_Wk': _L0_xattn_in['Wk'], 'L0_xattn_bk': _L0_xattn_in['bk'], 'L0_xattn_Wv': _L0_xattn_in['Wv'], 'L0_xattn_bv': _L0_xattn_in['bv'], 'L0_xattn_Wo': _L0_xattn_in['Wo'], 'L0_xattn_bo': _L0_xattn_in['bo'], 'L0_attn_wq': _L0_attn_in['wq'], 'L0_attn_bq': _L0_attn_in['bq'], 'L0_attn_wk': _L0_attn_in['wk'], 'L0_attn_bk': _L0_attn_in['bk'], 'L0_attn_wv': _L0_attn_in['wv'], 'L0_attn_bv': _L0_attn_in['bv'], 'L0_attn_wo': _L0_attn_in['wo'], 'L0_attn_bo': _L0_attn_in['bo'], 'L0_attn_w3d': _L0_attn_in['w3d'], 'L0_attn_b3d': _L0_attn_in['b3d'], 'L0_ffn_router_w': _L0_ffn_in['router_w'], 'L0_ffn_sg': _L0_ffn_in['sg'], 'L0_ffn_su': _L0_ffn_in['su'], 'L0_ffn_sd': _L0_ffn_in['sd'], 'L0_ffn_eg': _L0_ffn_in['eg'], 'L0_ffn_eu': _L0_ffn_in['eu'], 'L0_ffn_ed': _L0_ffn_in['ed'], 'L1_xattn_w1': _L1_xattn_in['w1'], 'L1_xattn_b1': _L1_xattn_in['b1'], 'L1_xattn_w2': _L1_xattn_in['w2'], 'L1_xattn_b2': _L1_xattn_in['b2'], 'L1_xattn_g1': _L1_xattn_in['g1'], 'L1_xattn_beta1': _L1_xattn_in['beta1'], 'L1_xattn_g2': _L1_xattn_in['g2'], 'L1_xattn_beta2': _L1_xattn_in['beta2'], 'L1_xattn_g3': _L1_xattn_in['g3'], 'L1_xattn_beta3': _L1_xattn_in['beta3'], 'L1_attn_Wq': _L1_attn_in['Wq'], 'L1_attn_Wk': _L1_attn_in['Wk'], 'L1_attn_Wv': _L1_attn_in['Wv'], 'L1_attn_lq1': _L1_attn_in['lq1'], 'L1_attn_lq2': _L1_attn_in['lq2'], 'L1_attn_lk1': _L1_attn_in['lk1'], 'L1_attn_lk2': _L1_attn_in['lk2'], 'L1_attn_Wo': _L1_attn_in['Wo'], 'L1_attn_bo': _L1_attn_in['bo'], 'L1_attn_ln1_g': _L1_attn_in['ln1_g'], 'L1_attn_ln1_b': _L1_attn_in['ln1_b'], 'L1_attn_ln2_g': _L1_attn_in['ln2_g'], 'L1_attn_ln2_b': _L1_attn_in['ln2_b'], 'L1_attn_W1': _L1_attn_in['W1'], 'L1_attn_b1': _L1_attn_in['b1'], 'L1_attn_W2': _L1_attn_in['W2'], 'L1_attn_b2': _L1_attn_in['b2'], 'L1_ffn_Wq': _L1_ffn_in['Wq'], 'L1_ffn_keys': _L1_ffn_in['keys'], 'L1_ffn_W_down': _L1_ffn_in['W_down'], 'L1_ffn_W_up': _L1_ffn_in['W_up']}

def reference(x, ctx_1024, L0_xattn_Wq, L0_xattn_bq, L0_xattn_Wk, L0_xattn_bk, L0_xattn_Wv, L0_xattn_bv, L0_xattn_Wo, L0_xattn_bo, L0_attn_wq, L0_attn_bq, L0_attn_wk, L0_attn_bk, L0_attn_wv, L0_attn_bv, L0_attn_wo, L0_attn_bo, L0_attn_w3d, L0_attn_b3d, L0_ffn_router_w, L0_ffn_sg, L0_ffn_su, L0_ffn_sd, L0_ffn_eg, L0_ffn_eu, L0_ffn_ed, L1_xattn_w1, L1_xattn_b1, L1_xattn_w2, L1_xattn_b2, L1_xattn_g1, L1_xattn_beta1, L1_xattn_g2, L1_xattn_beta2, L1_xattn_g3, L1_xattn_beta3, L1_attn_Wq, L1_attn_Wk, L1_attn_Wv, L1_attn_lq1, L1_attn_lq2, L1_attn_lk1, L1_attn_lk2, L1_attn_Wo, L1_attn_bo, L1_attn_ln1_g, L1_attn_ln1_b, L1_attn_ln2_g, L1_attn_ln2_b, L1_attn_W1, L1_attn_b1, L1_attn_W2, L1_attn_b2, L1_ffn_Wq, L1_ffn_keys, L1_ffn_W_down, L1_ffn_W_up):
    import jax
    import jax.numpy as jnp

    def _L0_xattn_ref(q, k, v, Wq, bq, Wk, bk, Wv, bv, Wo, bo):
        import math
        import jax, jax.numpy as jnp
        import numpy as np
        B, TQ, TK, D = (4, 512, 2048, 256)
        N_HEAD = 16
        STRIDE = 16
        Bb, Tq, Dd = q.shape
        Tk = k.shape[1]
        H, dh, s = (N_HEAD, Dd // N_HEAD, STRIDE)
        Q = (q @ Wq.T + bq).reshape(Bb, Tq, H, dh).transpose(0, 2, 1, 3)
        K = (k @ Wk.T + bk).reshape(Bb, Tk, H, dh).transpose(0, 2, 1, 3)
        V = (v @ Wv.T + bv).reshape(Bb, Tk, H, dh).transpose(0, 2, 1, 3)
        L = Tk // s
        idx = jnp.arange(H)[:, None] + s * jnp.arange(L)[None, :]
        Kg = jnp.take_along_axis(K, idx[None, :, :, None], axis=2)
        Vg = jnp.take_along_axis(V, idx[None, :, :, None], axis=2)
        scores = jnp.einsum('bhqd,bhld->bhql', Q, Kg) / math.sqrt(dh)
        attn = jax.nn.softmax(scores, axis=-1)
        out = jnp.einsum('bhql,bhld->bhqd', attn, Vg)
        out = out.transpose(0, 2, 1, 3).reshape(Bb, Tq, Dd)
        return out @ Wo.T + bo

    def _L0_attn_ref(x, wq, bq, wk, bk, wv, bv, wo, bo, w3d, b3d):
        import jax, jax.numpy as jnp
        import numpy as np
        H = 16

        def _pairwise_l2(pos):
            sq = jnp.sum((pos[:, :, None, :] - pos[:, None, :, :]) ** 2, axis=-1)
            safe = jnp.where(sq > 0, sq, 1.0)
            return jnp.where(sq > 0, jnp.sqrt(safe), 0.0)
        B, S, D = x.shape
        hd = D // H
        scale = 1.0 / hd ** 0.5
        V = (x @ wv.T + bv).reshape(B, S, H, hd).transpose(0, 2, 1, 3)
        pos = x @ w3d.T + b3d
        dist = _pairwise_l2(pos)
        scores = -dist[:, None, :, :] * scale
        causal = jnp.triu(jnp.ones((S, S), dtype=bool), k=1)
        scores = jnp.where(causal[None, None], -jnp.inf, scores)
        attn = jax.nn.softmax(scores, axis=-1)
        attn = jnp.nan_to_num(attn, nan=0.0)
        out = jnp.einsum('bhqk,bhkd->bhqd', attn, V)
        out = out.transpose(0, 2, 1, 3).reshape(B, S, D)
        return out @ wo.T + bo

    def _L0_ffn_ref(hidden_states, router_w, sg, su, sd, eg, eu, ed):
        import jax, jax.numpy as jnp
        import numpy as np
        D, H, O, E, K = (256, 512, 256, 8, 2)
        B, S = (4, 256)
        b, s, d = hidden_states.shape
        shared_out = jnp.einsum('bsh,oh->bso', jax.nn.silu(jnp.einsum('bsd,hd->bsh', hidden_states, sg)) * jnp.einsum('bsd,hd->bsh', hidden_states, su), sd)
        flat = hidden_states.reshape(-1, d)
        T = flat.shape[0]
        logits = flat @ router_w.T
        probs = jax.nn.softmax(logits.astype(jnp.float32), axis=-1)
        topk_w, topk_idx = jax.lax.top_k(probs, K)
        topk_w = topk_w / jnp.sum(topk_w, axis=-1, keepdims=True)
        topk_w = topk_w.astype(hidden_states.dtype)
        combine = jnp.zeros((T, probs.shape[-1]), hidden_states.dtype)
        combine = combine.at[jnp.arange(T)[:, None], topk_idx].add(topk_w)
        gate = jnp.einsum('td,ehd->teh', flat, eg)
        up = jnp.einsum('td,ehd->teh', flat, eu)
        eout = jnp.einsum('teh,eoh->teo', jax.nn.silu(gate) * up, ed)
        routed = jnp.einsum('teo,te->to', eout, combine)
        return shared_out + routed.reshape(b, s, -1)

    def _L1_xattn_ref(y, Z, w1, b1, w2, b2, g1, beta1, g2, beta2, g3, beta3):
        import jax, jax.numpy as jnp
        import numpy as np
        B, S, D, DFF = (4, 512, 256, 1024)
        EPS = 1e-05

        def layernorm(x, gamma, beta):
            mu = jnp.mean(x, axis=-1, keepdims=True)
            var = jnp.var(x, axis=-1, keepdims=True)
            return (x - mu) * jax.lax.rsqrt(var + EPS) * gamma + beta

        def attention(Q, K, V, causal):
            d_k = Q.shape[-1]
            scores = jnp.einsum('bqd,bkd->bqk', Q, K) / jnp.sqrt(jnp.asarray(d_k, Q.dtype))
            if causal:
                q_len, k_len = (scores.shape[-2], scores.shape[-1])
                mask = jnp.tril(jnp.ones((q_len, k_len), dtype=bool))
                scores = jnp.where(mask[None], scores, jnp.asarray(-jnp.inf, scores.dtype))
            w = jax.nn.softmax(scores, axis=-1)
            return jnp.einsum('bqk,bkd->bqd', w, V)
        sa = attention(y, y, y, causal=True)
        y = layernorm(y + sa, g1, beta1)
        ca = attention(y, Z, Z, causal=False)
        y = layernorm(y + ca, g2, beta2)
        h = jax.nn.relu(jnp.einsum('bsd,df->bsf', y, w1) + b1)
        ff = jnp.einsum('bsf,fd->bsd', h, w2) + b2
        y = layernorm(y + ff, g3, beta3)
        return y

    def _L1_attn_ref(x, Wq, Wk, Wv, lq1, lq2, lk1, lk2, Wo, bo, ln1_g, ln1_b, ln2_g, ln2_b, W1, b1, W2, b2):
        import jax, jax.numpy as jnp
        import numpy as np
        B, N, DM, H, FF = (8, 512, 256, 16, 1024)
        D = DM // H // 2
        LAMBDA_INIT = 0.8 - 0.6 * float(np.exp(-0.3 * 1.0))

        def _layernorm(x, g, b, eps=1e-05):
            mu = jnp.mean(x, axis=-1, keepdims=True)
            var = jnp.mean(jnp.square(x - mu), axis=-1, keepdims=True)
            return (x - mu) * jax.lax.rsqrt(var + eps) * g + b

        def _rmsnorm(x, eps=1e-05):
            return x * jax.lax.rsqrt(jnp.mean(x * x, axis=-1, keepdims=True) + eps)

        def _diff_attn(x, Wq, Wk, Wv, lq1, lq2, lk1, lk2, Wo, bo):
            b, n, d = x.shape
            scale = D ** (-0.5)
            q = (x @ Wq.T).reshape(b, n, H, D, 2).transpose(0, 1, 4, 2, 3).reshape(b, n, 2 * H, D) * scale
            k = (x @ Wk.T).reshape(b, n, H, D, 2).transpose(0, 1, 4, 2, 3).reshape(b, n, 2 * H, D)
            v = (x @ Wv.T).reshape(b, n, H, 2 * D).transpose(0, 2, 1, 3)
            att = jnp.einsum('bnqd,bnkd->bnqk', q, k)
            att = jnp.nan_to_num(att)
            att = jax.nn.softmax(att.astype(jnp.float32), axis=-1)
            lam = jnp.exp(jnp.sum(lq1 * lk1)) - jnp.exp(jnp.sum(lq2 * lk2)) + LAMBDA_INIT
            att6 = att.reshape(b, n, 2, H, 2, H)
            att2 = att6[:, :, 0, :, 0, :] - lam * att6[:, :, 1, :, 1, :]
            out = jnp.einsum('bnah,bhnd->bnad', att2, v)
            out = _rmsnorm(out) * (1.0 - LAMBDA_INIT)
            out = out.reshape(b, n, d)
            return out @ Wo.T + bo
        skip = x
        h = _layernorm(x, ln1_g, ln1_b)
        src2 = _diff_attn(h, Wq, Wk, Wv, lq1, lq2, lk1, lk2, Wo, bo)
        conn = skip + src2
        skip2 = conn
        h2 = _layernorm(conn, ln2_g, ln2_b)
        src3 = jax.nn.relu(h2 @ W1.T + b1) @ W2.T + b2
        return skip2 + src3

    def _L1_ffn_ref(x, Wq, keys, W_down, W_up):
        import jax, jax.numpy as jnp
        import numpy as np
        HEADS = 8
        DIM = 256
        DIM_KEY = 128
        NUM_KEYS = 64
        TOPK = 16
        b, n, d = x.shape
        q = (x @ Wq.T).reshape(b, n, 2, HEADS, DIM_KEY).transpose(2, 0, 1, 3, 4)
        sim = jnp.einsum('pbnhd,hkpd->pbnhk', q, keys)
        sx, ix = jax.lax.top_k(sim[0], TOPK)
        sy, iy = jax.lax.top_k(sim[1], TOPK)
        all_scores = (sx[..., :, None] + sy[..., None, :]).reshape(b, n, HEADS, TOPK * TOPK)
        scores, pk_indices = jax.lax.top_k(all_scores, TOPK)
        wd = W_down[pk_indices]
        wu = W_up[pk_indices]
        h = jnp.einsum('bnd,bnhkd->bnhk', x, wd)
        h = jax.nn.gelu(h, approximate=False)
        h = h * jax.nn.softmax(scores, axis=-1)
        return jnp.einsum('bnhk,bnhkd->bnd', h, wu)
    x = x + _L0_xattn_ref(_layernorm(x, axis=-1), ctx_1024, ctx_1024, L0_xattn_Wq, L0_xattn_bq, L0_xattn_Wk, L0_xattn_bk, L0_xattn_Wv, L0_xattn_bv, L0_xattn_Wo, L0_xattn_bo)
    x = x + _L0_attn_ref(_layernorm(x, axis=-1), L0_attn_wq, L0_attn_bq, L0_attn_wk, L0_attn_bk, L0_attn_wv, L0_attn_bv, L0_attn_wo, L0_attn_bo, L0_attn_w3d, L0_attn_b3d)
    x = x + _L0_ffn_ref(_layernorm(x, axis=-1), L0_ffn_router_w, L0_ffn_sg, L0_ffn_su, L0_ffn_sd, L0_ffn_eg, L0_ffn_eu, L0_ffn_ed)
    x = x + _L1_xattn_ref(_layernorm(x, axis=-1), ctx_1024, L1_xattn_w1, L1_xattn_b1, L1_xattn_w2, L1_xattn_b2, L1_xattn_g1, L1_xattn_beta1, L1_xattn_g2, L1_xattn_beta2, L1_xattn_g3, L1_xattn_beta3)
    x = x + _L1_attn_ref(_layernorm(x, axis=-1), L1_attn_Wq, L1_attn_Wk, L1_attn_Wv, L1_attn_lq1, L1_attn_lq2, L1_attn_lk1, L1_attn_lk2, L1_attn_Wo, L1_attn_bo, L1_attn_ln1_g, L1_attn_ln1_b, L1_attn_ln2_g, L1_attn_ln2_b, L1_attn_W1, L1_attn_b1, L1_attn_W2, L1_attn_b2)
    x = x + _L1_ffn_ref(_layernorm(x, axis=-1), L1_ffn_Wq, L1_ffn_keys, L1_ffn_W_down, L1_ffn_W_up)
    return x

_drawn_inputs = setup_inputs


def setup_inputs(seed=0):
    import zlib

    import numpy as np

    out = dict(_drawn_inputs(seed))
    spreads = {'L0_xattn_bq': (0.0, 0.8),
     'L0_xattn_bk': (0.0, 2.0),
     'L0_xattn_bv': (0.0, 0.1),
     'L0_xattn_bo': (0.0, 0.1),
     'L1_xattn_b1': (0.0, 0.1),
     'L1_xattn_b2': (0.0, 0.1),
     'L1_xattn_g1': (1.0, 0.2),
     'L1_xattn_beta1': (0.0, 0.1),
     'L1_xattn_g2': (1.0, 0.2),
     'L1_xattn_beta2': (0.0, 0.1),
     'L1_xattn_g3': (1.0, 0.2),
     'L1_xattn_beta3': (0.0, 0.1),
     'L1_attn_bo': (0.0, 0.1),
     'L1_attn_ln1_g': (1.0, 0.6),
     'L1_attn_ln1_b': (0.0, 0.8),
     'L1_attn_ln2_g': (1.0, 0.6),
     'L1_attn_ln2_b': (0.0, 0.8),
     'L1_attn_b1': (0.0, 0.331),
     'L1_attn_b2': (0.0, 0.1)}
    factors = {'L0_xattn_Wq': 8.0,
     'L0_xattn_Wk': 8.0,
     'L0_attn_bv': 5.699,
     'L0_attn_w3d': 23.385,
     'L0_attn_b3d': 64.0,
     'L1_attn_Wq': 2.846,
     'L1_attn_Wk': 2.78,
     'L1_attn_lq1': 8.0,
     'L1_attn_lq2': 8.0,
     'L1_attn_lk1': 8.0,
     'L1_attn_lk2': 8.0}
    for name, (base, spread) in spreads.items():
        noise = np.random.default_rng([zlib.crc32(name.encode()), seed]).standard_normal(out[name].shape)
        drawn = base * np.exp(spread * noise) if base else spread * noise
        out[name] = jnp.asarray(drawn.astype(out[name].dtype))
    for name, factor in factors.items():
        out[name] = (out[name] * factor).astype(out[name].dtype)
    return out
```

```python
from contextlib import ExitStack

import numpy as np
import concourse.bass as bass
from concourse import mybir

F32 = mybir.dt.float32
ALU = mybir.AluOpType
ACT = mybir.ActivationFunctionType
AX = mybir.AxisListType

NB, S, D = 128, 32, 256
P = 128
T = 4
BT = P // S
G = NB * S // (P * T)
KT = D // P
NK = 257
H = 16
HID, NE = 512, 8
FF = 1024
NPH, NKEY, TOP = 16, 64, 16
EPS = 1e-5
LAMBDA_INIT = 0.8 - 0.6 * float(np.exp(-0.3 * 1.0))
NEG = -3.0e38
PAD = 3.0e38
FMAX = 3.4028234663852886e38
PAIRS = [(a, b) for a in range(TOP) for b in range(TOP) if (a + 1) * (b + 1) <= TOP]
NP = len(PAIRS)
EW = 2 * KT * HID + (HID // P) * D


class Steps:

    def __init__(self, marks):
        self.n, self.marks = 0, marks

    def step(self, *name):
        self.n += 1
        if name:
            self.marks[name] = self.n
        return 1

    def __getitem__(self, name):
        return self.marks.get(name if isinstance(name, tuple) else (name,), 1)


def load_layout():
    return [("wq0", KT * D), ("wk0", KT * D), ("wv0", KT * D), ("wo0", KT * D), ("bq0", KT), ("bk0", KT),
            ("bv0", KT), ("bo0", D), ("wv1", KT * (D + 3)), ("wo1", KT * D), ("bv1", KT), ("bo1", D),
            ("b3d", 3), ("router", KT * NE), ("w1x", KT * FF), ("b1x", FF // P), ("w2x", FF // P * D),
            ("b2x", D), ("g1", D), ("be1", D), ("g2", D), ("be2", D), ("g3", D), ("be3", D),
            ("wqkv", KT * 3 * D), ("wo2", KT * D), ("bo2", D), ("lg1", D), ("lb1", D), ("lg2", D),
            ("lb2", D), ("w1a", KT * FF), ("b1a", FF // P), ("w2a", FF // P * D), ("b2a", D),
            ("wd50", KT * NP), ("wu50", D), ("lqk", 32), ("ident", P), ("headmask", P),
            ("blockones", P), ("causalT", P), ("causal", P), ("eye32", S), ("blkind", BT)]


def build(nc, marks, dram):
    with ExitStack() as ctx:
        def sb(name, cols):
            return ctx.enter_context(nc.sbuf_tensor(name, [P, cols], F32))[:]

        def sem(name):
            return ctx.enter_context(nc.semaphore(name))

        w = {n: sb(n, c) for n, c in load_layout()}
        ps = ctx.enter_context(nc.psum_tensor("ps", [P, 8, 512], F32))
        x = sb("x", T * D).rearrange("p (t d) -> p t d", t=T)
        xn = sb("xn", T * D).rearrange("p (t d) -> p t d", t=T)
        hh = sb("hh", T * D).rearrange("p (t d) -> p t d", t=T)
        aT = sb("aT", KT * 512).rearrange("p (k n) -> p k n", k=KT)
        ctxT = sb("ctxT", T * KT * BT * NK).rearrange("p (t k b n) -> p t k b n", t=T, k=KT, b=BT)
        ctxL = hh
        stream = sb("stream", 2 * EW).rearrange("p (s n) -> p s n", s=2)
        work = sb("work", 4096)
        hT = sb("hT", 4096)
        sbuf = sb("sbuf", 2048)
        qkv = hT[:, 0:2 * 3 * D].rearrange("p (s n) -> p s n", s=2)
        cmat = sb("cmat", KT * NPH * NKEY).rearrange("p (k n) -> p k n", k=KT)
        cvec = sb("cvec", 2 * D).rearrange("p (s n) -> p s n", s=2)
        pb = sb("pb", 2 * NK).rearrange("p (s n) -> p s n", s=2)
        pT = sb("pT", 2 * 384).rearrange("p (s n) -> p s n", s=2)
        ob = sb("ob", 2 * D).rearrange("p (s n) -> p s n", s=2)
        oT = sb("oT", 2 * KT * P).rearrange("p (s k n) -> p s k n", s=2, k=KT)
        st = sb("st", T * 6).rearrange("p (t n) -> p t n", t=T)
        mv = sb("mv", T * 2).rearrange("p (t n) -> p t n", t=T)
        ve = sb("ve", T)
        rstd = sb("rstd", T)
        mhalf = sb("mhalf", T)
        mx = sb("mx", 64).rearrange("p (s n) -> p s n", s=2)
        sm = sb("sm", 64).rearrange("p (s n) -> p s n", s=2)
        ri = sb("ri", 64).rearrange("p (s n) -> p s n", s=2)
        rs = sb("rs", T)
        nm = sb("nm", T)
        nm2 = sb("nm2", T)
        w4 = sb("w4", 2 * BT).rearrange("p (s n) -> p s n", s=2)
        pos = sb("pos", T * 3).rearrange("p (t n) -> p t n", t=T)
        own = sb("own", 3)
        dg = sb("dg", 2 * 96).rearrange("p (s n) -> p s n", s=2)
        df = sb("df", 96)
        dist = sb("dist", T * S).rearrange("p (t n) -> p t n", t=T)
        attT = work[:, 1100:1100 + 2 * P].rearrange("p (s n) -> p s n", s=2)
        lg = sb("lg", T * 14).rearrange("p (t n) -> p t n", t=T)
        lrep = sb("lrep", T * 14).rearrange("p (t n) -> p t n", t=T)
        m8 = sb("m8", T * 8).rearrange("p (t n) -> p t n", t=T)
        ex = sb("ex", T * NE).rearrange("p (t n) -> p t n", t=T)
        comb = sb("comb", T * NE).rearrange("p (t n) -> p t n", t=T)
        neglam = sb("neglam", 1)
        lsum = sb("lsum", 2)
        ltmp = sb("ltmp", 16)
        onesb = sb("onesb", P)

        def kt(name):
            return w[name].rearrange("p (k n) -> p k n", k=KT)

        keyT = work[:, 0:2048].rearrange("p (s f n) -> p s f n", s=2, f=2)
        valM = work[:, 2048:4096].rearrange("p (s f b n) -> p s f b n", s=2, f=2, b=BT)
        valA = work[:, 0:T * (D + 1)].rearrange("p (t n) -> p t n", t=T)
        prod = work.rearrange("p (s n) -> p s n", s=2)
        qT = hT[:, 0:KT * 512].rearrange("p (k n) -> p k n", k=KT)
        hE = hT.rearrange("p (s f n) -> p s f n", s=2, f=HID // P)
        hF = hT.rearrange("p (f n) -> p f n", f=FF // P)
        sg = sbuf[:, 0:1024].rearrange("p (s n) -> p s n", s=2)
        sc = sbuf.rearrange("p (s n) -> p s n", s=2)
        a2 = hh
        wqp = hT.rearrange("p (a d) -> p a d", a=NPH)
        keysp = work[:, 0:NPH * NKEY].rearrange("p (a k) -> p a k", a=NPH)
        rep64 = sbuf[:, 0:1024].rearrange("p (a k) -> p a k", a=NPH)
        s16 = sbuf[:, 1024:1280].rearrange("p (a k) -> p a k", a=NPH)
        cand = qkv[:, 0, 0:8 * NP].rearrange("p (h n) -> p h n", h=8)
        rep1 = sbuf[:, 1280:1280 + 8 * NP].rearrange("p (h n) -> p h n", h=8)
        rep2 = qkv[:, 1, 0:8 * NP].rearrange("p (h n) -> p h n", h=8)
        cexp = work[:, 0:2 * 8 * NP].rearrange("p (s h n) -> p s h n", s=2, h=8)
        cm = sbuf[:, 1700:1764].rearrange("p (h n) -> p h n", h=8)
        cm2 = sbuf[:, 1764:1828].rearrange("p (h n) -> p h n", h=8)
        phd = work[:, 1024:1024 + 2 * NP].rearrange("p (s n) -> p s n", s=2)
        g50 = work[:, 1200:1200 + 2 * NP].rearrange("p (s n) -> p s n", s=2)
        u50 = work[:, 1400:1400 + 2 * NP].rearrange("p (s n) -> p s n", s=2)

        names = ["pe_done", "vec_done", "act_done", "pool_done", "w_in", "x_in", "ctx_in0", "ctx_in1",
                 "ctx_in2", "ctx_in3", "ctxl_in", "stream0", "stream1", "out_done"]
        sems = {n: sem(n) for n in names}
        pe_done, vec_done, act_done, pool_done = (sems[n] for n in names[:4])
        w_in, x_in, ctxl_in, out_done = (sems[n] for n in ("w_in", "x_in", "ctxl_in", "out_done"))
        ctx_in = [sems[f"ctx_in{t}"] for t in range(T)]
        stream_in = [sems["stream0"], sems["stream1"]]
        first, last = min(s.num for s in sems.values()), max(s.num for s in sems.values())
        assert last - first + 1 == len(names)

        PE, V, A, O = (Steps(marks.setdefault("0" + e, {})) for e in "pvao")
        with nc.Block() as block:
            @block.sync
            def _(sp):
                for n, _c in load_layout():
                    sp.dma_start(w[n], dram[n]).then_inc(w_in, 16)
                sp.dma_start(wqp, dram["wqp"].rearrange("p (a d) -> p a d", a=NPH)).then_inc(w_in, 16)
                sp.dma_start(keysp, dram["keysp"].rearrange("p (a k) -> p a k", a=NPH)).then_inc(w_in, 16)

            n_in = 16 * (len(load_layout()) + 2)

            @block.tensor
            def _(pe):
                pe.wait_ge(w_in, n_in)
                for a in range(NPH):
                    for k in range(KT):
                        ins = nc.tensor.matmul(ps[:, 2 + 2 * k + a // 8, (a % 8) * NKEY:(a % 8 + 1) * NKEY],
                                               wqp[:, a, k * P:(k + 1) * P], keysp[:, a, :], start=True, stop=True)
                ins.then_inc(pe_done, PE.step("cmat"))
                for i, (b, wo) in enumerate((("bv0", "wo0"), ("bv1", "wo1"))):
                    for k in range(KT):
                        pe.wait_ge(vec_done, V["bv", i, k])
                        ins = nc.tensor.matmul(ps[:, i, 0:D], ob[:, i, k * P:(k + 1) * P], kt(wo)[:, k, :],
                                               start=k == 0, stop=k == KT - 1)
                    ins.then_inc(pe_done, PE.step("cvec", i))

            @block.scalar
            def _(act):
                act.wait_ge(pe_done, PE["cmat"])
                for k in range(KT):
                    nc.scalar.copy(cmat[:, k, :], ps[:, 2 + 2 * k:4 + 2 * k, :]).then_inc(act_done, A.step("cmat", k))
                act.wait_ge(vec_done, V["lsum"])
                nc.scalar.activation(lsum, lsum, ACT.Exp).then_inc(act_done, A.step("lexp"))

            @block.vector
            def _(v):
                nc.vector.memset(mhalf, -0.5).then_inc(vec_done, V.step())
                nc.vector.memset(lg, PAD).then_inc(vec_done, V.step())
                nc.vector.memset(onesb, 1.0).then_inc(vec_done, V.step("ones"))
                v.wait_ge(w_in, n_in)
                v.wait_ge(vec_done, V.n)
                for i, b in enumerate(("bv0", "bv1")):
                    for k in range(KT):
                        nc.vector.tensor_scalar(ob[:, i, k * P:(k + 1) * P], onesb, w[b][:, k:k + 1], None,
                                                ALU.mult).then_inc(vec_done, V.step("bv", i, k))
                nc.vector.tensor_tensor(ltmp, w["lqk"][:, 0:16], w["lqk"][:, 16:32], ALU.mult).then_inc(vec_done, V.step())
                v.wait_ge(vec_done, V.n)
                nc.vector.tensor_reduce(lsum, ltmp.rearrange("p (a b) -> p a b", a=2), AX.X,
                                        ALU.add).then_inc(vec_done, V.step("lsum"))
                v.wait_ge(act_done, A["lexp"])
                nc.vector.scalar_tensor_tensor(neglam, lsum[:, 1:2], -LAMBDA_INIT, lsum[:, 0:1], ALU.add,
                                               ALU.subtract).then_inc(vec_done, V.step())
                for i, b in enumerate(("bo0", "bo1")):
                    v.wait_ge(pe_done, PE["cvec", i])
                    nc.vector.tensor_tensor(cvec[:, i, :], ps[:, i, 0:D], w[b], ALU.add).then_inc(vec_done, V.step())

        nc.gpsimd.sem_clear(range(first, last + 1))
        nc.all_engine_barrier()

        PE, V, A, O = (Steps(marks.setdefault("1" + e, {})) for e in "pvao")
        SLOT = {}
        for i in range(NE + 1 + T):
            SLOT[i] = 16 * (i // 2 + 1)
        cslot = [(NE + 1 + t) % 2 for t in range(T)]

        def ctxN(t):
            return stream[:, cslot[t], 0:2 * BT * D].rearrange("p (f b n) -> p f b n", f=2, b=BT)

        def b16(ap, n):
            return ap.unsqueeze(2).broadcast_to([P, ap.shape[1], n])

        def qk_product(e, t, c):
            q = qkv[:, t % 2, c * 64:(c + 1) * 64].rearrange("p (a d) -> p a d", a=8)
            k = qkv[:, t % 2, D:2 * D].rearrange("p (a d) -> p a d", a=32)
            return e.tensor_tensor(prod[:, c % 2, :].rearrange("p (a b d) -> p a b d", a=8, b=32),
                                   q.unsqueeze(2).broadcast_to([P, 8, 32, 8]),
                                   k.unsqueeze(1).broadcast_to([P, 8, 32, 8]), ALU.mult)

        def pv_product(e, t, c):
            a = a2[:, t, c * 128:(c + 1) * 128].rearrange("p (a h) -> p a h", a=8)
            vv = qkv[:, t % 2, 2 * D:3 * D].rearrange("p (d h) -> p d h", d=16)
            return e.tensor_tensor(prod[:, c, :].rearrange("p (a d h) -> p a d h", a=8, d=16),
                                   a.unsqueeze(2).broadcast_to([P, 8, 16, 16]),
                                   vv.unsqueeze(1).broadcast_to([P, 8, 16, 16]), ALU.mult)

        with nc.Fori(0, G) as g:
            with nc.Block() as block:

                @block.sync
                def _(sp):
                    rows = bass.ds(g * P, P)
                    sp.dma_start(x, dram["x"][rows, :].rearrange("p (t d) -> p t d", t=T)).then_inc(x_in, 16)
                    n = KT * BT * NK
                    for t in range(T):
                        sp.dma_start(ctxT[:, t].rearrange("p k b n -> p (k b n)"),
                                     dram["ctxT"][rows, t * n:(t + 1) * n]).then_inc(ctx_in[t], 16)
                    for i in range(NE + 1):
                        if i >= 2:
                            sp.wait_ge(pe_done, PE["down", i - 2])
                        sp.dma_start(stream[:, i % 2, :], dram["experts"][i * P:(i + 1) * P, :]).then_inc(stream_in[i % 2], 16)
                        if i == 1:
                            sp.dma_start(ctxL[0:BT], dram["ctxL"][bass.ds(g * BT, BT), :].rearrange(
                                "p (t d) -> p t d", t=T)).then_inc(ctxl_in, 16)
                    n = 2 * BT * D
                    for t in range(T):
                        if t < 2:
                            sp.wait_ge(pe_done, PE["down", NE - 1 + t])
                        else:
                            sp.wait_ge(pe_done, PE["xpv", t - 2])
                        sp.dma_start(stream[:, cslot[t], 0:n],
                                     dram["ctxN"][rows, t * n:(t + 1) * n]).then_inc(stream_in[cslot[t]], 16)
                    for t in range(T):
                        sp.wait_ge(vec_done, V["x6", t])
                        sp.dma_start(dram["out"][rows, t * D:(t + 1) * D], x[:, t, :]).then_inc(out_done, 16)
                    sp.wait_ge(out_done, 16 * T)

                @block.gpsimd
                def _(pool):
                    def mine():
                        pool.wait_ge(pool_done, O.n)

                    def rsqrt(tag):
                        pool.wait_ge(vec_done, V[tag, "var"])
                        nc.gpsimd.tensor_tensor(rstd, ve, mhalf, ALU.pow).then_inc(pool_done, O.step(tag, "rstd"))

                    def add(tag, t, out, a, b):
                        nc.gpsimd.tensor_tensor(out, a, b, ALU.add).then_inc(pool_done, O.step(tag, t))

                    for i, tag in enumerate(("n0", "n1")):
                        rsqrt(tag)
                        for t in range(T):
                            pool.wait_ge(vec_done, V[tag, t])
                            add("xb" + tag, t, x[:, t], x[:, t], cvec[:, i])
                    rsqrt("n2")
                    rsqrt("y0")
                    for tag, be in (("y1", "be1"), ("y2", "be2")):
                        rsqrt(tag)
                        for t in range(T):
                            pool.wait_ge(vec_done, V[tag, "g", t])
                            add(tag, t, xn[:, t], xn[:, t], w[be])
                    for t in range(T):
                        pool.wait_ge(pe_done, PE["y2", "T", t])
                        add("y2b", t, xn[:, t], xn[:, t], w["b2x"])
                    rsqrt("y3")
                    for t in range(T):
                        pool.wait_ge(vec_done, V["y0", t])
                        add("xbe3", t, x[:, t], x[:, t], w["be3"])
                    rsqrt("z")
                    rsqrt("h1")
                    for t in range(T):
                        pool.wait_ge(vec_done, V["h1", "g", t])
                        add("h1", t, hh[:, t], hh[:, t], w["lb1"])
                    for t in range(T):
                        add("zb", t, xn[:, t], xn[:, t], w["bo2"])
                    for i in range(T + 1):
                        if i < T:
                            t = i
                            for c in (1, 3):
                                pool.wait_ge(act_done, A["qkv", t])
                                if c == 3:
                                    pool.wait_ge(vec_done, V["dred", t, 1])
                                elif t >= 2:
                                    pool.wait_ge(vec_done, V["pred", t - 2, 1])
                                    pool.wait_ge(vec_done, V["dred", t - 1, 3])
                                elif t >= 1:
                                    pool.wait_ge(vec_done, V["dred", t - 1, 3])
                                qk_product(nc.gpsimd, t, c).then_inc(pool_done, O.step("dprod", t, c))
                        if i >= 1:
                            t = i - 1
                            pool.wait_ge(vec_done, V["datt", t])
                            if i < T:
                                pool.wait_ge(vec_done, V["dred", i, 3])
                            pv_product(nc.gpsimd, t, 1).then_inc(pool_done, O.step("pprod", t))
                    rsqrt("h2")
                    for t in range(T):
                        pool.wait_ge(vec_done, V["h2", "g", t])
                        add("h2", t, hh[:, t], hh[:, t], w["lb2"])
                    for t in range(T):
                        add("cb", t, xn[:, t], xn[:, t], w["b2a"])
                    for t in range(T):
                        pool.wait_ge(pool_done, O["cb", t])
                        add("xc", t, x[:, t], x[:, t], xn[:, t])
                    rsqrt("n5")

                @block.tensor
                def _(pe):
                    mm, tr = nc.tensor.matmul, nc.tensor.transpose
                    ident = w["ident"]

                    def turn(tag, src, done, steps, key):
                        for t in range(T):
                            pe.wait_ge(done, steps[key + (t,)])
                            if t >= 2:
                                pe.wait_ge(act_done, A[tag, "T", t - 2])
                            for k in range(KT):
                                ins = tr(ps[:, t % 2, k * P:(k + 1) * P], src[:, t, k * P:(k + 1) * P], ident)
                            ins.then_inc(pe_done, PE.step(tag, "T", t))

                    def project(out, t, wt, cols):
                        for k in range(KT):
                            ins = mm(out, aT[:, k, t * P:(t + 1) * P], wt[:, k, cols], start=k == 0, stop=k == KT - 1)
                        return ins

                    def out_proj(tag, t, tbank, wbank, wo, free):
                        pe.wait_ge(vec_done, V[tag, "o", t])
                        free(0)
                        for k in range(KT):
                            ins = tr(ps[:, tbank[0], tbank[1] + k * P:tbank[1] + (k + 1) * P], ob[:, t % 2, k * P:(k + 1) * P], ident)
                        ins.then_inc(pe_done, PE.step(tag, "oT", t))
                        free(1)
                        pe.wait_ge(act_done, A[tag, "oT", t])
                        for k in range(KT):
                            ins = mm(ps[:, wbank, 0:D], oT[:, t % 2, k, :], kt(wo)[:, k, :], start=k == 0, stop=k == KT - 1)
                        ins.then_inc(pe_done, PE.step(tag, "wo", t))

                    turn("n0", xn, vec_done, V, ("n0",))
                    pe.wait_ge(act_done, A["n0", "T", T - 1])
                    for f in range(2):
                        for k in range(KT):
                            ins = mm(ps[:, 6 + f, :], kt("wq0")[:, k, f * P:(f + 1) * P], aT[:, k, :], start=k == 0, stop=k == KT - 1)
                        ins.then_inc(pe_done, PE.step("q0", f))
                    for i in range(T + 2):
                        if i < T:
                            t = i
                            pe.wait_ge(ctx_in[t], 16)
                            if t >= 1:
                                pe.wait_ge(vec_done, V["keyT", t - 1])
                            for f in range(2):
                                for k in range(KT):
                                    ins = mm(ps[:, 2 + f, :], kt("wk0")[:, k, f * P:(f + 1) * P],
                                             ctxT[:, t, k, :, f * P:(f + 1) * P], start=k == 0, stop=k == KT - 1)
                            ins.then_inc(pe_done, PE.step("k0", t))
                            if t >= 1:
                                pe.wait_ge(vec_done, V["valM", t - 1])
                            for f in range(2):
                                for b in range(BT):
                                    for k in range(KT):
                                        ins = mm(ps[:, 4 + f, b * P:(b + 1) * P], ctxT[:, t, k, b, f * P:(f + 1) * P],
                                                 kt("wv0")[:, k, f * P:(f + 1) * P], start=k == 0, stop=k == KT - 1)
                            ins.then_inc(pe_done, PE.step("v0", t))
                            pe.wait_ge(act_done, A["qT", 0])
                            pe.wait_ge(act_done, A["qT", 1])
                            pe.wait_ge(vec_done, V["keyT", t])
                            if t >= 1:
                                pe.wait_ge(vec_done, V["sub0", t - 1])
                            for b in range(BT):
                                for f in range(2):
                                    ins = mm(ps[S * b:S * (b + 1), 6, f * P:(f + 1) * P],
                                             qT[:, f, t * P + S * b:t * P + S * (b + 1)],
                                             keyT[:, t % 2, f, b * P:(b + 1) * P], start=True, stop=True)
                            ins.then_inc(pe_done, PE.step("s0", t))
                        if 1 <= i <= T:
                            t = i - 1
                            pe.wait_ge(act_done, A["exp0", t])
                            if t >= 1:
                                pe.wait_ge(act_done, A["pT0", t - 1])
                            for f in range(2):
                                ins = tr(ps[:, 7, f * P:(f + 1) * P], pb[:, t % 2, f * P:(f + 1) * P], ident)
                            ins.then_inc(pe_done, PE.step("pT0", t))
                            pe.wait_ge(act_done, A["pT0", t])
                            pe.wait_ge(vec_done, V["valM", t])
                            if t >= 1:
                                pe.wait_ge(vec_done, V["l0", "o", t - 1])
                            for b in range(BT):
                                for f in range(2):
                                    ins = mm(ps[S * b:S * (b + 1), 0, f * P:(f + 1) * P],
                                             pT[:, t % 2, f * P + S * b:f * P + S * (b + 1)],
                                             valM[:, t % 2, f, b, :], start=True, stop=True)
                            ins.then_inc(pe_done, PE.step("pv0", t))
                        if i >= 2:
                            t = i - 2

                            def free(n):
                                if t >= 1 and n == 0:
                                    pe.wait_ge(vec_done, V["x1", t - 1])
                            out_proj("l0", t, (1, 256), 1, "wo0", free)

                    pe.wait_ge(vec_done, V["x1", T - 1])
                    turn("n1", xn, vec_done, V, ("n1",))
                    for t in range(T):
                        pe.wait_ge(act_done, A["n1", "T", t])
                        if t >= 2:
                            pe.wait_ge(act_done, A["valA", t - 2])
                            pe.wait_ge(vec_done, V["dg", t - 2])
                        project(ps[:, 2 + t % 2, 0:D + 3], t, kt("wv1"), slice(0, D + 3)).then_inc(pe_done, PE.step("v1", t))
                    for t in range(T):
                        pe.wait_ge(vec_done, V["dg", t])
                        if t >= 2:
                            pe.wait_ge(vec_done, V["sq", t - 2])
                        mm(ps[:, 4 + t % 2, 0:96], w["blockones"], dg[:, t % 2, :], start=True,
                           stop=True).then_inc(pe_done, PE.step("pos", t))
                    for i in range(T + 1):
                        if i < T:
                            t = i
                            pe.wait_ge(vec_done, V["attT", t])
                            pe.wait_ge(act_done, A["valA", t])
                            if t >= 2:
                                pe.wait_ge(vec_done, V["l1", "o", t - 2])
                            mm(ps[:, 6 + t % 2, 0:D + 1], attT[:, t % 2, :], valA[:, t, :], start=True,
                               stop=True).then_inc(pe_done, PE.step("av1", t))
                        if i >= 1:
                            t = i - 1

                            def free(n):
                                if t >= 2 and n == 0:
                                    pe.wait_ge(act_done, A["l1", "oT", t - 2])
                                if t >= 2 and n == 1:
                                    pe.wait_ge(vec_done, V["x2", t - 2])
                            out_proj("l1", t, (2 + t % 2, 0), 4 + t % 2, "wo1", free)

                    turn("n2", xn, vec_done, V, ("n2",))
                    for t in range(T):
                        pe.wait_ge(act_done, A["n2", "T", t])
                        ins = project(ps[:, 6, t * NE:(t + 1) * NE], t, kt("router"), slice(0, NE))
                    ins.then_inc(pe_done, PE.step("router"))
                    pe.wait_ge(vec_done, V["x2", T - 1])

                    def gate_up(e):
                        we = stream[:, e % 2, :]
                        pe.wait_ge(stream_in[e % 2], SLOT[e])
                        for f in range(HID // P):
                            n = e * (HID // P) + f
                            if n >= 2:
                                pe.wait_ge(act_done, A["silu", n - 2])
                                pe.wait_ge(vec_done, V["hid", n - 2])
                            for u in range(2):
                                for k in range(KT):
                                    c = (u * KT + k) * HID + f * P
                                    ins = mm(ps[:, 2 * u + f % 2, :], we[:, c:c + P], aT[:, k, :], start=k == 0, stop=k == KT - 1)
                            ins.then_inc(pe_done, PE.step("gu", n))

                    def down(e):
                        we = stream[:, e % 2, 2 * KT * HID:EW].rearrange("p (f d) -> p f d", f=HID // P)
                        pe.wait_ge(vec_done, V["hid", (e + 1) * (HID // P) - 1])
                        if e == 1:
                            pe.wait_ge(vec_done, V["logits"])
                        for t in range(T):
                            if e >= 2:
                                pe.wait_ge(vec_done, V["acc", e - 2, t | 1])
                            for f in range(HID // P):
                                c = (t % 2) * D
                                ins = mm(ps[:, 4 + 2 * (e % 2) + t // 2, c:c + D], hE[:, e % 2, f, t * P:(t + 1) * P],
                                         we[:, f, :], start=f == 0, stop=f == HID // P - 1)
                            ins.then_inc(pe_done, PE.step(*(("down", e) if t == T - 1 else ("down", e, t))))

                    for e in range(NE + 2):
                        if e <= NE:
                            gate_up(e)
                        if e >= 1:
                            down(e - 1)

                    turn("y0", xn, vec_done, V, ("y0",))
                    for i in range(T + 1):
                        if i < T:
                            t = i
                            pe.wait_ge(act_done, A["y0", "T", t])
                            if t >= 2:
                                pe.wait_ge(vec_done, V["cs", t - 2])
                            for k in range(KT):
                                ins = mm(ps[:, 2 + t % 2, 0:P], aT[:, k, t * P:(t + 1) * P], aT[:, k, t * P:(t + 1) * P],
                                         start=k == 0, stop=k == KT - 1)
                            ins.then_inc(pe_done, PE.step("cs", t))
                        if i >= 1:
                            t = i - 1
                            pe.wait_ge(act_done, A["cexp", t])
                            pe.wait_ge(vec_done, V["acc", NE - 1 + t % 2, T - 1])
                            if t >= 2:
                                pe.wait_ge(act_done, A["cpT", t - 2])
                            tr(ps[:, 4 + t % 2, 0:P], pb[:, t % 2, 0:P], ident).then_inc(pe_done, PE.step("cpT", t))
                            pe.wait_ge(act_done, A["cpT", t])
                            if t >= 2:
                                pe.wait_ge(vec_done, V["y1p", t - 2])
                            mm(ps[:, 6 + t % 2, 0:D], pT[:, t % 2, 0:P], xn[:, t, :], start=True,
                               stop=True).then_inc(pe_done, PE.step("cpv", t))

                    turn("y1", xn, pool_done, O, ("y1",))
                    for i in range(T + 1):
                        if i < T:
                            t = i
                            pe.wait_ge(act_done, A["y1", "T", t])
                            if t >= 2:
                                pe.wait_ge(act_done, A["xexp", t - 2])
                            for b in range(BT):
                                for k in range(KT):
                                    ins = mm(ps[S * b:S * (b + 1), 2 + t % 2, 0:NK], aT[:, k, t * P + S * b:t * P + S * (b + 1)],
                                             ctxT[:, t, k, b, :], start=k == 0, stop=k == KT - 1)
                            ins.then_inc(pe_done, PE.step("xs", t))
                        if i >= 1:
                            t = i - 1
                            pe.wait_ge(act_done, A["xexp", t])
                            pe.wait_ge(vec_done, V["w4", t])
                            if t >= 2:
                                pe.wait_ge(act_done, A["xpT", t - 2])
                            for f in range(2):
                                tr(ps[:, 4 + t % 2, f * P:(f + 1) * P], pb[:, t % 2, f * P:(f + 1) * P], ident)
                            tr(ps[0:BT, 4 + t % 2, 256:384], w4[:, t % 2, :], ident).then_inc(pe_done, PE.step("xpT", t))
                            pe.wait_ge(act_done, A["xpT", t])
                            pe.wait_ge(stream_in[cslot[t]], SLOT[NE + 1 + t])
                            if t == 0:
                                pe.wait_ge(ctxl_in, 16)
                            if t >= 2:
                                pe.wait_ge(vec_done, V["y2p", t - 2])
                            mm(ps[:, 6 + t % 2, 0:D], pT[0:BT, t % 2, 256:384], ctxL[0:BT, t, :], start=True, stop=False,
                               skip_group_check=True)
                            for b in range(BT):
                                for f in range(2):
                                    ins = mm(ps[S * b:S * (b + 1), 6 + t % 2, 0:D], pT[:, t % 2, f * P + S * b:f * P + S * (b + 1)],
                                             ctxN(t)[:, f, b, :], start=False, stop=f == 1, skip_group_check=True)
                            ins.then_inc(pe_done, PE.step("xpv", t))

                    def ffn(tag, w1, w2):
                        for f in range(FF // P):
                            if f == 0:
                                for t in range(T):
                                    pe.wait_ge(act_done, A[tag, "T", t])
                            if f >= 2:
                                pe.wait_ge(act_done, A[tag, "relu", f - 2])
                            for k in range(KT):
                                ins = mm(ps[:, 2 + f % 2, :], kt(w1)[:, k, f * P:(f + 1) * P], aT[:, k, :], start=k == 0, stop=k == KT - 1)
                            ins.then_inc(pe_done, PE.step(tag, "f1", f))
                        w2v = w[w2].rearrange("p (f d) -> p f d", f=FF // P)
                        pe.wait_ge(act_done, A[tag, "relu", FF // P - 1])
                        for t in range(T):
                            if t >= 2:
                                pe.wait_ge(vec_done, V[tag, "f2", t - 2])
                            for f in range(FF // P):
                                ins = mm(ps[:, 6 + t % 2, 0:D], hF[:, f, t * P:(t + 1) * P], w2v[:, f, :],
                                         start=f == 0, stop=f == FF // P - 1)
                            ins.then_inc(pe_done, PE.step(tag, "f2", t))

                    turn("y2", xn, pool_done, O, ("y2",))
                    ffn("y2", "w1x", "w2x")

                    turn("h1", hh, pool_done, O, ("h1",))
                    for i in range(T + 2):
                        if i < T:
                            t = i
                            pe.wait_ge(act_done, A["h1", "T", t])
                            if t >= 2:
                                pe.wait_ge(act_done, A["qkv", t - 2])
                            project(ps[:, 2 + t % 2, :], t, kt("wqkv"), slice(0, 512))
                            project(ps[:, 4 + t % 2, 0:D], t, kt("wqkv"), slice(512, 768)).then_inc(pe_done, PE.step("qkv", t))
                        if i >= 2:
                            t = i - 2

                            def free(n):
                                if t >= 2 and n == 0:
                                    pe.wait_ge(act_done, A["l4", "oT", t - 2])
                                if t >= 2 and n == 1:
                                    pe.wait_ge(vec_done, V["conn", t - 2])
                            out_proj("l4", t, (6 + t % 2, 256), 6 + t % 2, "wo2", free)

                    turn("h2", hh, pool_done, O, ("h2",))
                    ffn("h2", "w1a", "w2a")

                    turn("n5", xn, vec_done, V, ("n5",))
                    for i in range(T + 1):
                        if i < T:
                            t = i
                            pe.wait_ge(act_done, A["n5", "T", t])
                            if t >= 2:
                                pe.wait_ge(vec_done, V["rep64", t - 2])
                                pe.wait_ge(act_done, A["g50", t - 2])
                            project(ps[:, 2 + 2 * (t % 2), :], t, cmat, slice(0, 512))
                            project(ps[:, 3 + 2 * (t % 2), :], t, cmat, slice(512, 1024))
                            project(ps[:, 6 + t % 2, 0:NP], t, kt("wd50"), slice(0, NP)).then_inc(pe_done, PE.step("sim", t))
                        if i >= 1:
                            t = i - 1
                            pe.wait_ge(vec_done, V["u50", t])
                            if t >= 1:
                                pe.wait_ge(act_done, A["uT", t - 1])
                            if t == 0:
                                pe.wait_ge(act_done, A["n5", "T", T - 1])
                            tr(ps[0:NP, 0, 0:P], u50[:, t % 2, :], ident).then_inc(pe_done, PE.step("uT", t))
                            pe.wait_ge(act_done, A["uT", t])
                            if t >= 1:
                                pe.wait_ge(vec_done, V["x6", t - 1])
                            mm(ps[:, 1, 0:D], pT[0:NP, t % 2, 0:P], w["wu50"][0:NP, :], start=True,
                               stop=True).then_inc(pe_done, PE.step("up", t))

                @block.scalar
                def _(act):
                    sa = nc.scalar.activation

                    def turn(tag, reader):
                        if reader:
                            act.wait_ge(pe_done, PE[reader])
                        for t in range(T):
                            act.wait_ge(pe_done, PE[tag, "T", t])
                            nc.scalar.copy(aT[:, :, t * P:(t + 1) * P], ps[:, t % 2, 0:KT * P].rearrange("p (k n) -> p k n", k=KT)).then_inc(act_done, A.step(tag, "T", t))

                    def o_turn(tag, t, bank, col):
                        act.wait_ge(pe_done, PE[tag, "oT", t])
                        if t >= 2:
                            act.wait_ge(pe_done, PE[tag, "wo", t - 2])
                        nc.scalar.copy(oT[:, t % 2].rearrange("p k n -> p (k n)"), ps[:, bank, col:col + 256]).then_inc(
                            act_done, A.step(tag, "oT", t))

                    turn("n0", None)
                    for f in range(2):
                        act.wait_ge(pe_done, PE["q0", f])
                        sa(qT[:, f, :], ps[:, 6 + f, :], ACT.Identity, bias=w["bq0"][:, f:f + 1]).then_inc(act_done, A.step("qT", f))
                    for i in range(T + 2):
                        if i < T:
                            t = i
                            act.wait_ge(vec_done, V["sub0", t])
                            sa(pb[:, t % 2, 0:256], pb[:, t % 2, 0:256], ACT.Exp, scale=0.25).then_inc(act_done, A.step("exp0", t))
                        if 1 <= i <= T:
                            t = i - 1
                            act.wait_ge(pe_done, PE["pT0", t])
                            if t >= 2:
                                act.wait_ge(pe_done, PE["pv0", t - 2])
                            nc.scalar.copy(pT[:, t % 2, 0:256], ps[:, 7, 0:256]).then_inc(act_done, A.step("pT0", t))
                        if i >= 2:
                            o_turn("l0", i - 2, 1, 256)

                    turn("n1", ("q0", 1))
                    for t in range(T):
                        act.wait_ge(pe_done, PE["v1", t])
                        nc.scalar.copy(valA[:, t, 0:D], ps[:, 2 + t % 2, 0:D]).then_inc(act_done, A.step("valA", t))
                    act.wait_ge(vec_done, V["sq", T - 1])
                    sa(dist, dist, ACT.Sqrt).then_inc(act_done, A.step())
                    act.wait_ge(act_done, A.n)
                    sa(dist, dist, ACT.Exp, scale=-0.25).then_inc(act_done, A.step("dexp"))
                    for t in range(T):
                        o_turn("l1", t, 2 + t % 2, 0)

                    turn("n2", ("v1", T - 1))
                    act.wait_ge(vec_done, V["lsub"])
                    sa(ex, ex, ACT.Exp).then_inc(act_done, A.step("lexp"))
                    for n in range((NE + 1) * (HID // P)):
                        act.wait_ge(pe_done, PE["gu", n])
                        if n >= 2:
                            act.wait_ge(vec_done, V["hid", n - 2])
                        sa(sg[:, n % 2, :], ps[:, n % 2, :], ACT.Silu).then_inc(act_done, A.step("silu", n))

                    turn("y0", ("gu", (NE + 1) * (HID // P) - 1))
                    for i in range(T + 1):
                        if i < T:
                            t = i
                            act.wait_ge(vec_done, V["cmax", t])
                            sa(pb[:, t % 2, 0:P], pb[:, t % 2, 0:P], ACT.Exp, bias=nm[:, t:t + 1],
                               accum_out=rs[:, t:t + 1]).then_inc(act_done, A.step("cexp", t))
                        if i >= 1:
                            t = i - 1
                            act.wait_ge(pe_done, PE["cpT", t])
                            if t >= 2:
                                act.wait_ge(pe_done, PE["cpv", t - 2])
                            nc.scalar.copy(pT[:, t % 2, 0:P], ps[:, 4 + t % 2, 0:P]).then_inc(act_done, A.step("cpT", t))

                    turn("y1", ("cs", T - 1))
                    for i in range(T + 1):
                        if i < T:
                            t = i
                            act.wait_ge(vec_done, V["xmax", t])
                            if t >= 2:
                                act.wait_ge(pe_done, PE["xpT", t - 2])
                                act.wait_ge(vec_done, V["w4", t - 2])
                            sa(pb[:, t % 2, 0:NK], ps[:, 2 + t % 2, 0:NK], ACT.Exp, bias=nm[:, t:t + 1], scale=1.0 / 16,
                               accum_out=rs[:, t:t + 1]).then_inc(act_done, A.step("xexp", t))
                        if i >= 1:
                            t = i - 1
                            act.wait_ge(pe_done, PE["xpT", t])
                            if t >= 2:
                                act.wait_ge(pe_done, PE["xpv", t - 2])
                            nc.scalar.copy(pT[:, t % 2, 0:256], ps[:, 4 + t % 2, 0:256]).then_inc(act_done, A.step())
                            nc.scalar.copy(pT[0:BT, t % 2, 256:384], ps[0:BT, 4 + t % 2, 256:384]).then_inc(act_done, A.step("xpT", t))

                    def ffn(tag, b1):
                        for f in range(FF // P):
                            act.wait_ge(pe_done, PE[tag, "f1", f])
                            sa(hF[:, f, :], ps[:, 2 + f % 2, :], ACT.Relu, bias=w[b1][:, f:f + 1]).then_inc(act_done, A.step(tag, "relu", f))

                    turn("y2", ("xs", T - 1))
                    ffn("y2", "b1x")

                    turn("h1", ("y2", "f1", FF // P - 1))
                    for i in range(T + 2):
                        if i < T:
                            t = i
                            act.wait_ge(pe_done, PE["qkv", t])
                            if t >= 2:
                                act.wait_ge(vec_done, V["pprod", t - 2])
                                act.wait_ge(pool_done, O["pprod", t - 2])
                            nc.scalar.copy(qkv[:, t % 2, 0:512], ps[:, 2 + t % 2, :]).then_inc(act_done, A.step())
                            nc.scalar.copy(qkv[:, t % 2, 512:768], ps[:, 4 + t % 2, 0:256]).then_inc(act_done, A.step("qkv", t))
                            act.wait_ge(vec_done, V["dsub", t])
                            sa(sc[:, t % 2, :], sc[:, t % 2, :], ACT.Exp, scale=8.0 ** -0.5).then_inc(act_done, A.step("dexp2", t))
                        if 1 <= i <= T:
                            t = i - 1
                            act.wait_ge(vec_done, V["rms", t])
                            sa(mx[:, t % 2, 16:32], mx[:, t % 2, 16:32], ACT.Sqrt,
                               scale=(1.0 - LAMBDA_INIT) ** -2).then_inc(act_done, A.step("rms", t))
                        if i >= 2:
                            o_turn("l4", i - 2, 6 + (i % 2), 256)

                    turn("h2", ("qkv", T - 1))
                    ffn("h2", "b1a")

                    turn("n5", ("h2", "f1", FF // P - 1))
                    for i in range(T + 1):
                        if i < T:
                            t = i
                            act.wait_ge(pe_done, PE["sim", t])
                            if t >= 2:
                                act.wait_ge(vec_done, V["u50", t - 2])
                            sa(g50[:, t % 2, :], ps[:, 6 + t % 2, 0:NP], ACT.Gelu).then_inc(act_done, A.step("g50", t))
                            act.wait_ge(vec_done, V["csub", t])
                            sa(cexp[:, t % 2], cexp[:, t % 2], ACT.Exp).then_inc(act_done, A.step("cexp2", t))
                        if i >= 1:
                            t = i - 1
                            act.wait_ge(pe_done, PE["uT", t])
                            if t >= 2:
                                act.wait_ge(pe_done, PE["up", t - 2])
                            nc.scalar.copy(pT[0:NP, t % 2, 0:P], ps[0:NP, 0, 0:P]).then_inc(act_done, A.step("uT", t))

                @block.vector
                def _(v):
                    vv = nc.vector

                    def own_steps():
                        v.wait_ge(vec_done, V.n)

                    def norm(tag, src, dst, ready=None, gain=None, dst_free=None):
                        for t in range(T):
                            if ready:
                                ready(t)
                            if V.n:
                                own_steps() if t == 0 else None
                            vv.bn_stats(st[:, t, :], src[:, t, :]).then_inc(vec_done, V.step(tag, "st", t))
                        for t in range(T):
                            v.wait_ge(vec_done, V[tag, "st", t])
                            vv.bn_aggr(mv[:, t, :], st[:, t, :]).then_inc(vec_done, V.step())
                        own_steps()
                        vv.tensor_scalar(ve, mv[:, :, 1], EPS, None, ALU.add).then_inc(vec_done, V.step(tag, "var"))
                        v.wait_ge(pool_done, O[tag, "rstd"])
                        for t in range(T):
                            if dst_free:
                                dst_free(t)
                            vv.tensor_scalar(dst[:, t, :], src[:, t, :], mv[:, t, 0:1], rstd[:, t:t + 1], ALU.subtract,
                                             ALU.mult).then_inc(vec_done, V.step(tag, t))
                        if gain:
                            for t in range(T):
                                v.wait_ge(vec_done, V[tag, t])
                                vv.tensor_tensor(dst[:, t, :], dst[:, t, :], w[gain], ALU.mult).then_inc(vec_done, V.step(tag, "g", t))

                    v.wait_ge(x_in, 16)
                    norm("n0", x, xn)
                    for i in range(T + 2):
                        if i < T:
                            t = i
                            v.wait_ge(pe_done, PE["k0", t])
                            if t >= 2:
                                v.wait_ge(pe_done, PE["s0", t - 2])
                            hm = w["headmask"].unsqueeze(1)
                            for f in range(2):
                                vv.scalar_tensor_tensor(keyT[:, t % 2, f, :].rearrange("p (b n) -> p b n", b=BT),
                                                        ps[:, 2 + f, :].rearrange("p (b n) -> p b n", b=BT), w["bk0"][:, f:f + 1],
                                                        hm.broadcast_to([P, BT, P]), ALU.add,
                                                        ALU.mult).then_inc(vec_done, V.step(*(("keyT", t) if f else ())))
                            v.wait_ge(pe_done, PE["v0", t])
                            if t >= 2:
                                v.wait_ge(pe_done, PE["pv0", t - 2])
                            vv.tensor_tensor(valM[:, t % 2].rearrange("p f b n -> p (f b) n"),
                                             ps[:, 4:6, :].rearrange("p f (b n) -> p (f b) n", b=BT),
                                             hm.broadcast_to([P, 2 * BT, P]), ALU.mult).then_inc(vec_done, V.step("valM", t))
                            v.wait_ge(pe_done, PE["s0", t])
                            if t >= 2:
                                v.wait_ge(pe_done, PE["pT0", t - 2])
                            own_steps()
                            sv = ps[:, 6, 0:256].rearrange("p (h l) -> p h l", h=H)
                            vv.tensor_reduce(mx[:, 0, 0:H], sv, AX.X, ALU.max).then_inc(vec_done, V.step())
                            own_steps()
                            vv.tensor_tensor(pb[:, t % 2, 0:256].rearrange("p (h l) -> p h l", h=H), sv, b16(mx[:, 0, 0:H], 16),
                                             ALU.subtract).then_inc(vec_done, V.step("sub0", t))
                        if 1 <= i <= T:
                            t = i - 1
                            v.wait_ge(act_done, A["exp0", t])
                            own_steps()
                            vv.tensor_reduce(sm[:, 0, 0:H], pb[:, t % 2, 0:256].rearrange("p (h l) -> p h l", h=H), AX.X,
                                             ALU.add).then_inc(vec_done, V.step())
                            own_steps()
                            vv.reciprocal(ri[:, 0, 0:H], sm[:, 0, 0:H]).then_inc(vec_done, V.step())
                            own_steps()
                            v.wait_ge(pe_done, PE["pv0", t])
                            if t >= 2:
                                v.wait_ge(pe_done, PE["l0", "oT", t - 2])
                            vv.tensor_tensor(ob[:, t % 2, :].rearrange("p (h l) -> p h l", h=H),
                                             ps[:, 0, 0:256].rearrange("p (h l) -> p h l", h=H), b16(ri[:, 0, 0:H], 16),
                                             ALU.mult).then_inc(vec_done, V.step("l0", "o", t))
                        if i >= 2:
                            t = i - 2
                            v.wait_ge(pe_done, PE["l0", "wo", t])
                            v.wait_ge(pool_done, O["xbn0", t])
                            vv.tensor_tensor(x[:, t, :], ps[:, 1, 0:D], x[:, t, :], ALU.add).then_inc(vec_done, V.step("x1", t))

                    def xn_turned(tag):
                        return lambda t: v.wait_ge(pe_done, PE[tag, "T", t])

                    norm("n1", x, xn, dst_free=xn_turned("n0"))
                    vv.memset(valA[:, :, D:D + 1], 1.0).then_inc(vec_done, V.step("ones1"))
                    e3 = w["eye32"].unsqueeze(1).broadcast_to([P, 3, S])
                    for t in range(T):
                        v.wait_ge(act_done, A["valA", t])
                        vv.tensor_tensor(pos[:, t, :], ps[:, 2 + t % 2, D:D + 3], w["b3d"], ALU.add).then_inc(vec_done, V.step())
                        own_steps()
                        if t >= 2:
                            v.wait_ge(pe_done, PE["pos", t - 2])
                        vv.tensor_tensor(dg[:, t % 2, :].rearrange("p (c j) -> p c j", c=3), b16(pos[:, t, :], S), e3,
                                         ALU.mult).then_inc(vec_done, V.step("dg", t))
                    for t in range(T):
                        v.wait_ge(pe_done, PE["pos", t])
                        pv = ps[:, 4 + t % 2, 0:96].rearrange("p (c j) -> p c j", c=3)
                        d3 = df.rearrange("p (c j) -> p c j", c=3)
                        own_steps()
                        vv.tensor_tensor(d3, pv, e3, ALU.mult).then_inc(vec_done, V.step())
                        own_steps()
                        vv.tensor_reduce(own, d3, AX.X, ALU.add).then_inc(vec_done, V.step())
                        own_steps()
                        vv.tensor_tensor(d3, pv, b16(own, S), ALU.subtract).then_inc(vec_done, V.step())
                        own_steps()
                        vv.tensor_tensor(df, df, df, ALU.mult).then_inc(vec_done, V.step())
                        own_steps()
                        vv.tensor_reduce(dist[:, t, :], df.rearrange("p (c j) -> p j c", c=3), AX.X, ALU.add).then_inc(vec_done, V.step("sq", t))
                    v.wait_ge(act_done, A["dexp"])
                    for i in range(T + 2):
                        if i < T:
                            t = i
                            if t >= 2:
                                v.wait_ge(pe_done, PE["av1", t - 2])
                            vv.tensor_tensor(attT[:, t % 2, :].rearrange("p (b j) -> p b j", b=BT),
                                             dist[:, t, :].unsqueeze(1).broadcast_to([P, BT, S]),
                                             w["causalT"].rearrange("p (b j) -> p b j", b=BT), ALU.mult).then_inc(vec_done, V.step("attT", t))
                        if 1 <= i <= T:
                            t = i - 1
                            v.wait_ge(pe_done, PE["av1", t])
                            own_steps()
                            vv.reciprocal(ri[:, 0, 0:1], ps[:, 6 + t % 2, D:D + 1]).then_inc(vec_done, V.step())
                            own_steps()
                            if t >= 2:
                                v.wait_ge(pe_done, PE["l1", "oT", t - 2])
                            vv.tensor_scalar(ob[:, t % 2, :], ps[:, 6 + t % 2, 0:D], ri[:, 0, 0:1], None,
                                             ALU.mult).then_inc(vec_done, V.step("l1", "o", t))
                        if i >= 2:
                            t = i - 2
                            v.wait_ge(pe_done, PE["l1", "wo", t])
                            v.wait_ge(pool_done, O["xbn1", t])
                            vv.tensor_tensor(x[:, t, :], ps[:, 4 + t % 2, 0:D], x[:, t, :], ALU.add).then_inc(vec_done, V.step("x2", t))

                    norm("n2", x, xn, dst_free=xn_turned("n1"))
                    v.wait_ge(pe_done, PE["router"])
                    vv.tensor_copy(lg[:, :, 0:NE], ps[:, 6, 0:T * NE].rearrange("p (t n) -> p t n", t=T)).then_inc(vec_done, V.step("logits"))
                    own_steps()
                    for t in range(T):
                        vv.max(m8[:, t, :], lg[:, t, :]).then_inc(vec_done, V.step())
                    own_steps()
                    for t in range(T):
                        vv.match_replace(lrep[:, t, :], m8[:, t, :], lg[:, t, :], NEG).then_inc(vec_done, V.step())
                    vv.tensor_tensor(ex, lg[:, :, 0:NE], m8[:, :, 6:7].broadcast_to([P, T, NE]), ALU.subtract).then_inc(vec_done, V.step("lsub"))
                    v.wait_ge(act_done, A["lexp"])
                    own_steps()
                    vv.scalar_tensor_tensor(comb, lrep[:, :, 0:NE], NEG, ex, ALU.is_equal, ALU.mult).then_inc(vec_done, V.step())
                    own_steps()
                    vv.tensor_reduce(sm[:, 0, 0:T], comb, AX.X, ALU.add).then_inc(vec_done, V.step())
                    own_steps()
                    vv.reciprocal(ri[:, 0, 0:T], sm[:, 0, 0:T]).then_inc(vec_done, V.step())
                    own_steps()
                    vv.tensor_tensor(comb, comb, b16(ri[:, 0, 0:T], NE), ALU.mult).then_inc(vec_done, V.step("comb"))
                    own_steps()
                    for e in range(NE + 2):
                        if e <= NE:
                            for f in range(HID // P):
                                n = e * (HID // P) + f
                                v.wait_ge(act_done, A["silu", n])
                                if e >= 2 and f == 0:
                                    v.wait_ge(pe_done, PE["down", e - 2])
                                vv.tensor_tensor(hE[:, e % 2, f, :], ps[:, 2 + f % 2, :], sg[:, n % 2, :], ALU.mult).then_inc(vec_done, V.step("hid", n))
                        if e >= 1:
                            for t in range(T):
                                c, bank = (t % 2) * D, 4 + 2 * ((e - 1) % 2) + t // 2
                                v.wait_ge(pe_done, PE["down", e - 1] if t >= 2 else PE["down", e - 1, 1])
                                if e >= 2:
                                    v.wait_ge(vec_done, V["acc", e - 2, t])
                                if e - 1 < NE:
                                    vv.scalar_tensor_tensor(x[:, t, :], ps[:, bank, c:c + D], comb[:, t, e - 1:e], x[:, t, :],
                                                            ALU.mult, ALU.add).then_inc(vec_done, V.step("acc", e - 1, t))
                                else:
                                    vv.tensor_tensor(x[:, t, :], ps[:, bank, c:c + D], x[:, t, :], ALU.add).then_inc(vec_done, V.step("acc", e - 1, t))

                    norm("y0", x, xn, dst_free=xn_turned("n2"))
                    for i in range(T + 1):
                        if i < T:
                            t = i
                            v.wait_ge(pe_done, PE["cs", t])
                            if t >= 2:
                                v.wait_ge(pe_done, PE["cpT", t - 2])
                            vv.scalar_tensor_tensor(pb[:, t % 2, 0:P], ps[:, 2 + t % 2, 0:P], 1.0 / 16, w["causal"], ALU.mult,
                                                    ALU.add).then_inc(vec_done, V.step("cs", t))
                            own_steps()
                            vv.tensor_reduce(nm[:, t:t + 1], pb[:, t % 2, 0:P], AX.X, ALU.max, negate=True).then_inc(vec_done, V.step("cmax", t))
                        if i >= 1:
                            t = i - 1
                            v.wait_ge(act_done, A["cexp", t])
                            own_steps()
                            vv.reciprocal(ri[:, 0, t:t + 1], rs[:, t:t + 1]).then_inc(vec_done, V.step())
                            own_steps()
                            v.wait_ge(pe_done, PE["cpv", t])
                            vv.scalar_tensor_tensor(xn[:, t, :], ps[:, 6 + t % 2, 0:D], ri[:, 0, t:t + 1], xn[:, t, :], ALU.mult,
                                                    ALU.add).then_inc(vec_done, V.step("y1p", t))

                    norm("y1", xn, xn, gain="g1")
                    for i in range(T + 1):
                        if i < T:
                            t = i
                            v.wait_ge(pe_done, PE["xs", t])
                            vv.tensor_reduce(nm2[:, t:t + 1], ps[:, 2 + t % 2, 0:NK], AX.X, ALU.max, negate=True).then_inc(vec_done, V.step())
                            own_steps()
                            vv.tensor_scalar(nm[:, t:t + 1], nm2[:, t:t + 1], 1.0 / 16, None, ALU.mult).then_inc(vec_done, V.step("xmax", t))
                            v.wait_ge(act_done, A["xexp", t])
                            if t >= 2:
                                v.wait_ge(pe_done, PE["xpT", t - 2])
                            vv.tensor_scalar(w4[:, t % 2, :], w["blkind"], pb[:, t % 2, NK - 1:NK], None, ALU.mult).then_inc(vec_done, V.step("w4", t))
                        if i >= 1:
                            t = i - 1
                            own_steps()
                            vv.reciprocal(ri[:, 0, t:t + 1], rs[:, t:t + 1]).then_inc(vec_done, V.step())
                            own_steps()
                            v.wait_ge(pe_done, PE["xpv", t])
                            vv.scalar_tensor_tensor(xn[:, t, :], ps[:, 6 + t % 2, 0:D], ri[:, 0, t:t + 1], xn[:, t, :], ALU.mult,
                                                    ALU.add).then_inc(vec_done, V.step("y2p", t))
                    norm("y2", xn, xn, gain="g2")
                    for t in range(T):
                        v.wait_ge(pe_done, PE["y2", "f2", t])
                        v.wait_ge(pool_done, O["y2b", t])
                        vv.tensor_tensor(xn[:, t, :], ps[:, 6 + t % 2, 0:D], xn[:, t, :], ALU.add).then_inc(vec_done, V.step("y2", "f2", t))
                    norm("y3", xn, xn, gain="g3")
                    for t in range(T):
                        v.wait_ge(pool_done, O["xbe3", t])
                        v.wait_ge(vec_done, V["y3", "g", t])
                        vv.tensor_tensor(x[:, t, :], x[:, t, :], xn[:, t, :], ALU.add).then_inc(vec_done, V.step("x4", t))

                    norm("z", x, xn)
                    norm("h1", xn, hh, gain="lg1")
                    for i in range(T + 2):
                        if i < T:
                            t = i
                            v.wait_ge(act_done, A["qkv", t])
                            own_steps()
                            for c in range(4):
                                if c % 2 == 0:
                                    if c == 2:
                                        v.wait_ge(vec_done, V["dred", t, 0])
                                    qk_product(vv, t, c).then_inc(vec_done, V.step("dprodv", t, c))
                                    own_steps()
                                else:
                                    v.wait_ge(pool_done, O["dprod", t, c])
                                vv.tensor_reduce(sc[:, t % 2, c * 256:(c + 1) * 256],
                                                 prod[:, c % 2, :].rearrange("p (n d) -> p n d", d=8), AX.X,
                                                 ALU.add).then_inc(vec_done, V.step("dred", t, c))
                            own_steps()
                            s2 = sc[:, t % 2, :]
                            s3 = s2.rearrange("p (q k) -> p q k", q=32)
                            vv.tensor_scalar(s2, s2, FMAX, -FMAX, ALU.min, ALU.max).then_inc(vec_done, V.step())
                            own_steps()
                            vv.tensor_reduce(sm[:, t % 2, :], s3, AX.X, ALU.max).then_inc(vec_done, V.step())
                            own_steps()
                            vv.tensor_tensor(s3, s3, b16(sm[:, t % 2, :], 32), ALU.subtract).then_inc(vec_done, V.step("dsub", t))
                        if 1 <= i <= T:
                            t = i - 1
                            v.wait_ge(act_done, A["dexp2", t])
                            own_steps()
                            s3 = sc[:, t % 2, :].rearrange("p (q k) -> p q k", q=32)
                            vv.tensor_reduce(sm[:, t % 2, :], s3, AX.X, ALU.add).then_inc(vec_done, V.step())
                            own_steps()
                            vv.reciprocal(ri[:, t % 2, :], sm[:, t % 2, :]).then_inc(vec_done, V.step())
                            own_steps()
                            vv.tensor_scalar(ri[:, t % 2, 16:32], ri[:, t % 2, 16:32], neglam, None, ALU.mult).then_inc(vec_done, V.step())
                            aa = a2[:, t, :].rearrange("p (a h) -> p a h", a=16)
                            vv.tensor_tensor(aa, s3[:, 0:16, 0:16], b16(ri[:, t % 2, 0:16], 16), ALU.mult).then_inc(vec_done, V.step())
                            own_steps()
                            e1 = s3[:, 16:32, 16:32]
                            vv.tensor_tensor(e1, e1, b16(ri[:, t % 2, 16:32], 16), ALU.mult).then_inc(vec_done, V.step())
                            own_steps()
                            vv.tensor_tensor(aa, aa, e1, ALU.add).then_inc(vec_done, V.step("datt", t))
                            own_steps()
                            pv_product(vv, t, 0).then_inc(vec_done, V.step("pprod", t))
                            own_steps()
                            if t >= 2:
                                v.wait_ge(pe_done, PE["l4", "oT", t - 2])
                            for c in range(2):
                                if c:
                                    v.wait_ge(pool_done, O["pprod", t])
                                vv.tensor_reduce(ob[:, t % 2, c * 128:(c + 1) * 128],
                                                 prod[:, c, :].rearrange("p (n h) -> p n h", h=16), AX.X,
                                                 ALU.add).then_inc(vec_done, V.step("pred", t, c))
                            own_steps()
                            vv.tensor_tensor(a2[:, t, :], ob[:, t % 2, :], ob[:, t % 2, :], ALU.mult).then_inc(vec_done, V.step())
                            own_steps()
                            vv.tensor_reduce(mx[:, t % 2, 0:16], a2[:, t, :].rearrange("p (a d) -> p a d", a=16), AX.X,
                                             ALU.add).then_inc(vec_done, V.step())
                            own_steps()
                            vv.tensor_scalar(mx[:, t % 2, 16:32], mx[:, t % 2, 0:16], 1.0 / 16, EPS, ALU.mult,
                                             ALU.add).then_inc(vec_done, V.step("rms", t))
                            v.wait_ge(act_done, A["rms", t])
                            vv.reciprocal(mx[:, t % 2, 0:16], mx[:, t % 2, 16:32]).then_inc(vec_done, V.step())
                            own_steps()
                            o3 = ob[:, t % 2, :].rearrange("p (a d) -> p a d", a=16)
                            vv.tensor_tensor(o3, o3, b16(mx[:, t % 2, 0:16], 16), ALU.mult).then_inc(vec_done, V.step("l4", "o", t))
                        if i >= 2:
                            t = i - 2
                            v.wait_ge(pe_done, PE["l4", "wo", t])
                            v.wait_ge(pool_done, O["zb", t])
                            vv.tensor_tensor(xn[:, t, :], ps[:, 6 + t % 2, 0:D], xn[:, t, :], ALU.add).then_inc(vec_done, V.step("conn", t))
                    norm("h2", xn, hh, gain="lg2")
                    for t in range(T):
                        v.wait_ge(pe_done, PE["h2", "f2", t])
                        v.wait_ge(pool_done, O["xc", t])
                        vv.tensor_tensor(x[:, t, :], ps[:, 6 + t % 2, 0:D], x[:, t, :], ALU.add).then_inc(vec_done, V.step("h2", "f2", t))

                    norm("n5", x, xn)
                    for i in range(T + 1):
                        if i < T:
                            t = i
                            v.wait_ge(pe_done, PE["sim", t])
                            own_steps()
                            sim = ps[:, 2 + 2 * (t % 2):4 + 2 * (t % 2), :].rearrange("p s (a k) -> p (s a) k", a=8)
                            for a in range(NPH):
                                vv.max(s16[:, a, 0:8], sim[:, a, :]).then_inc(vec_done, V.step("m1", a))
                            for a in range(NPH):
                                v.wait_ge(vec_done, V.n - NPH + 1)
                                vv.match_replace(rep64[:, a, :], s16[:, a, 0:8], sim[:, a, :], NEG).then_inc(
                                    vec_done, V.step(*(("rep64", t) if a == NPH - 1 else ())))
                            for a in range(NPH):
                                v.wait_ge(vec_done, V.n - NPH + 1)
                                vv.max(s16[:, a, 8:16], rep64[:, a, :]).then_inc(vec_done, V.step())
                            own_steps()
                            sx, sy = s16[:, 0:8, :], s16[:, 8:16, :]
                            off = 0
                            for a0, a1 in ((0, 1), (1, 2), (2, 3), (3, 4), (4, 5), (5, 8), (8, 16)):
                                na, nb = a1 - a0, TOP // a1 if a1 < TOP else 1
                                c4 = cand[:, :, off:off + na * nb].rearrange("p h (a b) -> p h a b", a=na)
                                vv.tensor_tensor(c4, sx[:, :, a0:a1].unsqueeze(3).broadcast_to([P, 8, na, nb]),
                                                 sy[:, :, 0:nb].unsqueeze(2).broadcast_to([P, 8, na, nb]),
                                                 ALU.add).then_inc(vec_done, V.step())
                                off += na * nb
                            assert off == NP
                            own_steps()
                            for h in range(8):
                                vv.max(cm[:, h, :], cand[:, h, :]).then_inc(vec_done, V.step())
                            own_steps()
                            vv.tensor_tensor(cexp[:, t % 2], cand, cm[:, :, 0:1].broadcast_to([P, 8, NP]), ALU.subtract).then_inc(vec_done, V.step("csub", t))
                            for h in range(8):
                                vv.match_replace(rep1[:, h, :], cm[:, h, :], cand[:, h, :], NEG).then_inc(vec_done, V.step())
                            for h in range(8):
                                v.wait_ge(vec_done, V.n - 7)
                                vv.max(cm2[:, h, :], rep1[:, h, :]).then_inc(vec_done, V.step())
                            for h in range(8):
                                v.wait_ge(vec_done, V.n - 7)
                                vv.match_replace(rep2[:, h, :], cm2[:, h, :], rep1[:, h, :], NEG).then_inc(vec_done, V.step())
                            own_steps()
                            v.wait_ge(act_done, A["cexp2", t])
                            cflat = cexp[:, t % 2].rearrange("p h n -> p (h n)")
                            vv.scalar_tensor_tensor(cflat, rep2.rearrange("p h n -> p (h n)"), NEG, cflat, ALU.is_equal, ALU.mult).then_inc(vec_done, V.step())
                            own_steps()
                            vv.tensor_reduce(sm[:, 0, 0:8], cexp[:, t % 2], AX.X, ALU.add).then_inc(vec_done, V.step())
                            own_steps()
                            vv.reciprocal(ri[:, 0, 0:8], sm[:, 0, 0:8]).then_inc(vec_done, V.step())
                            own_steps()
                            vv.tensor_tensor(cexp[:, t % 2], cexp[:, t % 2], b16(ri[:, 0, 0:8], NP), ALU.mult).then_inc(vec_done, V.step())
                            own_steps()
                            vv.tensor_reduce(phd[:, t % 2, :], cexp[:, t % 2].rearrange("p h n -> p n h"), AX.X, ALU.add).then_inc(vec_done, V.step())
                            own_steps()
                            if t >= 2:
                                v.wait_ge(pe_done, PE["uT", t - 2])
                            v.wait_ge(act_done, A["g50", t])
                            vv.tensor_tensor(u50[:, t % 2, :], phd[:, t % 2, :], g50[:, t % 2, :], ALU.mult).then_inc(vec_done, V.step("u50", t))
                        if i >= 1:
                            t = i - 1
                            v.wait_ge(pe_done, PE["up", t])
                            vv.tensor_tensor(x[:, t, :], ps[:, 1, 0:D], x[:, t, :], ALU.add).then_inc(vec_done, V.step("x6", t))

            nc.gpsimd.sem_clear(range(first, last + 1))
            nc.all_engine_barrier()


def lay_out(a):
    def kmaj(wt):
        k, n = wt.shape
        return wt.reshape(k // P, P, n).transpose(1, 0, 2).reshape(P, -1)

    def row(b):
        return np.broadcast_to(b.reshape(1, -1), (P, b.size))

    def col(b):
        return b.reshape(-1, P).T

    i = np.arange(P)
    blk = (i[:, None] // S) == (i[None, :] // S)
    out = {
        "wq0": kmaj(a["L0_xattn_Wq"].T), "wk0": kmaj(a["L0_xattn_Wk"].T), "wv0": kmaj(a["L0_xattn_Wv"].T),
        "wo0": kmaj(a["L0_xattn_Wo"].T), "bq0": col(a["L0_xattn_bq"]), "bk0": col(a["L0_xattn_bk"]),
        "bv0": col(a["L0_xattn_bv"]), "bo0": row(a["L0_xattn_bo"]),
        "wv1": kmaj(np.concatenate([a["L0_attn_wv"], a["L0_attn_w3d"]]).T), "wo1": kmaj(a["L0_attn_wo"].T),
        "bv1": col(a["L0_attn_bv"]), "bo1": row(a["L0_attn_bo"]), "b3d": row(a["L0_attn_b3d"]),
        "router": kmaj(a["L0_ffn_router_w"].T),
        "w1x": kmaj(a["L1_xattn_w1"]), "b1x": col(a["L1_xattn_b1"]), "w2x": kmaj(a["L1_xattn_w2"]),
        "b2x": row(a["L1_xattn_b2"]), "g1": row(a["L1_xattn_g1"]), "be1": row(a["L1_xattn_beta1"]),
        "g2": row(a["L1_xattn_g2"]), "be2": row(a["L1_xattn_beta2"]), "g3": row(a["L1_xattn_g3"]),
        "be3": row(a["L1_xattn_beta3"]),
        "wqkv": kmaj(np.concatenate([a["L1_attn_Wq"].reshape(16, 8, 2, D).transpose(2, 0, 1, 3).reshape(D, D),
                                     a["L1_attn_Wk"].reshape(16, 8, 2, D).transpose(2, 0, 1, 3).reshape(D, D),
                                     a["L1_attn_Wv"].reshape(16, 16, D).transpose(1, 0, 2).reshape(D, D)]).T),
        "wo2": kmaj(a["L1_attn_Wo"].T), "bo2": row(a["L1_attn_bo"]),
        "lg1": row(a["L1_attn_ln1_g"]), "lb1": row(a["L1_attn_ln1_b"]), "lg2": row(a["L1_attn_ln2_g"]),
        "lb2": row(a["L1_attn_ln2_b"]), "w1a": kmaj(a["L1_attn_W1"].T), "b1a": col(a["L1_attn_b1"]),
        "w2a": kmaj(a["L1_attn_W2"].T), "b2a": row(a["L1_attn_b2"]),
        "lqk": row(np.concatenate([a["L1_attn_" + n] for n in ("lq1", "lq2", "lk1", "lk2")])),
        "ident": np.eye(P), "headmask": (i[:, None] // H) == (i[None, :] // H), "blockones": blk,
        "causalT": blk & (i[None, :] >= i[:, None]), "causal": np.where(blk & (i[None, :] <= i[:, None]), 0.0, -1e30),
        "eye32": (i[:, None] % S) == np.arange(S)[None, :], "blkind": (i[:, None] // S) == np.arange(BT)[None, :],
        "wqp": a["L1_ffn_Wq"].reshape(NPH, P, D).transpose(1, 0, 2).reshape(P, -1),
        "keysp": a["L1_ffn_keys"].transpose(3, 2, 0, 1).reshape(P, -1),
    }
    rows = [p * TOP + q for p, q in PAIRS]
    out["wd50"] = kmaj(a["L1_ffn_W_down"][rows].T)
    wu = np.zeros((P, D), np.float32)
    wu[:NP] = a["L1_ffn_W_up"][rows]
    out["wu50"] = wu
    gate = [*a["L0_ffn_eg"], a["L0_ffn_sg"]]
    up = [*a["L0_ffn_eu"], a["L0_ffn_su"]]
    down = [*a["L0_ffn_ed"], a["L0_ffn_sd"]]
    out["experts"] = np.concatenate([np.concatenate([kmaj(x.T), kmaj(y.T), kmaj(z.T)], 1) for x, y, z in zip(gate, up, down)])
    out["x"] = a["x"].reshape(G, T, P, D).transpose(0, 2, 1, 3).reshape(G * P, T * D)
    order = [h + H * l for h in range(H) for l in range(NK // H)]
    c = a["ctx_1024"].reshape(G, T, BT, NK, D)
    cp = c[:, :, :, order + [NK - 1], :]
    out["ctxT"] = cp.reshape(G, T, BT, NK, KT, P).transpose(0, 5, 1, 4, 2, 3).reshape(G * P, -1)
    out["ctxN"] = c[:, :, :, order, :].reshape(G, T, BT, 2, P, D).transpose(0, 4, 1, 3, 2, 5).reshape(G * P, -1)
    out["ctxL"] = c[:, :, :, NK - 1, :].transpose(0, 2, 1, 3).reshape(G * BT, -1)
    return {k: np.ascontiguousarray(x, dtype=np.float32) for k, x in out.items()}


def kernel(**inputs):
    import concourse.bacc as bacc
    from concourse.bass_utils import run_bass_kernel_spmd

    arrays = lay_out({k: np.asarray(x) for k, x in inputs.items()})
    marks = {}
    for _ in range(2):
        nc = bacc.Bacc("TRN2", target_bir_lowering=False, num_devices=1)
        dram = {k: nc.dram_tensor("in_" + k, x.shape, F32, kind="ExternalInput").ap() for k, x in arrays.items()}
        dram["out"] = nc.dram_tensor("out_0", (G * P, T * D), F32, kind="ExternalOutput").ap()
        build(nc, marks, dram)
    r = run_bass_kernel_spmd(nc, [{"in_" + k: x for k, x in arrays.items()}], core_ids=[0])
    y = r.results[0]["out_0"]
    return y.reshape(G, P, T, D).transpose(0, 2, 1, 3).reshape(NB, S, D)
```

```python
from contextlib import ExitStack

import numpy as np
import concourse.bass as bass
from concourse import mybir

F32 = mybir.dt.float32
ALU = mybir.AluOpType
ACT = mybir.ActivationFunctionType
AX = mybir.AxisListType

NB, S, D = 128, 32, 256
P = 128
T = 4
BT = P // S
G = NB * S // (P * T)
KT = D // P
NK = 257
H = 16
HID, NE = 512, 8
FF = 1024
NPH, NKEY, TOP = 16, 64, 16
EPS = 1e-5
LAMBDA_INIT = 0.8 - 0.6 * float(np.exp(-0.3 * 1.0))
RMS = (1.0 - LAMBDA_INIT) ** -2
NEG = -3.0e38
PAD = 3.0e38
FMAX = 3.4028234663852886e38
PAIRS = [(a, b) for a in range(TOP) for b in range(TOP) if (a + 1) * (b + 1) <= TOP]
NP = len(PAIRS)
EW = 2 * KT * HID + (HID // P) * D


class Steps:

    def __init__(self, marks):
        self.n, self.marks = 0, marks

    def step(self, *name):
        self.n += 1
        if name:
            self.marks[name] = self.n
        return 1

    def __getitem__(self, name):
        return self.marks.get(name if isinstance(name, tuple) else (name,), 1)


def load_layout():
    return [("wq0", KT * D), ("wk0", KT * D), ("wv0", KT * D), ("wo0", KT * D), ("bq0", KT), ("bk0", KT),
            ("bv0", KT), ("wv1", KT * (D + 3)), ("wo1", KT * D), ("bv1", KT),
            ("b3d", 3), ("router", KT * NE), ("w1x", KT * FF), ("b1x", FF // P), ("w2x", FF // P * D),
            ("b2x", D), ("g1", D), ("be1", D), ("g2", D), ("be2", D), ("g3", D), ("be3", D),
            ("wqkv", KT * 3 * D), ("wo2", KT * D), ("bo2", D), ("lg1", D), ("lb1", D), ("lg2", D),
            ("lb2", D), ("w1a", KT * FF), ("b1a", FF // P), ("w2a", FF // P * D), ("b2a", D),
            ("wd50", KT * NP), ("wu50", D), ("lqk", 32), ("ident", P), ("headmask", P),
            ("blockones", P), ("causalT", P), ("causal", P), ("eye32", S), ("blkind", BT)]


def slots_front():
    norm = [2, 2, 2]
    return ([*norm, 4, *[11] * (T + 2), *norm, *[4] * (T + 1), *[4] * (T + 2), *norm, 6],
            [4] * ((NE + 2) * 4))


def slots_back():
    norm = [3, 3, 3]
    ffn = [2] * (FF // P) + [4] * (T + 1)
    return ([*norm, *[3] * (T + 2), *norm, *[6] * (T + 2), *norm, *ffn, 3, 3, 3, 2, 2, *norm],
            [*[6.5] * (T * 4), *[2] * 8, *norm, *ffn, *norm, *[6] * (T * 3), 3, 3, 3])


def order(streams):
    out = []
    for front, back in zip(slots_front(), slots_back()):
        if streams != "fb":
            out += streams * len(front if streams == "f" else back)
            continue
        sf, sb, i, j = 0.0, 0.0, 0, 0
        while i < len(front) or j < len(back):
            if j == len(back) or (i < len(front) and sf / sum(front) <= sb / sum(back)):
                sf += front[i]
                out.append("f")
                i += 1
            else:
                sb += back[j]
                out.append("b")
                j += 1
    return out


def build(nc, marks, dram):
    with ExitStack() as ctx:
        def sb(name, cols):
            return ctx.enter_context(nc.sbuf_tensor(name, [P, cols], F32))[:]

        def sem(name):
            return ctx.enter_context(nc.semaphore(name))

        w = {n: sb(n, c) for n, c in load_layout()}
        ps = ctx.enter_context(nc.psum_tensor("ps", [P, 8, 512], F32))
        def tiles(name, n=D):
            return sb(name, T * n).rearrange("p (t d) -> p t d", t=T)

        def pair(name, n):
            return sb(name, 2 * n).rearrange("p (s n) -> p s n", s=2)

        NCT = KT * BT * NK
        stream = pair("stream", EW)
        cmat = sb("cmat", KT * NPH * NKEY).rearrange("p (k n) -> p k n", k=KT)
        cvec = pair("cvec", D)
        xA = tiles("xA")
        aTA = sb("aTA", KT * 512).rearrange("p (k n) -> p k n", k=KT)
        hTA = sb("hTA", 4096)
        ctxA0 = sb("ctxA0", KT * BT * 256)
        pbA, pTA, obA = pair("pbA", D), pair("pTA", D), pair("obA", D)
        oTA = pair("oTA", D).rearrange("p s (k n) -> p s k n", k=KT)
        stA, mvA, veA, rstdA = tiles("stA", 6), tiles("mvA", 2), sb("veA", T), sb("rstdA", T)
        smA, riA, mxA = sb("smA", H), sb("riA", H), sb("mxA", H)
        pos, own = tiles("pos", 3), sb("own", 3)
        dist = tiles("dist", S)
        lg, lrep, m8 = tiles("lg", 14), tiles("lrep", 14), tiles("m8", 8)
        ex, comb = tiles("ex", NE), tiles("comb", NE)
        xB, xnB = tiles("xB"), tiles("xnB")
        aTB = sb("aTB", KT * 512).rearrange("p (k n) -> p k n", k=KT)
        hTB = sb("hTB", 4096)
        work = sb("work", 2 * NCT)
        sbuf = sb("sbuf", 2048)
        pb, pT, ob = pair("pb", NK), pair("pT", 384), pair("ob", D)
        oTB = pair("oTB", D).rearrange("p s (k n) -> p s k n", k=KT)
        stB, mvB, veB, rstdB = tiles("stB", 6), tiles("mvB", 2), sb("veB", T), sb("rstdB", T)
        mx, sm, ri = pair("mx", 32), pair("sm", 32), pair("ri", 32)
        rs, nm, nm2 = sb("rs", T), sb("nm", T), sb("nm2", T)
        w4 = pair("w4", BT)
        mhalf, neglam, lsum, ltmp = sb("mhalf", 16), sb("neglam", 1), sb("lsum", 2), sb("ltmp", 16)

        def kt(name):
            return w[name].rearrange("p (k n) -> p k n", k=KT)

        ctxA = [a.rearrange("p (k b n) -> p k b n", k=KT, b=BT) for a in (ctxA0, stream[:, 0, 0:2048])]
        keyT = stream[:, 1, 0:2048].rearrange("p (s f n) -> p s f n", s=2, f=2)
        qT = hTA[:, 0:1024].rearrange("p (k n) -> p k n", k=KT)
        valM = hTA[:, 1024:3072].rearrange("p (s f b n) -> p s f b n", s=2, f=2, b=BT)
        valA = hTA[:, 0:T * (D + 1)].rearrange("p (t n) -> p t n", t=T)
        attT = hTA[:, 1100:1100 + 2 * P].rearrange("p (s n) -> p s n", s=2)
        dg = hTA[:, 1400:1592].rearrange("p (s n) -> p s n", s=2)
        df = hTA[:, 1600:1696]
        xnA = hTA[:, 3072:4096].rearrange("p (t d) -> p t d", t=T)
        hE = hTA.rearrange("p (s f n) -> p s f n", s=2, f=HID // P)
        ctxB = work.rearrange("p (s k b n) -> p s k b n", s=2, k=KT, b=BT)
        ctxN = hTB.rearrange("p (s f b n) -> p s f b n", s=2, f=2, b=BT)
        ctxL = sbuf[:, 0:T * D].rearrange("p (t d) -> p t d", t=T)
        hF = hTB.rearrange("p (f n) -> p f n", f=FF // P)
        hh = sbuf[:, 0:T * D].rearrange("p (t d) -> p t d", t=T)
        prod = work[:, 0:4096].rearrange("p (s n) -> p s n", s=2)
        qkv = hTB[:, 0:2 * 3 * D].rearrange("p (s n) -> p s n", s=2)
        sc = sbuf.rearrange("p (s n) -> p s n", s=2)
        a2 = pb[:, :, 0:D]
        wqp = hTB.rearrange("p (a d) -> p a d", a=NPH)
        keysp = work[:, 0:NPH * NKEY].rearrange("p (a k) -> p a k", a=NPH)
        rep64 = sbuf[:, 0:1024].rearrange("p (a k) -> p a k", a=NPH)
        s16 = sbuf[:, 1024:1280].rearrange("p (a k) -> p a k", a=NPH)
        cand = hTB[:, 0:8 * NP].rearrange("p (h n) -> p h n", h=8)
        rep1 = sbuf[:, 1280:1280 + 8 * NP].rearrange("p (h n) -> p h n", h=8)
        rep2 = hTB[:, 512:512 + 8 * NP].rearrange("p (h n) -> p h n", h=8)
        cexp = work[:, 0:2 * 8 * NP].rearrange("p (s h n) -> p s h n", s=2, h=8)
        cm = sbuf[:, 1700:1764].rearrange("p (h n) -> p h n", h=8)
        cm2 = sbuf[:, 1764:1828].rearrange("p (h n) -> p h n", h=8)
        phd = work[:, 1024:1024 + 2 * NP].rearrange("p (s n) -> p s n", s=2)
        g50 = work[:, 1200:1200 + T * NP]
        u50 = work[:, 1400:1400 + 2 * NP].rearrange("p (s n) -> p s n", s=2)

        names = ["pe_done", "vec_done", "act_done", "pool_done", "w_in", "x_in", "ctxA0", "ctxA1", "ctxB0", "ctxB1",
                 "ctxN0", "ctxN1", "ctxl_in", "gu0", "gu1", "dn0", "dn1", "out_done"]
        sems = {n: sem(n) for n in names}
        pe_done, vec_done, act_done, pool_done = (sems[n] for n in names[:4])
        w_in, x_in, ctxl_in, out_done = (sems[n] for n in ("w_in", "x_in", "ctxl_in", "out_done"))
        ctxA_in, ctxB_in, ctxN_in, gu_in, dn_in = ([sems[n + "0"], sems[n + "1"]] for n in ("ctxA", "ctxB", "ctxN", "gu", "dn"))
        first, last = min(s.num for s in sems.values()), max(s.num for s in sems.values())
        assert last - first + 1 == len(names)

        PE, V, A, O = (Steps(marks.setdefault("0" + e, {})) for e in "pvao")
        with nc.Block() as block:
            @block.sync
            def _(sp):
                for n, _c in load_layout():
                    sp.dma_start(w[n], dram[n]).then_inc(w_in, 16)
                for i in range(2):
                    sp.dma_start(cvec[:, i, :], dram["bo01"][:, i * D:(i + 1) * D]).then_inc(w_in, 16)
                sp.dma_start(wqp, dram["wqp"].rearrange("p (a d) -> p a d", a=NPH)).then_inc(w_in, 16)
                sp.dma_start(keysp, dram["keysp"].rearrange("p (a k) -> p a k", a=NPH)).then_inc(w_in, 16)

            n_in = 16 * (len(load_layout()) + 4)

            @block.tensor
            def _(pe):
                pe.wait_ge(w_in, n_in)
                for a in range(NPH):
                    for k in range(KT):
                        ins = nc.tensor.matmul(ps[:, 2 + 2 * k + a // 8, (a % 8) * NKEY:(a % 8 + 1) * NKEY],
                                               wqp[:, a, k * P:(k + 1) * P], keysp[:, a, :], start=True, stop=True)
                ins.then_inc(pe_done, PE.step("cmat"))
                for i, (b, wo) in enumerate((("bv0", "wo0"), ("bv1", "wo1"))):
                    for k in range(KT):
                        pe.wait_ge(vec_done, V["bv", i, k])
                        ins = nc.tensor.matmul(ps[:, i, 0:D], obA[:, i, k * P:(k + 1) * P], kt(wo)[:, k, :],
                                               start=k == 0, stop=k == KT - 1)
                    ins.then_inc(pe_done, PE.step("cvec", i))

            @block.scalar
            def _(act):
                act.wait_ge(pe_done, PE["cmat"])
                for k in range(KT):
                    nc.scalar.copy(cmat[:, k, :], ps[:, 2 + 2 * k:4 + 2 * k, :]).then_inc(act_done, A.step("cmat", k))
                act.wait_ge(vec_done, V["lsum"])
                nc.scalar.activation(lsum, lsum, ACT.Exp).then_inc(act_done, A.step("lexp"))

            @block.vector
            def _(v):
                nc.vector.memset(mhalf, -0.5).then_inc(vec_done, V.step())
                nc.vector.memset(lg, PAD).then_inc(vec_done, V.step())
                nc.vector.memset(pbA[:, 0, 0:P], 1.0).then_inc(vec_done, V.step("ones"))
                v.wait_ge(w_in, n_in)
                v.wait_ge(vec_done, V.n)
                for i, b in enumerate(("bv0", "bv1")):
                    for k in range(KT):
                        nc.vector.tensor_scalar(obA[:, i, k * P:(k + 1) * P], pbA[:, 0, 0:P], w[b][:, k:k + 1], None,
                                                ALU.mult).then_inc(vec_done, V.step("bv", i, k))
                nc.vector.tensor_tensor(ltmp, w["lqk"][:, 0:16], w["lqk"][:, 16:32], ALU.mult).then_inc(vec_done, V.step())
                v.wait_ge(vec_done, V.n)
                nc.vector.tensor_reduce(lsum, ltmp.rearrange("p (a b) -> p a b", a=2), AX.X,
                                        ALU.add).then_inc(vec_done, V.step("lsum"))
                v.wait_ge(act_done, A["lexp"])
                nc.vector.scalar_tensor_tensor(neglam, lsum[:, 1:2], -LAMBDA_INIT, lsum[:, 0:1], ALU.add,
                                               ALU.subtract).then_inc(vec_done, V.step())
                for i in range(2):
                    v.wait_ge(pe_done, PE["cvec", i])
                    nc.vector.tensor_tensor(cvec[:, i, :], ps[:, i, 0:D], cvec[:, i, :], ALU.add).then_inc(vec_done, V.step())

        nc.gpsimd.sem_clear(range(first, last + 1))
        nc.all_engine_barrier()

        def qk_product(e, t, c):
            q = qkv[:, t % 2, c * 64:(c + 1) * 64].rearrange("p (a d) -> p a d", a=8)
            k = qkv[:, t % 2, D:2 * D].rearrange("p (a d) -> p a d", a=32)
            return e.tensor_tensor(prod[:, c % 2, :].rearrange("p (a b d) -> p a b d", a=8, b=32),
                                   q.unsqueeze(2).broadcast_to([P, 8, 32, 8]),
                                   k.unsqueeze(1).broadcast_to([P, 8, 32, 8]), ALU.mult)

        def pv_product(e, t, c):
            a = a2[:, t % 2, c * 128:(c + 1) * 128].rearrange("p (a h) -> p a h", a=8)
            vals = qkv[:, t % 2, 2 * D:3 * D].rearrange("p (d h) -> p d h", d=16)
            return e.tensor_tensor(prod[:, c, :].rearrange("p (a d h) -> p a d h", a=8, d=16),
                                   a.unsqueeze(2).broadcast_to([P, 8, 16, 16]),
                                   vals.unsqueeze(1).broadcast_to([P, 8, 16, 16]), ALU.mult)

        def b16(ap, n):
            return ap.unsqueeze(2).broadcast_to([P, ap.shape[1], n])

        def group(g, streams):
            PE, V, A, O = (Steps(marks.setdefault(streams + e, {})) for e in "pvao")

            def run(front, back):
                for s in order(streams):
                    next(front if s == "f" else back)

            with nc.Block() as block:

                @block.sync
                def _(sp):
                    rows = bass.ds(g * P, P)

                    def front():
                        sp.dma_start(xA, dram["x"][rows, :].rearrange("p (t d) -> p t d", t=T)).then_inc(x_in, 16)

                        def context(t):
                            src = dram["ctxT"][rows, t * NCT:(t + 1) * NCT].rearrange("p (a n) -> p a n", n=NK)[:, :, 0:256]
                            sp.dma_start(ctxA[t % 2].rearrange("p k b n -> p (k b) n"), src).then_inc(ctxA_in[t % 2], 16)

                        def gate_up(e):
                            sp.dma_start(stream[:, e % 2, 0:2048], dram["experts"][e * P:(e + 1) * P, 0:2048]).then_inc(gu_in[e % 2], 16)

                        def down(e):
                            sp.dma_start(stream[:, e % 2, 2048:EW], dram["experts"][e * P:(e + 1) * P, 2048:EW]).then_inc(dn_in[e % 2], 16)

                        context(0)
                        context(1)
                        down(0)
                        down(1)
                        for _ in range(4):
                            yield
                        for i in range(T + 2):
                            if 0 <= i < T - 2:
                                sp.wait_ge(pe_done, PE["v0", i])
                                context(i + 2)
                            if i == T:
                                sp.wait_ge(pe_done, PE["s0", T - 1])
                                gate_up(0)
                                gate_up(1)
                            yield
                        for _ in range(3 + T + 1 + T + 2 + 3 + 1):
                            yield
                        for e in range(NE + 2):
                            for f in range(4):
                                if f == 0 and 1 <= e and e + 1 <= NE:
                                    sp.wait_ge(pe_done, PE["gu", e * 4 - 1])
                                    gate_up(e + 1)
                                if f == 3 and 1 <= e and e + 1 <= NE:
                                    sp.wait_ge(pe_done, PE["down", e - 1])
                                    down(e + 1)
                                yield

                    def back():
                        grows = bass.ds((g - 1) * P, P)

                        def context(t):
                            sp.dma_start(ctxB[:, t % 2].rearrange("p k b n -> p (k b n)"),
                                         dram["ctxT"][grows, t * NCT:(t + 1) * NCT]).then_inc(ctxB_in[t % 2], 16)

                        def rows_of(t):
                            sp.dma_start(ctxN[:, t % 2].rearrange("p f b n -> p (f b n)"),
                                         dram["ctxN"][grows, t * 2048:(t + 1) * 2048]).then_inc(ctxN_in[t % 2], 16)

                        context(0)
                        context(1)
                        rows_of(0)
                        rows_of(1)
                        sp.dma_start(ctxL[0:BT], dram["ctxL"][bass.ds((g - 1) * BT, BT), :].rearrange(
                            "p (t d) -> p t d", t=T)).then_inc(ctxl_in, 16)
                        for _ in range(3 + T + 2 + 3):
                            yield
                        for i in range(T + 2):
                            if i < 2:
                                sp.wait_ge(pe_done, PE["xs", i])
                                context(i + 2)
                            if 2 <= i < 4:
                                sp.wait_ge(pe_done, PE["xpv", i - 2])
                                rows_of(i)
                            yield
                        for _ in range(3 + 8 + T + 1 + 8 + (T + 2) * 4 + 3 + 8 + T + 1 + 3):
                            yield
                        for i in range(T + 1):
                            yield
                            if i >= 1:
                                sp.wait_ge(vec_done, V["x6", i - 1])
                                sp.dma_start(dram["out"][grows, (i - 1) * D:i * D], xnB[:, i - 1, :]).then_inc(out_done, 16)
                            yield
                            yield

                    run(front(), back())
                    if "b" in streams:
                        sp.wait_ge(out_done, 16 * T)

                @block.gpsimd
                def _(pool):
                    def add(tag, t, out, a, b):
                        nc.gpsimd.tensor_tensor(out, a, b, ALU.add).then_inc(pool_done, O.step(tag, t))

                    def norm(tag, ve, rstd, then=None):
                        pool.wait_ge(vec_done, V[tag, "var"])
                        nc.gpsimd.tensor_tensor(rstd, ve, mhalf[:, 0:T], ALU.pow).then_inc(pool_done, O.step(tag, "rstd"))
                        yield
                        if then:
                            then(0)
                        yield
                        if then:
                            then(1)
                        yield

                    def front():
                        def with_row(tag, i):
                            def then(slot):
                                if slot == 1:
                                    for t in range(T):
                                        pool.wait_ge(vec_done, V[tag, t])
                                        add("xb" + tag, t, xA[:, t], xA[:, t], cvec[:, i])
                            return then
                        yield from norm("n0", veA, rstdA, with_row("n0", 0))
                        for _ in range(1 + T + 2):
                            yield
                        yield from norm("n1", veA, rstdA, with_row("n1", 1))
                        for _ in range(T + 1 + T + 2):
                            yield
                        yield from norm("n2", veA, rstdA)
                        for _ in range(1 + (NE + 2) * 4):
                            yield

                    def back():
                        def with_bias(tag, be, dst):
                            def then(slot):
                                if slot == 0:
                                    for t in range(T):
                                        pool.wait_ge(vec_done, V[tag, "g", t])
                                        add(tag, t, dst[:, t], dst[:, t], w[be])
                            return then

                        def last_gain(slot):
                            if slot == 1:
                                for t in range(T):
                                    pool.wait_ge(vec_done, V["y0", t])
                                    add("xbe3", t, xB[:, t], xB[:, t], w["be3"])
                        yield from norm("y0", veB, rstdB, last_gain)
                        for _ in range(T + 2):
                            yield
                        yield from norm("y1", veB, rstdB, with_bias("y1", "be1", xnB))
                        for _ in range(T + 2):
                            yield
                        yield from norm("y2", veB, rstdB, with_bias("y2", "be2", xnB))
                        for t in range(T):
                            pool.wait_ge(pe_done, PE["y2", "T", t])
                            add("y2b", t, xnB[:, t], xnB[:, t], w["b2x"])
                        for _ in range(8 + T + 1):
                            yield
                        yield from norm2("y3")
                        yield
                        yield from norm2("z")
                        yield from norm("h1", veB, rstdB, with_bias("h1", "lb1", hh))
                        for i in range(T + 2):
                            if i == 0:
                                for t in range(T):
                                    add("zb", t, xnB[:, t], xnB[:, t], w["bo2"])
                            if i < T:
                                pool.wait_ge(act_done, A["qkv", i])
                                if i >= 1:
                                    pool.wait_ge(vec_done, V["dred", i - 1, 3])
                                qk_product(nc.gpsimd, i, 1).then_inc(pool_done, O.step("dprod", i, 1))
                            yield
                            if 1 <= i <= T:
                                pool.wait_ge(vec_done, V["datt", i - 1])
                                if i < T:
                                    pool.wait_ge(vec_done, V["dred", i, 1])
                                else:
                                    pool.wait_ge(vec_done, V["dred", i - 1, 3])
                                pv_product(nc.gpsimd, i - 1, 1).then_inc(pool_done, O.step("pprod", i - 1))
                                pool.wait_ge(vec_done, V["rms", i - 1])
                                nc.gpsimd.tensor_tensor(mx[:, (i - 1) % 2, 0:16], mx[:, (i - 1) % 2, 16:32], mhalf[:, 0:16],
                                                        ALU.pow).then_inc(pool_done, O.step("rms", i - 1))
                            yield
                            if i < T:
                                pool.wait_ge(vec_done, V["dred", i, 1])
                                if i >= 1:
                                    pool.wait_ge(vec_done, V["pred", i - 1, 1])
                                qk_product(nc.gpsimd, i, 3).then_inc(pool_done, O.step("dprod", i, 3))
                            yield
                            yield
                        yield from norm("h2", veB, rstdB, with_bias("h2", "lb2", hh))
                        for t in range(T):
                            add("cb", t, xnB[:, t], xnB[:, t], w["b2a"])
                        for t in range(T):
                            pool.wait_ge(pool_done, O["cb", t])
                            add("xc", t, xB[:, t], xB[:, t], xnB[:, t])
                        for _ in range(8 + T + 1):
                            yield
                        yield from norm("n5", veB, rstdB)
                        for _ in range((T + 1) * 3):
                            yield

                    def norm2(tag):
                        pool.wait_ge(vec_done, V[tag, "var"])
                        nc.gpsimd.tensor_tensor(rstdB, veB, mhalf[:, 0:T], ALU.pow).then_inc(pool_done, O.step(tag, "rstd"))
                        yield
                        yield

                    run(front(), back())

                @block.tensor
                def _(pe):
                    mm, tr = nc.tensor.matmul, nc.tensor.transpose
                    ident = w["ident"]

                    def norm(tag, src, banks, done, steps, key, first=None):
                        yield
                        yield
                        for t in range(T):
                            pe.wait_ge(done, steps[key + (t,)])
                            if t >= 2:
                                pe.wait_ge(act_done, A[tag, "T", t - 2])
                            for k in range(KT):
                                ins = tr(ps[:, banks[t % 2], k * P:(k + 1) * P], src[:, t, k * P:(k + 1) * P], ident)
                            ins.then_inc(pe_done, PE.step(tag, "T", t))
                        if first:
                            first()
                        yield

                    def project(out, aT, t, wt, cols):
                        for k in range(KT):
                            ins = mm(out, aT[:, k, t * P:(t + 1) * P], wt[:, k, cols], start=k == 0, stop=k == KT - 1)
                        return ins

                    def out_proj(tag, t, bank, o, oT, wo):
                        for k in range(KT):
                            ins = tr(ps[:, bank, 256 + k * P:256 + (k + 1) * P], o[:, t % 2, k * P:(k + 1) * P], ident)
                        ins.then_inc(pe_done, PE.step(tag, "oT", t))
                        pe.wait_ge(act_done, A[tag, "oT", t])
                        for k in range(KT):
                            ins = mm(ps[:, bank, 0:D], oT[:, t % 2, k, :], kt(wo)[:, k, :], start=k == 0, stop=k == KT - 1)
                        ins.then_inc(pe_done, PE.step(tag, "wo", t))

                    def front():
                        yield from norm("n0", xnA, (0, 1), vec_done, V, ("n0",))
                        pe.wait_ge(act_done, A["n0", "T", T - 1])
                        for f in range(2):
                            for k in range(KT):
                                ins = mm(ps[:, 2 + f, :], kt("wq0")[:, k, f * P:(f + 1) * P], aTA[:, k, :], start=k == 0, stop=k == KT - 1)
                            ins.then_inc(pe_done, PE.step("q0", f))
                        yield
                        for i in range(T + 2):
                            if i < T:
                                t = i
                                pe.wait_ge(ctxA_in[t % 2], 16 * (t // 2 + 1))
                                if t == 0:
                                    pe.wait_ge(act_done, A["n0", "T", T - 1])
                                else:
                                    pe.wait_ge(vec_done, V["valM", t - 1])
                                for f in range(2):
                                    for k in range(KT):
                                        ins = mm(ps[:, f, :], kt("wk0")[:, k, f * P:(f + 1) * P],
                                                 ctxA[t % 2][:, k, :, f * P:(f + 1) * P], start=k == 0, stop=k == KT - 1)
                                    ins.then_inc(pe_done, PE.step("k0", t, f))
                            if 1 <= i <= T:
                                t = i - 1
                                pe.wait_ge(act_done, A["exp0", t])
                                if t >= 2:
                                    pe.wait_ge(vec_done, V["x1", t - 2])
                                if t == 0:
                                    pe.wait_ge(act_done, A["qT", 1])
                                for f in range(2):
                                    ins = tr(ps[:, 3, f * P:(f + 1) * P], pbA[:, t % 2, f * P:(f + 1) * P], ident)
                                ins.then_inc(pe_done, PE.step("pT0", t))
                                pe.wait_ge(act_done, A["pT0", t])
                                pe.wait_ge(vec_done, V["valM", t])
                                if t >= 1:
                                    pe.wait_ge(vec_done, V["l0", "o", t - 1])
                                for b in range(BT):
                                    for f in range(2):
                                        ins = mm(ps[S * b:S * (b + 1), 4, f * P:(f + 1) * P],
                                                 pTA[:, t % 2, f * P + S * b:f * P + S * (b + 1)],
                                                 valM[:, t % 2, f, b, :], start=True, stop=True)
                                ins.then_inc(pe_done, PE.step("pv0", t))
                            if i < T:
                                t = i
                                for f in range(2):
                                    pe.wait_ge(vec_done, V["keyT", t, f])
                                    for b in range(BT):
                                        for k in range(KT):
                                            ins = mm(ps[:, f, b * P:(b + 1) * P], ctxA[t % 2][:, k, b, f * P:(f + 1) * P],
                                                     kt("wv0")[:, k, f * P:(f + 1) * P], start=k == 0, stop=k == KT - 1)
                                ins.then_inc(pe_done, PE.step("v0", t))
                                pe.wait_ge(act_done, A["qT", 1])
                                if t >= 1:
                                    pe.wait_ge(vec_done, V["sub0", t - 1])
                                for b in range(BT):
                                    for f in range(2):
                                        ins = mm(ps[S * b:S * (b + 1), 2, f * P:(f + 1) * P],
                                                 qT[:, f, t * P + S * b:t * P + S * (b + 1)],
                                                 keyT[:, t % 2, f, b * P:(b + 1) * P], start=True, stop=True)
                                ins.then_inc(pe_done, PE.step("s0", t))
                            if i >= 2:
                                t = i - 2
                                pe.wait_ge(vec_done, V["l0", "o", t])
                                if t + 1 < T:
                                    pe.wait_ge(act_done, A["pT0", t + 1])
                                if t >= 1:
                                    pe.wait_ge(vec_done, V["x1", t - 1])
                                out_proj("l0", t, 3, obA, oTA, "wo0")
                            yield

                        yield from norm("n1", xnA, (0, 1), vec_done, V, ("n1",))
                        for i in range(T + 1):
                            if i < T:
                                t = i
                                pe.wait_ge(act_done, A["n1", "T", t])
                                pe.wait_ge(vec_done, V["x1", T - 1])
                                if t >= 2:
                                    pe.wait_ge(vec_done, V["dg", t - 2])
                                project(ps[:, 2 + t % 2, 0:D + 3], aTA, t, kt("wv1"), slice(0, D + 3)).then_inc(pe_done, PE.step("v1", t))
                            if i >= 1:
                                t = i - 1
                                pe.wait_ge(vec_done, V["dg", t])
                                if t >= 1:
                                    pe.wait_ge(vec_done, V["sq", t - 1])
                                mm(ps[:, 4, 0:96], w["blockones"], dg[:, t % 2, :], start=True,
                                   stop=True).then_inc(pe_done, PE.step("pos", t))
                            yield
                        for i in range(T + 2):
                            if i < T:
                                t = i
                                pe.wait_ge(vec_done, V["attT", t])
                                pe.wait_ge(act_done, A["valA", t])
                                if t >= 2:
                                    pe.wait_ge(vec_done, V["l1", "o", t - 2])
                                mm(ps[:, t % 2, 0:D + 1], attT[:, t % 2, :], valA[:, t, :], start=True,
                                   stop=True).then_inc(pe_done, PE.step("av1", t))
                            if i >= 2:
                                t = i - 2
                                pe.wait_ge(vec_done, V["l1", "o", t])
                                if t >= 2:
                                    pe.wait_ge(vec_done, V["x2", t - 2])
                                out_proj("l1", t, 2 + t % 2, obA, oTA, "wo1")
                            yield

                        yield from norm("n2", xnA, (0, 1), vec_done, V, ("n2",))
                        for t in range(T):
                            pe.wait_ge(act_done, A["n2", "T", t])
                            ins = project(ps[:, 4, t * NE:(t + 1) * NE], aTA, t, kt("router"), slice(0, NE))
                        ins.then_inc(pe_done, PE.step("router"))
                        yield
                        for e in range(NE + 2):
                            for f in range(4):
                                n = e * 4 + f
                                if e <= NE:
                                    we = stream[:, e % 2, :]
                                    if f == 0:
                                        pe.wait_ge(gu_in[e % 2], 16 * (e // 2 + 1))
                                    if n >= 2:
                                        pe.wait_ge(vec_done, V["hid", n - 2])
                                    for u in range(2):
                                        for k in range(KT):
                                            c = (u * KT + k) * HID + f * P
                                            ins = mm(ps[:, 2 * (f % 2) + u, :], we[:, c:c + P], aTA[:, k, :], start=k == 0, stop=k == KT - 1)
                                    ins.then_inc(pe_done, PE.step("gu", n))
                                if e >= 1 and f % 2 == 0:
                                    we = stream[:, (e - 1) % 2, 2048:EW].rearrange("p (f d) -> p f d", f=HID // P)
                                    if f == 0:
                                        pe.wait_ge(dn_in[(e - 1) % 2], 16 * ((e - 1) // 2 + 1))
                                        pe.wait_ge(vec_done, V["hid", e * 4 - 1])
                                    if e == 1 and f == 0:
                                        pe.wait_ge(vec_done, V["logits"])
                                    elif f == 0:
                                        pe.wait_ge(vec_done, V["acc", e - 2, 3])
                                    else:
                                        pe.wait_ge(vec_done, V["acc", e - 1, 1])
                                    for t in (f, f + 1):
                                        for j in range(HID // P):
                                            ins = mm(ps[:, 4, (t % 2) * D:(t % 2 + 1) * D], hE[:, (e - 1) % 2, j, t * P:(t + 1) * P],
                                                     we[:, j, :], start=j == 0, stop=j == HID // P - 1)
                                    ins.then_inc(pe_done, PE.step(*(("down", e - 1) if f else ("down", e - 1, 1))))
                                yield

                    def back():
                        yield from norm("y0", xnB, (5, 6), vec_done, V, ("y0",))
                        for i in range(T + 2):
                            if i < T:
                                t = i
                                pe.wait_ge(act_done, A["y0", "T", t if t else 2])
                                if t >= 1:
                                    pe.wait_ge(vec_done, V["cs", t - 1])
                                for k in range(KT):
                                    ins = mm(ps[:, 5, 0:P], aTB[:, k, t * P:(t + 1) * P], aTB[:, k, t * P:(t + 1) * P],
                                             start=k == 0, stop=k == KT - 1)
                                ins.then_inc(pe_done, PE.step("cs", t))
                            if 1 <= i <= T:
                                t = i - 1
                                pe.wait_ge(act_done, A["cexp", t])
                                pe.wait_ge(act_done, A["cpT", t - 1] if t else A["y0", "T", 3])
                                tr(ps[:, 6, 0:P], pb[:, t % 2, 0:P], ident).then_inc(pe_done, PE.step("cpT", t))
                            if i >= 2:
                                t = i - 2
                                pe.wait_ge(act_done, A["cpT", t])
                                if t >= 1:
                                    pe.wait_ge(vec_done, V["y1p", t - 1])
                                mm(ps[:, 7, 0:D], pT[:, t % 2, 0:P], xnB[:, t, :], start=True,
                                   stop=True).then_inc(pe_done, PE.step("cpv", t))
                            yield

                        yield from norm("y1", xnB, (5, 6), pool_done, O, ("y1",))
                        for i in range(T + 2):
                            if i < T:
                                t = i
                                pe.wait_ge(act_done, A["y1", "T", t if t else 2])
                                pe.wait_ge(ctxB_in[t % 2], 16 * (t // 2 + 1))
                                if t >= 1:
                                    pe.wait_ge(act_done, A["xexp", t - 1])
                                for b in range(BT):
                                    for k in range(KT):
                                        ins = mm(ps[S * b:S * (b + 1), 5, 0:NK], aTB[:, k, t * P + S * b:t * P + S * (b + 1)],
                                                 ctxB[:, t % 2, k, b, :], start=k == 0, stop=k == KT - 1)
                                ins.then_inc(pe_done, PE.step("xs", t))
                            if 1 <= i <= T:
                                t = i - 1
                                pe.wait_ge(vec_done, V["w4", t])
                                pe.wait_ge(act_done, A["xpT", t - 1] if t else A["y1", "T", 3])
                                for f in range(2):
                                    tr(ps[:, 6, f * P:(f + 1) * P], pb[:, t % 2, f * P:(f + 1) * P], ident)
                                tr(ps[0:BT, 6, 256:384], w4[:, t % 2, :], ident).then_inc(pe_done, PE.step("xpT", t))
                            if i >= 2:
                                t = i - 2
                                pe.wait_ge(act_done, A["xpT", t])
                                pe.wait_ge(ctxN_in[t % 2], 16 * (t // 2 + 1))
                                if t == 0:
                                    pe.wait_ge(ctxl_in, 16)
                                if t >= 1:
                                    pe.wait_ge(vec_done, V["y2p", t - 1])
                                mm(ps[:, 7, 0:D], pT[0:BT, t % 2, 256:384], ctxL[0:BT, t, :], start=True, stop=False,
                                   skip_group_check=True)
                                for b in range(BT):
                                    for f in range(2):
                                        ins = mm(ps[S * b:S * (b + 1), 7, 0:D], pT[:, t % 2, f * P + S * b:f * P + S * (b + 1)],
                                                 ctxN[:, t % 2, f, b, :], start=False, stop=f == 1, skip_group_check=True)
                                ins.then_inc(pe_done, PE.step("xpv", t))
                            yield

                        def ffn(tag, w1, w2):
                            for f in range(FF // P):
                                if f == 0:
                                    pe.wait_ge(act_done, A[tag, "T", T - 1])
                                if f >= 2:
                                    pe.wait_ge(act_done, A[tag, "relu", f - 2])
                                for k in range(KT):
                                    ins = mm(ps[:, 5 + f % 2, :], kt(w1)[:, k, f * P:(f + 1) * P], aTB[:, k, :], start=k == 0, stop=k == KT - 1)
                                ins.then_inc(pe_done, PE.step(tag, "f1", f))
                                yield
                            w2v = w[w2].rearrange("p (f d) -> p f d", f=FF // P)
                            pe.wait_ge(act_done, A[tag, "relu", FF // P - 1])
                            for t in range(T + 1):
                                if t < T:
                                    if t >= 2:
                                        pe.wait_ge(vec_done, V[tag, "f2", t - 2])
                                    for f in range(FF // P):
                                        ins = mm(ps[:, (7, 5)[t % 2], 0:D], hF[:, f, t * P:(t + 1) * P], w2v[:, f, :],
                                                 start=f == 0, stop=f == FF // P - 1)
                                    ins.then_inc(pe_done, PE.step(tag, "f2", t))
                                yield

                        yield from norm("y2", xnB, (5, 6), pool_done, O, ("y2",))
                        yield from ffn("y2", "w1x", "w2x")
                        for _ in range(5):
                            yield

                        def qkv_proj(t):
                            pe.wait_ge(act_done, A["h1", "T", T - 1])
                            if t >= 1:
                                pe.wait_ge(act_done, A["qkv", t - 1])
                            project(ps[:, 5, :], aTB, t, kt("wqkv"), slice(0, 512))
                            project(ps[:, 6, 0:D], aTB, t, kt("wqkv"), slice(512, 768)).then_inc(pe_done, PE.step("qkv", t))
                        yield from norm("h1", hh, (5, 6), pool_done, O, ("h1",), lambda: qkv_proj(0))
                        for i in range(T + 2):
                            yield
                            yield
                            if i + 1 < T:
                                qkv_proj(i + 1)
                            if i >= 2:
                                t = i - 2
                                pe.wait_ge(vec_done, V["l4", "o", t])
                                if t >= 1:
                                    pe.wait_ge(vec_done, V["conn", t - 1])
                                out_proj("l4", t, 7, ob, oTB, "wo2")
                            yield
                            yield

                        yield from norm("h2", hh, (5, 6), pool_done, O, ("h2",))
                        yield from ffn("h2", "w1a", "w2a")

                        def sim(t):
                            pe.wait_ge(act_done, A["n5", "T", T - 1])
                            if t >= 1:
                                pe.wait_ge(vec_done, V["rep64", t - 1])
                            project(ps[:, 5, :], aTB, t, cmat, slice(0, 512))
                            project(ps[:, 6, :], aTB, t, cmat, slice(512, 1024)).then_inc(pe_done, PE.step("sim", t))
                        yield from norm("n5", xnB, (5, 6), vec_done, V, ("n5",), lambda: sim(0))
                        for i in range(T + 1):
                            if i == 0:
                                pe.wait_ge(vec_done, V["h2", "f2", T - 2])
                                for t in range(T):
                                    ins = project(ps[:, 7, t * NP:(t + 1) * NP], aTB, t, kt("wd50"), slice(0, NP))
                                ins.then_inc(pe_done, PE.step("h50"))
                            if i >= 1:
                                t = i - 1
                                pe.wait_ge(vec_done, V["u50", t])
                                if t >= 1:
                                    pe.wait_ge(vec_done, V["x6", t - 1])
                                tr(ps[0:NP, 7, 256:384], u50[:, t % 2, :], ident).then_inc(pe_done, PE.step("uT", t))
                            yield
                            if i >= 1:
                                t = i - 1
                                pe.wait_ge(act_done, A["uT", t])
                                mm(ps[:, 7, 0:D], pT[0:NP, t % 2, 0:P], w["wu50"][0:NP, :], start=True,
                                   stop=True).then_inc(pe_done, PE.step("up", t))
                            if i + 1 < T:
                                sim(i + 1)
                            yield
                            yield

                    run(front(), back())

                @block.scalar
                def _(act):
                    sa = nc.scalar.activation

                    def norm(tag, aT, banks, reader, then=None):
                        yield
                        yield
                        if reader:
                            act.wait_ge(pe_done, PE[reader])
                        for t in range(T):
                            act.wait_ge(pe_done, PE[tag, "T", t])
                            nc.scalar.copy(aT[:, :, t * P:(t + 1) * P], ps[:, banks[t % 2], 0:KT * P].rearrange(
                                "p (k n) -> p k n", k=KT)).then_inc(act_done, A.step(tag, "T", t))
                        if then:
                            then()
                        yield

                    def o_turn(tag, t, oT, bank):
                        act.wait_ge(pe_done, PE[tag, "oT", t])
                        if t >= 2:
                            act.wait_ge(pe_done, PE[tag, "wo", t - 2])
                        nc.scalar.copy(oT[:, t % 2].rearrange("p k n -> p (k n)"), ps[:, bank, 256:512]).then_inc(
                            act_done, A.step(tag, "oT", t))

                    def front():
                        yield from norm("n0", aTA, (0, 1), None)
                        for f in range(2):
                            act.wait_ge(pe_done, PE["q0", f])
                            sa(qT[:, f, :], ps[:, 2 + f, :], ACT.Identity, bias=w["bq0"][:, f:f + 1]).then_inc(act_done, A.step("qT", f))
                        yield
                        for i in range(T + 2):
                            if 1 <= i <= T:
                                t = i - 1
                                act.wait_ge(pe_done, PE["pT0", t])
                                if t >= 2:
                                    act.wait_ge(pe_done, PE["pv0", t - 2])
                                nc.scalar.copy(pTA[:, t % 2, :], ps[:, 3, 0:256]).then_inc(act_done, A.step("pT0", t))
                            if i < T:
                                act.wait_ge(vec_done, V["sub0", i])
                                sa(pbA[:, i % 2, :], pbA[:, i % 2, :], ACT.Exp, scale=0.25).then_inc(act_done, A.step("exp0", i))
                            if i >= 2:
                                o_turn("l0", i - 2, oTA, 3)
                            yield
                        yield from norm("n1", aTA, (0, 1), ("q0", 1))
                        for i in range(T + 1):
                            if i < T:
                                act.wait_ge(pe_done, PE["v1", i])
                                nc.scalar.copy(valA[:, i, 0:D], ps[:, 2 + i % 2, 0:D]).then_inc(act_done, A.step("valA", i))
                            else:
                                act.wait_ge(vec_done, V["sq", T - 1])
                                sa(dist, dist, ACT.Sqrt).then_inc(act_done, A.step())
                                act.wait_ge(act_done, A.n)
                                sa(dist, dist, ACT.Exp, scale=-0.25).then_inc(act_done, A.step("dexp"))
                            yield
                        for i in range(T + 2):
                            if i >= 2:
                                o_turn("l1", i - 2, oTA, 2 + i % 2)
                            yield
                        yield from norm("n2", aTA, (0, 1), ("v1", T - 1))
                        act.wait_ge(vec_done, V["lsub"])
                        sa(ex, ex, ACT.Exp).then_inc(act_done, A.step("lexp"))
                        yield
                        for e in range(NE + 2):
                            for f in range(4):
                                if e <= NE:
                                    n = e * 4 + f
                                    act.wait_ge(pe_done, PE["gu", n])
                                    if f == 0 and e >= 2:
                                        act.wait_ge(pe_done, PE["down", e - 2])
                                    sa(hE[:, e % 2, f, :], ps[:, 2 * (f % 2), :], ACT.Silu).then_inc(act_done, A.step("silu", n))
                                yield

                    def back():
                        yield from norm("y0", aTB, (5, 6), None)
                        for i in range(T + 2):
                            if i < T:
                                t = i
                                act.wait_ge(vec_done, V["cmax", t])
                                sa(pb[:, t % 2, 0:P], pb[:, t % 2, 0:P], ACT.Exp, bias=nm[:, t:t + 1],
                                   accum_out=rs[:, t:t + 1]).then_inc(act_done, A.step("cexp", t))
                            if 1 <= i <= T:
                                t = i - 1
                                act.wait_ge(pe_done, PE["cpT", t])
                                if t >= 2:
                                    act.wait_ge(pe_done, PE["cpv", t - 2])
                                nc.scalar.copy(pT[:, t % 2, 0:P], ps[:, 6, 0:P]).then_inc(act_done, A.step("cpT", t))
                            yield
                        yield from norm("y1", aTB, (5, 6), ("cs", T - 1))
                        for i in range(T + 2):
                            if i < T:
                                t = i
                                act.wait_ge(vec_done, V["xmax", t])
                                if t >= 2:
                                    act.wait_ge(pe_done, PE["xpT", t - 2])
                                    act.wait_ge(vec_done, V["w4", t - 2])
                                sa(pb[:, t % 2, 0:NK], ps[:, 5, 0:NK], ACT.Exp, bias=nm[:, t:t + 1], scale=1.0 / 16,
                                   accum_out=rs[:, t:t + 1]).then_inc(act_done, A.step("xexp", t))
                            if 1 <= i <= T:
                                t = i - 1
                                act.wait_ge(pe_done, PE["xpT", t])
                                if t >= 2:
                                    act.wait_ge(pe_done, PE["xpv", t - 2])
                                nc.scalar.copy(pT[:, t % 2, 0:256], ps[:, 6, 0:256]).then_inc(act_done, A.step())
                                nc.scalar.copy(pT[0:BT, t % 2, 256:384], ps[0:BT, 6, 256:384]).then_inc(act_done, A.step("xpT", t))
                            yield

                        def ffn(tag, b1):
                            for f in range(FF // P):
                                act.wait_ge(pe_done, PE[tag, "f1", f])
                                sa(hF[:, f, :], ps[:, 5 + f % 2, :], ACT.Relu, bias=w[b1][:, f:f + 1]).then_inc(act_done, A.step(tag, "relu", f))
                                yield
                            for _ in range(T + 1):
                                yield

                        yield from norm("y2", aTB, (5, 6), ("xs", T - 1))
                        yield from ffn("y2", "b1x")
                        for _ in range(5):
                            yield

                        def qkv_copy(t):
                            act.wait_ge(pe_done, PE["qkv", t])
                            if t >= 2:
                                act.wait_ge(vec_done, V["pprod", t - 2])
                                act.wait_ge(pool_done, O["pprod", t - 2])
                            nc.scalar.copy(qkv[:, t % 2, 0:512], ps[:, 5, :]).then_inc(act_done, A.step())
                            nc.scalar.copy(qkv[:, t % 2, 512:768], ps[:, 6, 0:256]).then_inc(act_done, A.step("qkv", t))
                        yield from norm("h1", aTB, (5, 6), ("y2", "f1", FF // P - 1), lambda: qkv_copy(0))
                        for i in range(T + 2):
                            yield
                            yield
                            if i + 1 < T:
                                qkv_copy(i + 1)
                            if i >= 2:
                                o_turn("l4", i - 2, oTB, 7)
                            yield
                            if i < T:
                                act.wait_ge(vec_done, V["dsub", i])
                                sa(sc[:, i % 2, :], sc[:, i % 2, :], ACT.Exp, scale=8.0 ** -0.5).then_inc(act_done, A.step("dexp2", i))
                            yield
                        yield from norm("h2", aTB, (5, 6), ("qkv", T - 1))
                        yield from ffn("h2", "b1a")
                        yield from norm("n5", aTB, (5, 6), ("h2", "f1", FF // P - 1))
                        for i in range(T + 1):
                            if i == 0:
                                act.wait_ge(pe_done, PE["h50"])
                                sa(g50, ps[:, 7, 0:T * NP], ACT.Gelu).then_inc(act_done, A.step("g50"))
                            if i >= 1:
                                t = i - 1
                                act.wait_ge(pe_done, PE["uT", t])
                                if t >= 2:
                                    act.wait_ge(pe_done, PE["up", t - 2])
                                nc.scalar.copy(pT[0:NP, t % 2, 0:P], ps[0:NP, 7, 256:384]).then_inc(act_done, A.step("uT", t))
                            yield
                            if i < T:
                                act.wait_ge(vec_done, V["csub", i])
                                sa(cexp[:, i % 2], cexp[:, i % 2], ACT.Exp).then_inc(act_done, A.step("cexp2", i))
                            yield
                            yield

                    run(front(), back())

                @block.vector
                def _(v):
                    vv = nc.vector

                    def own_steps():
                        v.wait_ge(vec_done, V.n)

                    def norm(tag, src, dst, small, gain=None, before=None, turned=None, slots=3):
                        st, mv, ve, rstd = small
                        if before:
                            before()
                        for t in range(T):
                            if t == 0 and V.n:
                                own_steps()
                            vv.bn_stats(st[:, t, :], src[:, t, :]).then_inc(vec_done, V.step(tag, "st", t))
                        for t in range(T):
                            v.wait_ge(vec_done, V[tag, "st", t])
                            vv.bn_aggr(mv[:, t, :], st[:, t, :]).then_inc(vec_done, V.step())
                        own_steps()
                        vv.tensor_scalar(ve, mv[:, :, 1], EPS, None, ALU.add).then_inc(vec_done, V.step(tag, "var"))
                        yield
                        v.wait_ge(pool_done, O[tag, "rstd"])
                        for t in range(T):
                            if turned:
                                v.wait_ge(pe_done, PE[turned, "T", t])
                            vv.tensor_scalar(dst[:, t, :], src[:, t, :], mv[:, t, 0:1], rstd[:, t:t + 1], ALU.subtract,
                                             ALU.mult).then_inc(vec_done, V.step(tag, t))
                        if gain:
                            for t in range(T):
                                v.wait_ge(vec_done, V[tag, t])
                                vv.tensor_tensor(dst[:, t, :], dst[:, t, :], w[gain], ALU.mult).then_inc(vec_done, V.step(tag, "g", t))
                        for _ in range(slots - 1):
                            yield

                    smallA, smallB = (stA, mvA, veA, rstdA), (stB, mvB, veB, rstdB)

                    def front():
                        yield from norm("n0", xA, xnA, smallA, before=lambda: v.wait_ge(x_in, 16))
                        yield
                        hm = w["headmask"].unsqueeze(1)
                        for i in range(T + 2):
                            if i < T:
                                t = i
                                if t >= 2:
                                    v.wait_ge(pe_done, PE["s0", t - 2])
                                for f in range(2):
                                    v.wait_ge(pe_done, PE["k0", t, f])
                                    vv.scalar_tensor_tensor(keyT[:, t % 2, f, :].rearrange("p (b n) -> p b n", b=BT),
                                                            ps[:, f, :].rearrange("p (b n) -> p b n", b=BT), w["bk0"][:, f:f + 1],
                                                            hm.broadcast_to([P, BT, P]), ALU.add,
                                                            ALU.mult).then_inc(vec_done, V.step("keyT", t, f))
                            if 1 <= i <= T:
                                t = i - 1
                                v.wait_ge(act_done, A["exp0", t])
                                own_steps()
                                vv.tensor_reduce(smA, pbA[:, t % 2, :].rearrange("p (h l) -> p h l", h=H), AX.X,
                                                 ALU.add).then_inc(vec_done, V.step())
                                own_steps()
                                vv.reciprocal(riA, smA).then_inc(vec_done, V.step())
                                own_steps()
                                v.wait_ge(pe_done, PE["pv0", t])
                                if t >= 2:
                                    v.wait_ge(pe_done, PE["l0", "oT", t - 2])
                                vv.tensor_tensor(obA[:, t % 2, :].rearrange("p (h l) -> p h l", h=H),
                                                 ps[:, 4, 0:256].rearrange("p (h l) -> p h l", h=H), b16(riA, 16),
                                                 ALU.mult).then_inc(vec_done, V.step("l0", "o", t))
                            if i < T:
                                t = i
                                v.wait_ge(pe_done, PE["v0", t])
                                if t >= 2:
                                    v.wait_ge(pe_done, PE["pv0", t - 2])
                                vv.tensor_tensor(valM[:, t % 2].rearrange("p f b n -> p (f b) n"),
                                                 ps[:, 0:2, :].rearrange("p f (b n) -> p (f b) n", b=BT),
                                                 hm.broadcast_to([P, 2 * BT, P]), ALU.mult).then_inc(vec_done, V.step("valM", t))
                                v.wait_ge(pe_done, PE["s0", t])
                                if t >= 2:
                                    v.wait_ge(pe_done, PE["pT0", t - 2])
                                sv = ps[:, 2, 0:256].rearrange("p (h l) -> p h l", h=H)
                                own_steps()
                                vv.tensor_reduce(mxA, sv, AX.X, ALU.max).then_inc(vec_done, V.step())
                                own_steps()
                                vv.tensor_tensor(pbA[:, t % 2, :].rearrange("p (h l) -> p h l", h=H), sv, b16(mxA, 16),
                                                 ALU.subtract).then_inc(vec_done, V.step("sub0", t))
                            if i >= 2:
                                t = i - 2
                                v.wait_ge(pe_done, PE["l0", "wo", t])
                                v.wait_ge(pool_done, O["xbn0", t])
                                vv.tensor_tensor(xA[:, t, :], ps[:, 3, 0:D], xA[:, t, :], ALU.add).then_inc(vec_done, V.step("x1", t))
                            yield

                        yield from norm("n1", xA, xnA, smallA, turned="n0")
                        e3 = w["eye32"].unsqueeze(1).broadcast_to([P, 3, S])
                        for i in range(T + 1):
                            if i == 0:
                                own_steps()
                                v.wait_ge(pe_done, PE["pv0", T - 1])
                                vv.memset(valA[:, :, D:D + 1], 1.0).then_inc(vec_done, V.step())
                            if i < T:
                                t = i
                                v.wait_ge(act_done, A["valA", t])
                                vv.tensor_tensor(pos[:, t, :], ps[:, 2 + t % 2, D:D + 3], w["b3d"], ALU.add).then_inc(vec_done, V.step())
                                own_steps()
                                if t >= 2:
                                    v.wait_ge(pe_done, PE["pos", t - 2])
                                vv.tensor_tensor(dg[:, t % 2, :].rearrange("p (c j) -> p c j", c=3), b16(pos[:, t, :], S), e3,
                                                 ALU.mult).then_inc(vec_done, V.step("dg", t))
                            if i >= 1:
                                t = i - 1
                                v.wait_ge(pe_done, PE["pos", t])
                                pv = ps[:, 4, 0:96].rearrange("p (c j) -> p c j", c=3)
                                d3 = df.rearrange("p (c j) -> p c j", c=3)
                                own_steps()
                                vv.tensor_tensor(d3, pv, e3, ALU.mult).then_inc(vec_done, V.step())
                                own_steps()
                                vv.tensor_reduce(own, d3, AX.X, ALU.add).then_inc(vec_done, V.step())
                                own_steps()
                                vv.tensor_tensor(d3, pv, b16(own, S), ALU.subtract).then_inc(vec_done, V.step())
                                own_steps()
                                vv.tensor_tensor(df, df, df, ALU.mult).then_inc(vec_done, V.step())
                                own_steps()
                                vv.tensor_reduce(dist[:, t, :], df.rearrange("p (c j) -> p j c", c=3), AX.X, ALU.add).then_inc(vec_done, V.step("sq", t))
                            yield
                        for i in range(T + 2):
                            if i == 0:
                                v.wait_ge(act_done, A["dexp"])
                                own_steps()
                            if i < T:
                                t = i
                                if t >= 2:
                                    v.wait_ge(pe_done, PE["av1", t - 2])
                                vv.tensor_tensor(attT[:, t % 2, :].rearrange("p (b j) -> p b j", b=BT),
                                                 dist[:, t, :].unsqueeze(1).broadcast_to([P, BT, S]),
                                                 w["causalT"].rearrange("p (b j) -> p b j", b=BT), ALU.mult).then_inc(vec_done, V.step("attT", t))
                            if 1 <= i <= T:
                                t = i - 1
                                v.wait_ge(pe_done, PE["av1", t])
                                own_steps()
                                vv.reciprocal(riA[:, 0:1], ps[:, t % 2, D:D + 1]).then_inc(vec_done, V.step())
                                own_steps()
                                if t >= 2:
                                    v.wait_ge(pe_done, PE["l1", "oT", t - 2])
                                vv.tensor_scalar(obA[:, t % 2, :], ps[:, t % 2, 0:D], riA[:, 0:1], None,
                                                 ALU.mult).then_inc(vec_done, V.step("l1", "o", t))
                            if i >= 2:
                                t = i - 2
                                v.wait_ge(pe_done, PE["l1", "wo", t])
                                v.wait_ge(pool_done, O["xbn1", t])
                                vv.tensor_tensor(xA[:, t, :], ps[:, 2 + t % 2, 0:D], xA[:, t, :], ALU.add).then_inc(vec_done, V.step("x2", t))
                            yield

                        yield from norm("n2", xA, xnA, smallA, turned="n1")
                        v.wait_ge(pe_done, PE["router"])
                        vv.tensor_copy(lg[:, :, 0:NE], ps[:, 4, 0:T * NE].rearrange("p (t n) -> p t n", t=T)).then_inc(vec_done, V.step("logits"))
                        own_steps()
                        for t in range(T):
                            vv.max(m8[:, t, :], lg[:, t, :]).then_inc(vec_done, V.step())
                        own_steps()
                        for t in range(T):
                            vv.match_replace(lrep[:, t, :], m8[:, t, :], lg[:, t, :], NEG).then_inc(vec_done, V.step())
                        vv.tensor_tensor(ex, lg[:, :, 0:NE], m8[:, :, 6:7].broadcast_to([P, T, NE]), ALU.subtract).then_inc(vec_done, V.step("lsub"))
                        v.wait_ge(act_done, A["lexp"])
                        own_steps()
                        vv.scalar_tensor_tensor(comb, lrep[:, :, 0:NE], NEG, ex, ALU.is_equal, ALU.mult).then_inc(vec_done, V.step())
                        own_steps()
                        vv.tensor_reduce(smA[:, 0:T], comb, AX.X, ALU.add).then_inc(vec_done, V.step())
                        own_steps()
                        vv.reciprocal(riA[:, 0:T], smA[:, 0:T]).then_inc(vec_done, V.step())
                        own_steps()
                        vv.tensor_tensor(comb, comb, b16(riA[:, 0:T], NE), ALU.mult).then_inc(vec_done, V.step("comb"))
                        yield
                        for e in range(NE + 2):
                            for f in range(4):
                                if e >= 1 and f % 2 == 1:
                                    for t in (f - 1, f):
                                        c = (t % 2) * D
                                        v.wait_ge(pe_done, PE["down", e - 1] if f == 3 else PE["down", e - 1, 1])
                                        if e >= 2:
                                            v.wait_ge(vec_done, V["acc", e - 2, t])
                                        else:
                                            v.wait_ge(vec_done, V["comb"])
                                        if e - 1 < NE:
                                            vv.scalar_tensor_tensor(xA[:, t, :], ps[:, 4, c:c + D], comb[:, t, e - 1:e], xA[:, t, :],
                                                                    ALU.mult, ALU.add).then_inc(vec_done, V.step("acc", e - 1, t))
                                        else:
                                            vv.tensor_tensor(xA[:, t, :], ps[:, 4, c:c + D], xA[:, t, :], ALU.add).then_inc(vec_done, V.step("acc", e - 1, t))
                                if e <= NE:
                                    n = e * 4 + f
                                    v.wait_ge(act_done, A["silu", n])
                                    vv.tensor_tensor(hE[:, e % 2, f, :], ps[:, 2 * (f % 2) + 1, :], hE[:, e % 2, f, :], ALU.mult).then_inc(vec_done, V.step("hid", n))
                                yield

                    def back():
                        yield from norm("y0", xB, xnB, smallB)
                        for i in range(T + 2):
                            if i < T:
                                t = i
                                v.wait_ge(pe_done, PE["cs", t])
                                if t >= 2:
                                    v.wait_ge(pe_done, PE["cpT", t - 2])
                                vv.scalar_tensor_tensor(pb[:, t % 2, 0:P], ps[:, 5, 0:P], 1.0 / 16, w["causal"], ALU.mult,
                                                        ALU.add).then_inc(vec_done, V.step("cs", t))
                                own_steps()
                                vv.tensor_reduce(nm[:, t:t + 1], pb[:, t % 2, 0:P], AX.X, ALU.max, negate=True).then_inc(vec_done, V.step("cmax", t))
                            if i >= 2:
                                t = i - 2
                                v.wait_ge(act_done, A["cexp", t])
                                vv.reciprocal(ri[:, 0, t:t + 1], rs[:, t:t + 1]).then_inc(vec_done, V.step())
                                own_steps()
                                v.wait_ge(pe_done, PE["cpv", t])
                                vv.scalar_tensor_tensor(xnB[:, t, :], ps[:, 7, 0:D], ri[:, 0, t:t + 1], xnB[:, t, :], ALU.mult,
                                                        ALU.add).then_inc(vec_done, V.step("y1p", t))
                            yield

                        yield from norm("y1", xnB, xnB, smallB, gain="g1")
                        for i in range(T + 2):
                            if 1 <= i <= T:
                                t = i - 1
                                v.wait_ge(act_done, A["xexp", t])
                                if t >= 2:
                                    v.wait_ge(pe_done, PE["xpT", t - 2])
                                vv.tensor_scalar(w4[:, t % 2, :], w["blkind"], pb[:, t % 2, NK - 1:NK], None, ALU.mult).then_inc(vec_done, V.step("w4", t))
                            if i < T:
                                t = i
                                v.wait_ge(pe_done, PE["xs", t])
                                vv.tensor_reduce(nm2[:, t:t + 1], ps[:, 5, 0:NK], AX.X, ALU.max, negate=True).then_inc(vec_done, V.step())
                                own_steps()
                                vv.tensor_scalar(nm[:, t:t + 1], nm2[:, t:t + 1], 1.0 / 16, None, ALU.mult).then_inc(vec_done, V.step("xmax", t))
                            if i >= 2:
                                t = i - 2
                                if t == 0:
                                    own_steps()
                                vv.reciprocal(ri[:, 1, t:t + 1], rs[:, t:t + 1]).then_inc(vec_done, V.step())
                                own_steps()
                                v.wait_ge(pe_done, PE["xpv", t])
                                vv.scalar_tensor_tensor(xnB[:, t, :], ps[:, 7, 0:D], ri[:, 1, t:t + 1], xnB[:, t, :], ALU.mult,
                                                        ALU.add).then_inc(vec_done, V.step("y2p", t))
                            yield

                        def ffn(tag, ready, dst, key):
                            for _ in range(FF // P):
                                yield
                            for i in range(T + 1):
                                if i >= 1:
                                    t = i - 1
                                    v.wait_ge(pe_done, PE[tag, "f2", t])
                                    v.wait_ge(pool_done, O[ready, t])
                                    vv.tensor_tensor(dst[:, t, :], ps[:, (7, 5)[t % 2], 0:D], dst[:, t, :], ALU.add).then_inc(vec_done, V.step(tag, "f2", t))
                                yield

                        yield from norm("y2", xnB, xnB, smallB, gain="g2")
                        yield from ffn("y2", "y2b", xnB, None)
                        yield from norm("y3", xnB, xnB, smallB, gain="g3", slots=2)
                        for t in range(T):
                            v.wait_ge(pool_done, O["xbe3", t])
                            v.wait_ge(vec_done, V["y3", "g", t])
                            vv.tensor_tensor(xB[:, t, :], xB[:, t, :], xnB[:, t, :], ALU.add).then_inc(vec_done, V.step("x4", t))
                        yield

                        yield from norm("z", xB, xnB, smallB, slots=2)
                        yield from norm("h1", xnB, hh, smallB, gain="lg1", before=lambda: v.wait_ge(pe_done, PE["xpv", T - 1]))
                        for i in range(T + 2):
                            for c in range(4):
                                if i < T:
                                    t = i
                                    v.wait_ge(act_done, A["qkv", t])
                                    if c == 0:
                                        v.wait_ge(pe_done, PE["h1", "T", T - 1])
                                    own_steps()
                                    if c % 2 == 0:
                                        if c == 0 and 1 <= t:
                                            pass
                                        qk_product(vv, t, c).then_inc(vec_done, V.step())
                                        own_steps()
                                    else:
                                        v.wait_ge(pool_done, O["dprod", t, c])
                                    vv.tensor_reduce(sc[:, t % 2, c * 256:(c + 1) * 256],
                                                     prod[:, c % 2, :].rearrange("p (n d) -> p n d", d=8), AX.X,
                                                     ALU.add).then_inc(vec_done, V.step("dred", t, c))
                                if i < T and c == 3:
                                    s2 = sc[:, t % 2, :]
                                    s3 = s2.rearrange("p (q k) -> p q k", q=32)
                                    own_steps()
                                    vv.tensor_scalar(s2, s2, FMAX, -FMAX, ALU.min, ALU.max).then_inc(vec_done, V.step())
                                    own_steps()
                                    vv.tensor_reduce(sm[:, t % 2, :], s3, AX.X, ALU.max).then_inc(vec_done, V.step())
                                    own_steps()
                                    vv.tensor_tensor(s3, s3, b16(sm[:, t % 2, :], 32), ALU.subtract).then_inc(vec_done, V.step("dsub", t))
                                if 1 <= i <= T and c == 0:
                                    t = i - 1
                                    aa = a2[:, t % 2, :].rearrange("p (a h) -> p a h", a=16)
                                    v.wait_ge(act_done, A["dexp2", t])
                                    own_steps()
                                    s3 = sc[:, t % 2, :].rearrange("p (q k) -> p q k", q=32)
                                    vv.tensor_reduce(sm[:, t % 2, :], s3, AX.X, ALU.add).then_inc(vec_done, V.step())
                                    own_steps()
                                    vv.reciprocal(ri[:, t % 2, :], sm[:, t % 2, :]).then_inc(vec_done, V.step())
                                    own_steps()
                                    vv.tensor_scalar(ri[:, t % 2, 16:32], ri[:, t % 2, 16:32], neglam, None, ALU.mult).then_inc(vec_done, V.step())
                                    if t >= 2:
                                        v.wait_ge(pool_done, O["pprod", t - 2])
                                    vv.tensor_tensor(aa, s3[:, 0:16, 0:16], b16(ri[:, t % 2, 0:16], 16), ALU.mult).then_inc(vec_done, V.step())
                                    own_steps()
                                    e1 = s3[:, 16:32, 16:32]
                                    vv.tensor_tensor(e1, e1, b16(ri[:, t % 2, 16:32], 16), ALU.mult).then_inc(vec_done, V.step())
                                    own_steps()
                                    vv.tensor_tensor(aa, aa, e1, ALU.add).then_inc(vec_done, V.step("datt", t))
                                if 1 <= i <= T and c == 1:
                                    t = i - 1
                                    own_steps()
                                    pv_product(vv, t, 0).then_inc(vec_done, V.step("pprod", t))
                                    own_steps()
                                    if t >= 2:
                                        v.wait_ge(pe_done, PE["l4", "oT", t - 2])
                                    for j in range(2):
                                        if j:
                                            v.wait_ge(pool_done, O["pprod", t])
                                        vv.tensor_reduce(ob[:, t % 2, j * 128:(j + 1) * 128],
                                                         prod[:, j, :].rearrange("p (n h) -> p n h", h=16), AX.X,
                                                         ALU.add).then_inc(vec_done, V.step("pred", t, j))
                                    own_steps()
                                    vv.tensor_tensor(a2[:, t % 2, :], ob[:, t % 2, :], ob[:, t % 2, :], ALU.mult).then_inc(vec_done, V.step())
                                    own_steps()
                                    vv.tensor_reduce(mx[:, t % 2, 0:16], a2[:, t % 2, :].rearrange("p (a d) -> p a d", a=16), AX.X,
                                                     ALU.add).then_inc(vec_done, V.step())
                                    own_steps()
                                    vv.tensor_scalar(mx[:, t % 2, 16:32], mx[:, t % 2, 0:16], RMS / 16, EPS * RMS, ALU.mult,
                                                     ALU.add).then_inc(vec_done, V.step("rms", t))
                                if 1 <= i <= T and c == 2:
                                    t = i - 1
                                    v.wait_ge(pool_done, O["rms", t])
                                    o3 = ob[:, t % 2, :].rearrange("p (a d) -> p a d", a=16)
                                    vv.tensor_tensor(o3, o3, b16(mx[:, t % 2, 0:16], 16), ALU.mult).then_inc(vec_done, V.step("l4", "o", t))
                                if i >= 2 and c == 3:
                                    t = i - 2
                                    v.wait_ge(pe_done, PE["l4", "wo", t])
                                    v.wait_ge(pool_done, O["zb", t])
                                    vv.tensor_tensor(xnB[:, t, :], ps[:, 7, 0:D], xnB[:, t, :], ALU.add).then_inc(vec_done, V.step("conn", t))
                                yield
                        yield from norm("h2", xnB, hh, smallB, gain="lg2")
                        yield from ffn("h2", "xc", xB, None)

                        yield from norm("n5", xB, xnB, smallB)
                        for i in range(T + 1):
                            if i < T:
                                t = i
                                v.wait_ge(pe_done, PE["sim", t])
                                own_steps()
                                sim = ps[:, 5:7, :].rearrange("p s (a k) -> p (s a) k", a=8)
                                for a in range(NPH):
                                    vv.max(s16[:, a, 0:8], sim[:, a, :]).then_inc(vec_done, V.step())
                                for a in range(NPH):
                                    v.wait_ge(vec_done, V.n - NPH + 1)
                                    vv.match_replace(rep64[:, a, :], s16[:, a, 0:8], sim[:, a, :], NEG).then_inc(
                                        vec_done, V.step(*(("rep64", t) if a == NPH - 1 else ())))
                                for a in range(NPH):
                                    v.wait_ge(vec_done, V.n - NPH + 1)
                                    vv.max(s16[:, a, 8:16], rep64[:, a, :]).then_inc(vec_done, V.step())
                            yield
                            if i >= 1:
                                t = i - 1
                                v.wait_ge(pe_done, PE["up", t])
                                vv.tensor_tensor(xnB[:, t, :], ps[:, 7, 0:D], xB[:, t, :], ALU.add).then_inc(vec_done, V.step("x6", t))
                            if i < T:
                                t = i
                                own_steps()
                                sx, sy = s16[:, 0:8, :], s16[:, 8:16, :]
                                off = 0
                                for a0, a1 in ((0, 1), (1, 2), (2, 3), (3, 4), (4, 5), (5, 8), (8, 16)):
                                    na, nb = a1 - a0, TOP // a1
                                    c4 = cand[:, :, off:off + na * nb].rearrange("p h (a b) -> p h a b", a=na)
                                    vv.tensor_tensor(c4, sx[:, :, a0:a1].unsqueeze(3).broadcast_to([P, 8, na, nb]),
                                                     sy[:, :, 0:nb].unsqueeze(2).broadcast_to([P, 8, na, nb]),
                                                     ALU.add).then_inc(vec_done, V.step())
                                    off += na * nb
                                assert off == NP
                                own_steps()
                                for h in range(8):
                                    vv.max(cm[:, h, :], cand[:, h, :]).then_inc(vec_done, V.step())
                                own_steps()
                                vv.tensor_tensor(cexp[:, t % 2], cand, cm[:, :, 0:1].broadcast_to([P, 8, NP]), ALU.subtract).then_inc(vec_done, V.step("csub", t))
                                for h in range(8):
                                    vv.match_replace(rep1[:, h, :], cm[:, h, :], cand[:, h, :], NEG).then_inc(vec_done, V.step())
                            yield
                            if i < T:
                                t = i
                                for h in range(8):
                                    v.wait_ge(vec_done, V.n - 7)
                                    vv.max(cm2[:, h, :], rep1[:, h, :]).then_inc(vec_done, V.step())
                                for h in range(8):
                                    v.wait_ge(vec_done, V.n - 7)
                                    vv.match_replace(rep2[:, h, :], cm2[:, h, :], rep1[:, h, :], NEG).then_inc(vec_done, V.step())
                                own_steps()
                                v.wait_ge(act_done, A["cexp2", t])
                                cflat = cexp[:, t % 2].rearrange("p h n -> p (h n)")
                                vv.scalar_tensor_tensor(cflat, rep2.rearrange("p h n -> p (h n)"), NEG, cflat, ALU.is_equal, ALU.mult).then_inc(vec_done, V.step())
                                own_steps()
                                vv.tensor_reduce(sm[:, 0, 0:8], cexp[:, t % 2], AX.X, ALU.add).then_inc(vec_done, V.step())
                                own_steps()
                                vv.reciprocal(ri[:, 0, 0:8], sm[:, 0, 0:8]).then_inc(vec_done, V.step())
                                own_steps()
                                vv.tensor_tensor(cexp[:, t % 2], cexp[:, t % 2], b16(ri[:, 0, 0:8], NP), ALU.mult).then_inc(vec_done, V.step())
                                own_steps()
                                vv.tensor_reduce(phd[:, t % 2, :], cexp[:, t % 2].rearrange("p h n -> p n h"), AX.X, ALU.add).then_inc(vec_done, V.step())
                                own_steps()
                                if t >= 2:
                                    v.wait_ge(pe_done, PE["uT", t - 2])
                                v.wait_ge(act_done, A["g50"])
                                vv.tensor_tensor(u50[:, t % 2, :], phd[:, t % 2, :], g50[:, t * NP:(t + 1) * NP], ALU.mult).then_inc(vec_done, V.step("u50", t))
                            yield

                    run(front(), back())
                    if "f" in streams:
                        own_steps()
                        vv.tensor_copy(xB, xA).then_inc(vec_done, V.step())

            nc.gpsimd.sem_clear(range(first, last + 1))
            nc.all_engine_barrier()

        group(0, "f")
        with nc.Fori(1, G) as g:
            group(g, "fb")
        group(G, "b")


def lay_out(a):
    def kmaj(wt):
        k, n = wt.shape
        return wt.reshape(k // P, P, n).transpose(1, 0, 2).reshape(P, -1)

    def row(b):
        return np.broadcast_to(b.reshape(1, -1), (P, b.size))

    def col(b):
        return b.reshape(-1, P).T

    i = np.arange(P)
    blk = (i[:, None] // S) == (i[None, :] // S)
    out = {
        "wq0": kmaj(a["L0_xattn_Wq"].T), "wk0": kmaj(a["L0_xattn_Wk"].T), "wv0": kmaj(a["L0_xattn_Wv"].T),
        "wo0": kmaj(a["L0_xattn_Wo"].T), "bq0": col(a["L0_xattn_bq"]), "bk0": col(a["L0_xattn_bk"]),
        "bv0": col(a["L0_xattn_bv"]),
        "bo01": row(np.concatenate([a["L0_xattn_bo"], a["L0_attn_bo"]])),
        "wv1": kmaj(np.concatenate([a["L0_attn_wv"], a["L0_attn_w3d"]]).T), "wo1": kmaj(a["L0_attn_wo"].T),
        "bv1": col(a["L0_attn_bv"]), "b3d": row(a["L0_attn_b3d"]),
        "router": kmaj(a["L0_ffn_router_w"].T),
        "w1x": kmaj(a["L1_xattn_w1"]), "b1x": col(a["L1_xattn_b1"]), "w2x": kmaj(a["L1_xattn_w2"]),
        "b2x": row(a["L1_xattn_b2"]), "g1": row(a["L1_xattn_g1"]), "be1": row(a["L1_xattn_beta1"]),
        "g2": row(a["L1_xattn_g2"]), "be2": row(a["L1_xattn_beta2"]), "g3": row(a["L1_xattn_g3"]),
        "be3": row(a["L1_xattn_beta3"]),
        "wqkv": kmaj(np.concatenate([a["L1_attn_Wq"].reshape(16, 8, 2, D).transpose(2, 0, 1, 3).reshape(D, D),
                                     a["L1_attn_Wk"].reshape(16, 8, 2, D).transpose(2, 0, 1, 3).reshape(D, D),
                                     a["L1_attn_Wv"].reshape(16, 16, D).transpose(1, 0, 2).reshape(D, D)]).T),
        "wo2": kmaj(a["L1_attn_Wo"].T), "bo2": row(a["L1_attn_bo"]),
        "lg1": row(a["L1_attn_ln1_g"]), "lb1": row(a["L1_attn_ln1_b"]), "lg2": row(a["L1_attn_ln2_g"]),
        "lb2": row(a["L1_attn_ln2_b"]), "w1a": kmaj(a["L1_attn_W1"].T), "b1a": col(a["L1_attn_b1"]),
        "w2a": kmaj(a["L1_attn_W2"].T), "b2a": row(a["L1_attn_b2"]),
        "lqk": row(np.concatenate([a["L1_attn_" + n] for n in ("lq1", "lq2", "lk1", "lk2")])),
        "ident": np.eye(P), "headmask": (i[:, None] // H) == (i[None, :] // H), "blockones": blk,
        "causalT": blk & (i[None, :] >= i[:, None]), "causal": np.where(blk & (i[None, :] <= i[:, None]), 0.0, -1e30),
        "eye32": (i[:, None] % S) == np.arange(S)[None, :], "blkind": (i[:, None] // S) == np.arange(BT)[None, :],
        "wqp": a["L1_ffn_Wq"].reshape(NPH, P, D).transpose(1, 0, 2).reshape(P, -1),
        "keysp": a["L1_ffn_keys"].transpose(3, 2, 0, 1).reshape(P, -1),
    }
    rows = [p * TOP + q for p, q in PAIRS]
    out["wd50"] = kmaj(a["L1_ffn_W_down"][rows].T)
    wu = np.zeros((P, D), np.float32)
    wu[:NP] = a["L1_ffn_W_up"][rows]
    out["wu50"] = wu
    gate = [*a["L0_ffn_eg"], a["L0_ffn_sg"]]
    up = [*a["L0_ffn_eu"], a["L0_ffn_su"]]
    down = [*a["L0_ffn_ed"], a["L0_ffn_sd"]]
    out["experts"] = np.concatenate([np.concatenate([kmaj(x.T), kmaj(y.T), kmaj(z.T)], 1) for x, y, z in zip(gate, up, down)])
    out["x"] = a["x"].reshape(G, T, P, D).transpose(0, 2, 1, 3).reshape(G * P, T * D)
    order = [h + H * l for h in range(H) for l in range(NK // H)]
    c = a["ctx_1024"].reshape(G, T, BT, NK, D)
    cp = c[:, :, :, order + [NK - 1], :]
    out["ctxT"] = cp.reshape(G, T, BT, NK, KT, P).transpose(0, 5, 1, 4, 2, 3).reshape(G * P, -1)
    out["ctxN"] = c[:, :, :, order, :].reshape(G, T, BT, 2, P, D).transpose(0, 4, 1, 3, 2, 5).reshape(G * P, -1)
    out["ctxL"] = c[:, :, :, NK - 1, :].transpose(0, 2, 1, 3).reshape(G * BT, -1)
    return {k: np.ascontiguousarray(x, dtype=np.float32) for k, x in out.items()}


def kernel(**inputs):
    import concourse.bacc as bacc
    from concourse.bass_utils import run_bass_kernel_spmd

    arrays = lay_out({k: np.asarray(x) for k, x in inputs.items()})
    marks = {}
    for _ in range(2):
        nc = bacc.Bacc("TRN2", target_bir_lowering=False, num_devices=1)
        dram = {k: nc.dram_tensor("in_" + k, x.shape, F32, kind="ExternalInput").ap() for k, x in arrays.items()}
        dram["out"] = nc.dram_tensor("out_0", (G * P, T * D), F32, kind="ExternalOutput").ap()
        build(nc, marks, dram)
    r = run_bass_kernel_spmd(nc, [{"in_" + k: x for k, x in arrays.items()}], core_ids=[0])
    y = r.results[0]["out_0"]
    return y.reshape(G, P, T, D).transpose(0, 2, 1, 3).reshape(NB, S, D)
```

```python
from contextlib import ExitStack

import numpy as np
import concourse.bass as bass
from concourse import mybir

F32 = mybir.dt.float32
ALU = mybir.AluOpType
ACT = mybir.ActivationFunctionType
AX = mybir.AxisListType

NB, S, D = 128, 32, 256
P = 128
T = 4
BT = P // S
G = NB * S // (P * T)
KT = D // P
NK = 257
H = 16
HID, NE = 512, 8
FF = 1024
NPH, NKEY, TOP = 16, 64, 16
EPS = 1e-5
LAMBDA_INIT = 0.8 - 0.6 * float(np.exp(-0.3 * 1.0))
RMS = (1.0 - LAMBDA_INIT) ** -2
NEG = -3.0e38
PAD = 3.0e38
FMAX = 3.4028234663852886e38
PAIRS = [(a, b) for a in range(TOP) for b in range(TOP) if (a + 1) * (b + 1) <= TOP]
NP = len(PAIRS)
EW = 2 * KT * HID + (HID // P) * D


class Steps:

    def __init__(self, marks):
        self.n, self.marks = 0, marks

    def step(self, *name):
        self.n += 1
        if name:
            self.marks[name] = self.n
        return 1

    def __getitem__(self, name):
        return self.marks.get(name if isinstance(name, tuple) else (name,), 1)


EARLY = ("wq0", "wk0", "wv0", "wo0", "bq0", "bk0", "bv0", "wo1", "bv1", "lqk", "ident", "headmask")


def load_layout():
    return [("wq0", KT * D), ("wk0", KT * D), ("wv0", KT * D), ("wo0", KT * D), ("bq0", KT), ("bk0", KT),
            ("bv0", KT), ("wv1", KT * (D + 3)), ("wo1", KT * D), ("bv1", KT),
            ("b3d", 3), ("router", KT * NE), ("w1x", KT * FF), ("b1x", FF // P), ("w2x", FF // P * D),
            ("b2x", D), ("g1", D), ("be1", D), ("g2", D), ("be2", D), ("g3", D), ("be3", D),
            ("wqkv", KT * 3 * D), ("wo2", KT * D), ("bo2", D), ("lg1", KT), ("lb1", KT), ("lg2", KT),
            ("lb2", KT), ("g1c", KT), ("be1c", KT), ("g2c", KT), ("be2c", KT), ("w1a", KT * FF), ("b1a", FF // P), ("w2a", FF // P * D), ("b2a", D),
            ("wd50", KT * NP), ("wu50", D), ("lqk", 32), ("ident", P), ("headmask", P),
            ("blockones", P), ("causalT", P), ("causal", P), ("eye32", S), ("blkind", BT)]


ORDER = (
    "bbbbbfbbfbfbbbfbfbfbfbfbfbfffbbffbfbfbfbbfbbfbfbfbffbfffbfbfbbbbbfbfbbfbfbbfbbbbfbbfbbfbfbfbbfbf"
    "bfbbfbfbbffbbfbfbbfbfbbfbfbfbffbbbbbbfbbfbbbbbfbbbbbbfbbbbbbbbbbbbbbbbfbbbbfbbbbfbbfbbbbbfbbfbbf"
    "bbbffbbbbbbbfbbbbbbb")


def order(streams):
    return [s for s in ORDER if s in streams]


def build(nc, marks, dram):
    with ExitStack() as ctx:
        def sb(name, cols):
            return ctx.enter_context(nc.sbuf_tensor(name, [P, cols], F32))[:]

        def sem(name):
            return ctx.enter_context(nc.semaphore(name))

        w = {n: sb(n, c) for n, c in load_layout()}
        ps = ctx.enter_context(nc.psum_tensor("ps", [P, 8, 512], F32))
        def tiles(name, n=D):
            return sb(name, T * n).rearrange("p (t d) -> p t d", t=T)

        def pair(name, n):
            return sb(name, 2 * n).rearrange("p (s n) -> p s n", s=2)

        NCT = KT * BT * NK
        stream = pair("stream", EW)
        cmat = sb("cmat", KT * NPH * NKEY).rearrange("p (k n) -> p k n", k=KT)
        cvec = pair("cvec", D)
        xA = tiles("xA")
        aTA = sb("aTA", KT * 512).rearrange("p (k n) -> p k n", k=KT)
        hTA = sb("hTA", 4096)
        ctxA0 = sb("ctxA0", KT * BT * 256)
        pbA, pTA, obA = pair("pbA", D), pair("pTA", D), pair("obA", D)
        oTA = pair("oTA", D).rearrange("p s (k n) -> p s k n", k=KT)
        stA, mvA, veA, rstdA = tiles("stA", 6), tiles("mvA", 2), sb("veA", T), sb("rstdA", T)
        mrA, mrB = sb("mrA", T), sb("mrB", T)
        smA, riA, mxA = sb("smA", H), sb("riA", H), sb("mxA", H)
        pos, own = tiles("pos", 3), sb("own", 3)
        dist = tiles("dist", S)
        lg, lrep, m8 = tiles("lg", 14), tiles("lrep", 14), tiles("m8", 8)
        ex, comb = tiles("ex", NE), tiles("comb", NE)
        xB, xnB = tiles("xB"), tiles("xnB")
        aTB = sb("aTB", KT * 512).rearrange("p (k n) -> p k n", k=KT)
        hTB = sb("hTB", 4096)
        work = sb("work", 2 * NCT)
        sbuf = sb("sbuf", 2048)
        pb, pT, ob = pair("pb", NK), pair("pT", 384), pair("ob", D)
        oTB = pair("oTB", D).rearrange("p s (k n) -> p s k n", k=KT)
        stB, mvB, veB, rstdB = tiles("stB", 6), tiles("mvB", 2), sb("veB", T), sb("rstdB", T)
        mx, sm, ri = pair("mx", 32), pair("sm", 32), pair("ri", 32)
        rs, nm, nm2 = sb("rs", T), sb("nm", T), sb("nm2", T)
        w4 = pair("w4", BT)
        mhalf, neglam, lsum, ltmp = sb("mhalf", 16), sb("neglam", 1), sb("lsum", 2), sb("ltmp", 16)

        def kt(name):
            return w[name].rearrange("p (k n) -> p k n", k=KT)

        ctxA = [a.rearrange("p (k b n) -> p k b n", k=KT, b=BT) for a in (ctxA0, stream[:, 0, 0:2048])]
        keyT = stream[:, 1, 0:2048].rearrange("p (s f n) -> p s f n", s=2, f=2)
        qT = hTA[:, 0:1024].rearrange("p (k n) -> p k n", k=KT)
        valM = hTA[:, 1024:3072].rearrange("p (s f b n) -> p s f b n", s=2, f=2, b=BT)
        valA = hTA[:, 0:T * (D + 1)].rearrange("p (t n) -> p t n", t=T)
        attT = hTA[:, 1100:1100 + 2 * P].rearrange("p (s n) -> p s n", s=2)
        dg = hTA[:, 1400:1592].rearrange("p (s n) -> p s n", s=2)
        df = hTA[:, 1600:1696]
        xnA = hTA[:, 3072:4096].rearrange("p (t d) -> p t d", t=T)
        hE = hTA.rearrange("p (s f n) -> p s f n", s=2, f=HID // P)
        ctxB = work.rearrange("p (s k b n) -> p s k b n", s=2, k=KT, b=BT)
        ctxN = hTB.rearrange("p (s f b n) -> p s f b n", s=2, f=2, b=BT)
        ctxL = sbuf[:, 0:T * D].rearrange("p (t d) -> p t d", t=T)
        hF = hTB.rearrange("p (f n) -> p f n", f=FF // P)
        hh = sbuf[:, 0:T * D].rearrange("p (t d) -> p t d", t=T)
        prod = work[:, 0:4096].rearrange("p (s n) -> p s n", s=2)
        qkv = hTB[:, 0:2 * 3 * D].rearrange("p (s n) -> p s n", s=2)
        prodV = hTB[:, 2048:4096]
        sc = sbuf.rearrange("p (s n) -> p s n", s=2)
        a2 = pb[:, :, 0:D]
        wqp = hTB.rearrange("p (a d) -> p a d", a=NPH)
        keysp = work[:, 0:NPH * NKEY].rearrange("p (a k) -> p a k", a=NPH)
        rep64 = sbuf[:, 0:1024].rearrange("p (a k) -> p a k", a=NPH)
        s16 = sbuf[:, 1024:1280].rearrange("p (a k) -> p a k", a=NPH)
        cand = hTB[:, 0:8 * NP].rearrange("p (h n) -> p h n", h=8)
        rep1 = sbuf[:, 1280:1280 + 8 * NP].rearrange("p (h n) -> p h n", h=8)
        rep2 = hTB[:, 512:512 + 8 * NP].rearrange("p (h n) -> p h n", h=8)
        cexp = work[:, 0:2 * 8 * NP].rearrange("p (s h n) -> p s h n", s=2, h=8)
        cm = sbuf[:, 1700:1764].rearrange("p (h n) -> p h n", h=8)
        cm2 = sbuf[:, 1764:1828].rearrange("p (h n) -> p h n", h=8)
        phd = work[:, 1024:1024 + 2 * NP].rearrange("p (s n) -> p s n", s=2)
        g50 = work[:, 1200:1200 + T * NP]
        u50 = work[:, 1400:1400 + 2 * NP].rearrange("p (s n) -> p s n", s=2)

        names = ["pe_done", "vec_done", "act_done", "pool_done", "w_in", "x_in", "ctxA0", "ctxA1", "ctxB0", "ctxB1",
                 "ctxN0", "ctxN1", "ctxl_in", "gu0", "gu1", "dn0", "dn1", "out_done", "late_in"]
        sems = {n: sem(n) for n in names}
        pe_done, vec_done, act_done, pool_done = (sems[n] for n in names[:4])
        w_in, x_in, ctxl_in, out_done, late_in = (sems[n] for n in ("w_in", "x_in", "ctxl_in", "out_done", "late_in"))
        n_late = 16 * (len(load_layout()) - len(EARLY) + 2)
        ctxA_in, ctxB_in, ctxN_in, gu_in, dn_in = ([sems[n + "0"], sems[n + "1"]] for n in ("ctxA", "ctxB", "ctxN", "gu", "dn"))
        first, last = min(s.num for s in sems.values()), max(s.num for s in sems.values())
        assert last - first + 1 == len(names)

        PE, V, A, O = (Steps(marks.setdefault("0" + e, {})) for e in "pvao")
        with nc.Block() as block:
            @block.sync
            def _(sp):
                for n in EARLY:
                    sp.dma_start(w[n], dram[n]).then_inc(w_in, 16)
                for i in range(2):
                    sp.dma_start(cvec[:, i, :], dram["bo01"][:, i * D:(i + 1) * D]).then_inc(w_in, 16)

            n_in = 16 * (len(EARLY) + 2)

            @block.tensor
            def _(pe):
                pe.wait_ge(w_in, n_in)
                for i, (b, wo) in enumerate((("bv0", "wo0"), ("bv1", "wo1"))):
                    for k in range(KT):
                        pe.wait_ge(vec_done, V["bv", i, k])
                        ins = nc.tensor.matmul(ps[:, i, 0:D], obA[:, i, k * P:(k + 1) * P], kt(wo)[:, k, :],
                                               start=k == 0, stop=k == KT - 1)
                    ins.then_inc(pe_done, PE.step("cvec", i))

            @block.scalar
            def _(act):
                act.wait_ge(vec_done, V["lsum"])
                nc.scalar.activation(lsum, lsum, ACT.Exp).then_inc(act_done, A.step("lexp"))

            @block.vector
            def _(v):
                nc.vector.memset(mhalf, -0.5).then_inc(vec_done, V.step())
                nc.vector.memset(lg, PAD).then_inc(vec_done, V.step())
                nc.vector.memset(pbA[:, 0, 0:P], 1.0).then_inc(vec_done, V.step("ones"))
                v.wait_ge(w_in, n_in)
                v.wait_ge(vec_done, V.n)
                for i, b in enumerate(("bv0", "bv1")):
                    for k in range(KT):
                        nc.vector.tensor_scalar(obA[:, i, k * P:(k + 1) * P], pbA[:, 0, 0:P], w[b][:, k:k + 1], None,
                                                ALU.mult).then_inc(vec_done, V.step("bv", i, k))
                nc.vector.tensor_tensor(ltmp, w["lqk"][:, 0:16], w["lqk"][:, 16:32], ALU.mult).then_inc(vec_done, V.step())
                v.wait_ge(vec_done, V.n)
                nc.vector.tensor_reduce(lsum, ltmp.rearrange("p (a b) -> p a b", a=2), AX.X,
                                        ALU.add).then_inc(vec_done, V.step("lsum"))
                v.wait_ge(act_done, A["lexp"])
                nc.vector.scalar_tensor_tensor(neglam, lsum[:, 1:2], -LAMBDA_INIT, lsum[:, 0:1], ALU.add,
                                               ALU.subtract).then_inc(vec_done, V.step())
                for i in range(2):
                    v.wait_ge(pe_done, PE["cvec", i])
                    nc.vector.tensor_tensor(cvec[:, i, :], ps[:, i, 0:D], cvec[:, i, :], ALU.add).then_inc(vec_done, V.step())

        nc.gpsimd.sem_clear(range(first, last + 1))
        nc.all_engine_barrier()

        def qk_product(e, t, c):
            q = qkv[:, t % 2, c * 64:(c + 1) * 64].rearrange("p (a d) -> p a d", a=8)
            k = qkv[:, t % 2, D:2 * D].rearrange("p (a d) -> p a d", a=32)
            return e.tensor_tensor(prod[:, c % 2, :].rearrange("p (a b d) -> p a b d", a=8, b=32),
                                   q.unsqueeze(2).broadcast_to([P, 8, 32, 8]),
                                   k.unsqueeze(1).broadcast_to([P, 8, 32, 8]), ALU.mult)

        def pv_product(e, t, c):
            a = a2[:, t % 2, c * 128:(c + 1) * 128].rearrange("p (a h) -> p a h", a=8)
            vals = qkv[:, t % 2, 2 * D:3 * D].rearrange("p (d h) -> p d h", d=16)
            return e.tensor_tensor((prodV if c else prod[:, 0, :]).rearrange("p (a d h) -> p a d h", a=8, d=16),
                                   a.unsqueeze(2).broadcast_to([P, 8, 16, 16]),
                                   vals.unsqueeze(1).broadcast_to([P, 8, 16, 16]), ALU.mult)

        def b16(ap, n):
            return ap.unsqueeze(2).broadcast_to([P, ap.shape[1], n])

        HALF = T // 2

        def group(g, streams):
            PE, V, A, O = (Steps(marks.setdefault(streams + e, {})) for e in "pvao")

            def run(front, back):
                for s in order(streams):
                    next(front if s == "f" else back)

            def wait_scaled(e, tag, t):
                if t < HALF:
                    e.wait_ge(vec_done, V[tag, t])
                else:
                    e.wait_ge(act_done, A[tag, t])

            with nc.Block() as block:

                @block.sync
                def _(sp):
                    rows = bass.ds(g * P, P)

                    def front():
                        def late_weights():
                            for n, _c in load_layout():
                                if n not in EARLY:
                                    sp.dma_start(w[n], dram[n]).then_inc(late_in, 16)
                            sp.dma_start(wqp, dram["wqp"].rearrange("p (a d) -> p a d", a=NPH)).then_inc(late_in, 16)
                            sp.dma_start(keysp, dram["keysp"].rearrange("p (a k) -> p a k", a=NPH)).then_inc(late_in, 16)

                        sp.dma_start(xA, dram["x"][rows, :].rearrange("p (t d) -> p t d", t=T)).then_inc(x_in, 16)

                        def context(t):
                            src = dram["ctxT"][rows, t * NCT:(t + 1) * NCT].rearrange("p (a n) -> p a n", n=NK)[:, :, 0:256]
                            sp.dma_start(ctxA[t % 2].rearrange("p k b n -> p (k b) n"), src).then_inc(ctxA_in[t % 2], 16)

                        def gate_up(e):
                            sp.dma_start(stream[:, e % 2, 0:2048], dram["experts"][e * P:(e + 1) * P, 0:2048]).then_inc(gu_in[e % 2], 16)

                        def down(e):
                            sp.dma_start(stream[:, e % 2, 2048:EW], dram["experts"][e * P:(e + 1) * P, 2048:EW]).then_inc(dn_in[e % 2], 16)

                        context(0)
                        context(1)
                        if streams == "f":
                            late_weights()
                        down(0)
                        down(1)
                        for _ in range(4):
                            yield
                        for i in range(T + 2):
                            if 0 <= i < T - 2:
                                sp.wait_ge(pe_done, PE["v0", i])
                                context(i + 2)
                            if i == T:
                                sp.wait_ge(pe_done, PE["s0", T - 1])
                                gate_up(0)
                                gate_up(1)
                            yield
                        for _ in range(3 + T + 1 + T + 2 + 3 + 1):
                            yield
                        for e in range(NE + 2):
                            for f in range(4):
                                if f == 0 and 1 <= e and e + 1 <= NE:
                                    sp.wait_ge(pe_done, PE["gu", e * 4 - 1])
                                    gate_up(e + 1)
                                if f == 3 and 1 <= e and e + 1 <= NE:
                                    sp.wait_ge(pe_done, PE["down", e - 1])
                                    down(e + 1)
                                yield

                    def back():
                        grows = bass.ds((g - 1) * P, P)

                        def context(t):
                            sp.dma_start(ctxB[:, t % 2].rearrange("p k b n -> p (k b n)"),
                                         dram["ctxT"][grows, t * NCT:(t + 1) * NCT]).then_inc(ctxB_in[t % 2], 16)

                        def rows_of(t):
                            sp.dma_start(ctxN[:, t % 2].rearrange("p f b n -> p (f b n)"),
                                         dram["ctxN"][grows, t * 2048:(t + 1) * 2048]).then_inc(ctxN_in[t % 2], 16)

                        context(0)
                        context(1)
                        rows_of(0)
                        rows_of(1)
                        sp.dma_start(ctxL[0:BT], dram["ctxL"][bass.ds((g - 1) * BT, BT), :].rearrange(
                            "p (t d) -> p t d", t=T)).then_inc(ctxl_in, 16)
                        for _ in range(3 + T + 2 + 3):
                            yield
                        for i in range(T + 2):
                            if i < 2:
                                sp.wait_ge(pe_done, PE["xs", i])
                                context(i + 2)
                            if 2 <= i < 4:
                                sp.wait_ge(pe_done, PE["xpv", i - 2])
                                rows_of(i)
                            yield
                        for _ in range(3 + 8 + T + 1 + 8 + (T + 2) * 8 + 3 + 8 + T + 1 + 3):
                            yield
                        for i in range(T + 1):
                            for _ in range(4):
                                yield
                            if i >= 1:
                                sp.wait_ge(vec_done, V["x6", i - 1])
                                sp.dma_start(dram["out"][grows, (i - 1) * D:i * D], xnB[:, i - 1, :]).then_inc(out_done, 16)
                            for _ in range(3):
                                yield

                    run(front(), back())
                    if "b" in streams:
                        sp.wait_ge(out_done, 16 * T)

                @block.gpsimd
                def _(pool):
                    def add(tag, t, out, a, b):
                        nc.gpsimd.tensor_tensor(out, a, b, ALU.add).then_inc(pool_done, O.step(tag, t))

                    def norm(tag, ve, rstd, then=None):
                        pool.wait_ge(vec_done, V[tag, "var"])
                        nc.gpsimd.tensor_tensor(rstd, ve, mhalf[:, 0:T], ALU.pow).then_inc(pool_done, O.step(tag, "rstd"))
                        yield
                        if then:
                            then(0)
                        yield
                        if then:
                            then(1)
                        yield

                    def front():
                        def with_row(tag, i):
                            def then(slot):
                                if slot == 1:
                                    for t in range(T):
                                        wait_scaled(pool, tag, t)
                                        add("xb" + tag, t, xA[:, t], xA[:, t], cvec[:, i])
                            return then
                        yield from norm("n0", veA, rstdA, with_row("n0", 0))
                        for _ in range(1 + T + 2):
                            yield
                        yield from norm("n1", veA, rstdA, with_row("n1", 1))
                        for _ in range(T + 1 + T + 2):
                            yield
                        yield from norm("n2", veA, rstdA)
                        for _ in range(1 + (NE + 2) * 4):
                            yield

                    def back():
                        def with_bias(tag, be, dst):
                            def then(slot):
                                if slot == 1:
                                    for t in range(T):
                                        pool.wait_ge(vec_done, V[tag, "g", t])
                                        add(tag, t, dst[:, t], dst[:, t], w[be])
                            return then

                        def last_gain(slot):
                            if slot == 1:
                                for t in range(T):
                                    wait_scaled(pool, "y0", t)
                                    add("xbe3", t, xB[:, t], xB[:, t], w["be3"])
                        yield from norm("y0", veB, rstdB, last_gain)
                        for _ in range(T + 2):
                            yield
                        yield from norm("y1", veB, rstdB, with_bias("y1", "be1", xnB))
                        for _ in range(T + 2):
                            yield
                        yield from norm("y2", veB, rstdB, with_bias("y2", "be2", xnB))
                        for t in range(T):
                            pool.wait_ge(pool_done, O["y2", t])
                            add("y2b", t, xnB[:, t], xnB[:, t], w["b2x"])
                        for _ in range(8 + T + 1):
                            yield
                        yield from norm2("y3")
                        yield
                        yield from norm2("z")
                        yield from norm("h1", veB, rstdB)
                        for i in range(T + 2):
                            if i == 0:
                                for t in range(T):
                                    wait_scaled(pool, "h1", t)
                                    add("zb", t, xnB[:, t], xnB[:, t], w["bo2"])
                            if i < T:
                                pool.wait_ge(act_done, A["qkv", i])
                                if i >= 1:
                                    pool.wait_ge(vec_done, V["dred", i - 1, 3])
                                qk_product(nc.gpsimd, i, 1).then_inc(pool_done, O.step("dprod", i, 1))
                            yield
                            yield
                            if 1 <= i <= T:
                                pool.wait_ge(vec_done, V["datt", i - 1])
                                if i >= 2:
                                    pool.wait_ge(vec_done, V["pred", i - 2, 1])
                                pv_product(nc.gpsimd, i - 1, 1).then_inc(pool_done, O.step("pprod", i - 1))
                            yield
                            if i < T:
                                pool.wait_ge(vec_done, V["dred", i, 1])
                                qk_product(nc.gpsimd, i, 3).then_inc(pool_done, O.step("dprod", i, 3))
                            yield
                            yield
                            if 1 <= i <= T:
                                pool.wait_ge(vec_done, V["rms", i - 1])
                                nc.gpsimd.tensor_tensor(mx[:, (i - 1) % 2, 0:16], mx[:, (i - 1) % 2, 16:32], mhalf[:, 0:16],
                                                        ALU.pow).then_inc(pool_done, O.step("rms", i - 1))
                            for _ in range(3):
                                yield
                        yield from norm("h2", veB, rstdB)
                        for t in range(T):
                            wait_scaled(pool, "h2", t)
                            add("cb", t, xnB[:, t], xnB[:, t], w["b2a"])
                        for t in range(T):
                            pool.wait_ge(pool_done, O["cb", t])
                            add("xc", t, xB[:, t], xB[:, t], xnB[:, t])
                        for _ in range(8 + T + 1):
                            yield
                        yield from norm("n5", veB, rstdB)
                        for _ in range((T + 1) * 7):
                            yield

                    def norm2(tag):
                        pool.wait_ge(vec_done, V[tag, "var"])
                        nc.gpsimd.tensor_tensor(rstdB, veB, mhalf[:, 0:T], ALU.pow).then_inc(pool_done, O.step(tag, "rstd"))
                        yield
                        yield

                    run(front(), back())

                @block.tensor
                def _(pe):
                    mm, tr = nc.tensor.matmul, nc.tensor.transpose
                    ident = w["ident"]

                    def norm(tag, src, banks, first=None):
                        yield
                        yield
                        for t in range(T):
                            wait_scaled(pe, tag, t)
                            if t >= 2:
                                pe.wait_ge(act_done, A[tag, "T", t - 2])
                            for k in range(KT):
                                ins = tr(ps[:, banks[t % 2], k * P:(k + 1) * P], src[:, t, k * P:(k + 1) * P], ident)
                            ins.then_inc(pe_done, PE.step(tag, "T", t))
                        if first:
                            first()
                        yield

                    def project(out, aT, t, wt, cols):
                        for k in range(KT):
                            ins = mm(out, aT[:, k, t * P:(t + 1) * P], wt[:, k, cols], start=k == 0, stop=k == KT - 1)
                        return ins

                    def out_proj(tag, t, bank, o, oT, wo):
                        for k in range(KT):
                            ins = tr(ps[:, bank, 256 + k * P:256 + (k + 1) * P], o[:, t % 2, k * P:(k + 1) * P], ident)
                        ins.then_inc(pe_done, PE.step(tag, "oT", t))
                        pe.wait_ge(act_done, A[tag, "oT", t])
                        for k in range(KT):
                            ins = mm(ps[:, bank, 0:D], oT[:, t % 2, k, :], kt(wo)[:, k, :], start=k == 0, stop=k == KT - 1)
                        ins.then_inc(pe_done, PE.step(tag, "wo", t))

                    def front():
                        yield from norm("n0", xnA, (0, 1))
                        pe.wait_ge(act_done, A["n0", "T", T - 1])
                        for f in range(2):
                            for k in range(KT):
                                ins = mm(ps[:, 2 + f, :], kt("wq0")[:, k, f * P:(f + 1) * P], aTA[:, k, :], start=k == 0, stop=k == KT - 1)
                            ins.then_inc(pe_done, PE.step("q0", f))
                        yield
                        for i in range(T + 2):
                            if i < T:
                                t = i
                                pe.wait_ge(ctxA_in[t % 2], 16 * (t // 2 + 1))
                                if t == 0:
                                    pe.wait_ge(act_done, A["n0", "T", T - 1])
                                else:
                                    pe.wait_ge(vec_done, V["valM", t - 1])
                                for f in range(2):
                                    for k in range(KT):
                                        ins = mm(ps[:, f, :], kt("wk0")[:, k, f * P:(f + 1) * P],
                                                 ctxA[t % 2][:, k, :, f * P:(f + 1) * P], start=k == 0, stop=k == KT - 1)
                                    ins.then_inc(pe_done, PE.step("k0", t, f))
                            if 1 <= i <= T:
                                t = i - 1
                                pe.wait_ge(act_done, A["exp0", t])
                                if t >= 2:
                                    pe.wait_ge(vec_done, V["x1", t - 2])
                                if t == 0:
                                    pe.wait_ge(act_done, A["qT", 1])
                                for f in range(2):
                                    ins = tr(ps[:, 3, f * P:(f + 1) * P], pbA[:, t % 2, f * P:(f + 1) * P], ident)
                                ins.then_inc(pe_done, PE.step("pT0", t))
                                pe.wait_ge(act_done, A["pT0", t])
                                pe.wait_ge(vec_done, V["valM", t])
                                if t >= 1:
                                    pe.wait_ge(vec_done, V["l0", "o", t - 1])
                                for b in range(BT):
                                    for f in range(2):
                                        ins = mm(ps[S * b:S * (b + 1), 4, f * P:(f + 1) * P],
                                                 pTA[:, t % 2, f * P + S * b:f * P + S * (b + 1)],
                                                 valM[:, t % 2, f, b, :], start=True, stop=True)
                                ins.then_inc(pe_done, PE.step("pv0", t))
                            if i < T:
                                t = i
                                for f in range(2):
                                    pe.wait_ge(vec_done, V["keyT", t, f])
                                    for b in range(BT):
                                        for k in range(KT):
                                            ins = mm(ps[:, f, b * P:(b + 1) * P], ctxA[t % 2][:, k, b, f * P:(f + 1) * P],
                                                     kt("wv0")[:, k, f * P:(f + 1) * P], start=k == 0, stop=k == KT - 1)
                                ins.then_inc(pe_done, PE.step("v0", t))
                                pe.wait_ge(act_done, A["qT", 1])
                                if t >= 1:
                                    pe.wait_ge(vec_done, V["sub0", t - 1])
                                for b in range(BT):
                                    for f in range(2):
                                        ins = mm(ps[S * b:S * (b + 1), 2, f * P:(f + 1) * P],
                                                 qT[:, f, t * P + S * b:t * P + S * (b + 1)],
                                                 keyT[:, t % 2, f, b * P:(b + 1) * P], start=True, stop=True)
                                ins.then_inc(pe_done, PE.step("s0", t))
                            if i >= 2:
                                t = i - 2
                                pe.wait_ge(vec_done, V["l0", "o", t])
                                if t + 1 < T:
                                    pe.wait_ge(act_done, A["pT0", t + 1])
                                if t >= 1:
                                    pe.wait_ge(vec_done, V["x1", t - 1])
                                out_proj("l0", t, 3, obA, oTA, "wo0")
                            yield

                        if streams == "f":
                            pe.wait_ge(late_in, n_late)
                            for k in range(KT):
                                if k:
                                    pe.wait_ge(act_done, A["cmat", k - 1])
                                for a in range(NPH):
                                    ins = mm(ps[:, 5 + a // 8, (a % 8) * NKEY:(a % 8 + 1) * NKEY],
                                             wqp[:, a, k * P:(k + 1) * P], keysp[:, a, :], start=True, stop=True)
                                ins.then_inc(pe_done, PE.step("cmat", k))

                        yield from norm("n1", xnA, (0, 1))
                        for i in range(T + 1):
                            if i < T:
                                t = i
                                pe.wait_ge(act_done, A["n1", "T", t])
                                pe.wait_ge(vec_done, V["x1", T - 1])
                                if t >= 2:
                                    pe.wait_ge(vec_done, V["dg", t - 2])
                                project(ps[:, 2 + t % 2, 0:D + 3], aTA, t, kt("wv1"), slice(0, D + 3)).then_inc(pe_done, PE.step("v1", t))
                            if i >= 1:
                                t = i - 1
                                pe.wait_ge(vec_done, V["dg", t])
                                if t >= 1:
                                    pe.wait_ge(vec_done, V["sq", t - 1])
                                mm(ps[:, 4, 0:96], w["blockones"], dg[:, t % 2, :], start=True,
                                   stop=True).then_inc(pe_done, PE.step("pos", t))
                            yield
                        for i in range(T + 2):
                            if i < T:
                                t = i
                                pe.wait_ge(vec_done, V["attT", t])
                                pe.wait_ge(act_done, A["valA", t])
                                if t >= 2:
                                    pe.wait_ge(vec_done, V["l1", "o", t - 2])
                                mm(ps[:, t % 2, 0:D + 1], attT[:, t % 2, :], valA[:, t, :], start=True,
                                   stop=True).then_inc(pe_done, PE.step("av1", t))
                            if i >= 2:
                                t = i - 2
                                pe.wait_ge(vec_done, V["l1", "o", t])
                                if t >= 2:
                                    pe.wait_ge(vec_done, V["x2", t - 2])
                                out_proj("l1", t, 2 + t % 2, obA, oTA, "wo1")
                            yield

                        yield from norm("n2", xnA, (0, 1))
                        for t in range(T):
                            pe.wait_ge(act_done, A["n2", "T", t])
                            ins = project(ps[:, 4, t * NE:(t + 1) * NE], aTA, t, kt("router"), slice(0, NE))
                        ins.then_inc(pe_done, PE.step("router"))
                        yield
                        for e in range(NE + 2):
                            for f in range(4):
                                n = e * 4 + f
                                if e <= NE:
                                    we = stream[:, e % 2, :]
                                    if f == 0:
                                        pe.wait_ge(gu_in[e % 2], 16 * (e // 2 + 1))
                                    if n >= 2:
                                        pe.wait_ge(vec_done, V["hid", n - 2])
                                    for u in range(2):
                                        for k in range(KT):
                                            c = (u * KT + k) * HID + f * P
                                            ins = mm(ps[:, 2 * (f % 2) + u, :], we[:, c:c + P], aTA[:, k, :], start=k == 0, stop=k == KT - 1)
                                    ins.then_inc(pe_done, PE.step("gu", n))
                                if e >= 1 and f % 2 == 1:
                                    we = stream[:, (e - 1) % 2, 2048:EW].rearrange("p (f d) -> p f d", f=HID // P)
                                    if f == 1:
                                        pe.wait_ge(dn_in[(e - 1) % 2], 16 * ((e - 1) // 2 + 1))
                                        pe.wait_ge(vec_done, V["hid", e * 4 - 1])
                                    if e == 1 and f == 1:
                                        pe.wait_ge(vec_done, V["logits"])
                                    elif f == 1:
                                        pe.wait_ge(vec_done, V["acc", e - 2, 3])
                                    else:
                                        pe.wait_ge(vec_done, V["acc", e - 1, 1])
                                    for t in (f - 1, f):
                                        for j in range(HID // P):
                                            ins = mm(ps[:, 4, (t % 2) * D:(t % 2 + 1) * D], hE[:, (e - 1) % 2, j, t * P:(t + 1) * P],
                                                     we[:, j, :], start=j == 0, stop=j == HID // P - 1)
                                    ins.then_inc(pe_done, PE.step(*(("down", e - 1) if f == 3 else ("down", e - 1, 1))))
                                yield

                    def back():
                        yield from norm("y0", xnB, (5, 6))
                        for i in range(T + 2):
                            if i < T:
                                t = i
                                pe.wait_ge(act_done, A["y0", "T", t if t else 2])
                                if t >= 1:
                                    pe.wait_ge(vec_done, V["cs", t - 1])
                                for k in range(KT):
                                    ins = mm(ps[:, 5, 0:P], aTB[:, k, t * P:(t + 1) * P], aTB[:, k, t * P:(t + 1) * P],
                                             start=k == 0, stop=k == KT - 1)
                                ins.then_inc(pe_done, PE.step("cs", t))
                            if 1 <= i <= T:
                                t = i - 1
                                pe.wait_ge(act_done, A["cexp", t])
                                pe.wait_ge(act_done, A["cpT", t - 1] if t else A["y0", "T", 3])
                                tr(ps[:, 6, 0:P], pb[:, t % 2, 0:P], ident).then_inc(pe_done, PE.step("cpT", t))
                            if i >= 2:
                                t = i - 2
                                pe.wait_ge(act_done, A["cpT", t])
                                if t >= 1:
                                    pe.wait_ge(vec_done, V["y1p", t - 1])
                                mm(ps[:, 7, 0:D], pT[:, t % 2, 0:P], xnB[:, t, :], start=True,
                                   stop=True).then_inc(pe_done, PE.step("cpv", t))
                            yield

                        yield from norm("y1", xnB, (5, 6))
                        for i in range(T + 2):
                            if i < T:
                                t = i
                                pe.wait_ge(act_done, A["y1", "T", t if t else 2])
                                pe.wait_ge(ctxB_in[t % 2], 16 * (t // 2 + 1))
                                if t >= 1:
                                    pe.wait_ge(act_done, A["xexp", t - 1])
                                for b in range(BT):
                                    for k in range(KT):
                                        ins = mm(ps[S * b:S * (b + 1), 5, 0:NK], aTB[:, k, t * P + S * b:t * P + S * (b + 1)],
                                                 ctxB[:, t % 2, k, b, :], start=k == 0, stop=k == KT - 1)
                                ins.then_inc(pe_done, PE.step("xs", t))
                            if 1 <= i <= T:
                                t = i - 1
                                pe.wait_ge(vec_done, V["w4", t])
                                pe.wait_ge(act_done, A["xpT", t - 1] if t else A["y1", "T", 3])
                                for f in range(2):
                                    tr(ps[:, 6, f * P:(f + 1) * P], pb[:, t % 2, f * P:(f + 1) * P], ident)
                                tr(ps[0:BT, 6, 256:384], w4[:, t % 2, :], ident).then_inc(pe_done, PE.step("xpT", t))
                            if i >= 2:
                                t = i - 2
                                pe.wait_ge(act_done, A["xpT", t])
                                pe.wait_ge(ctxN_in[t % 2], 16 * (t // 2 + 1))
                                if t == 0:
                                    pe.wait_ge(ctxl_in, 16)
                                if t >= 1:
                                    pe.wait_ge(vec_done, V["y2p", t - 1])
                                mm(ps[:, 7, 0:D], pT[0:BT, t % 2, 256:384], ctxL[0:BT, t, :], start=True, stop=False,
                                   skip_group_check=True)
                                for b in range(BT):
                                    for f in range(2):
                                        ins = mm(ps[S * b:S * (b + 1), 7, 0:D], pT[:, t % 2, f * P + S * b:f * P + S * (b + 1)],
                                                 ctxN[:, t % 2, f, b, :], start=False, stop=f == 1, skip_group_check=True)
                                ins.then_inc(pe_done, PE.step("xpv", t))
                            yield

                        def ffn(tag, w1, w2):
                            for f in range(FF // P):
                                if f == 0:
                                    pe.wait_ge(act_done, A[tag, "T", T - 1])
                                if f >= 2:
                                    pe.wait_ge(act_done, A[tag, "relu", f - 2])
                                for k in range(KT):
                                    ins = mm(ps[:, 5 + f % 2, :], kt(w1)[:, k, f * P:(f + 1) * P], aTB[:, k, :], start=k == 0, stop=k == KT - 1)
                                ins.then_inc(pe_done, PE.step(tag, "f1", f))
                                yield
                            w2v = w[w2].rearrange("p (f d) -> p f d", f=FF // P)
                            pe.wait_ge(act_done, A[tag, "relu", FF // P - 1])
                            for t in range(T + 1):
                                if t < T:
                                    if t >= 2:
                                        pe.wait_ge(vec_done, V[tag, "f2", t - 2])
                                    for f in range(FF // P):
                                        ins = mm(ps[:, (7, 5)[t % 2], 0:D], hF[:, f, t * P:(t + 1) * P], w2v[:, f, :],
                                                 start=f == 0, stop=f == FF // P - 1)
                                    ins.then_inc(pe_done, PE.step(tag, "f2", t))
                                yield

                        yield from norm("y2", xnB, (5, 6))
                        yield from ffn("y2", "w1x", "w2x")
                        for _ in range(5):
                            yield

                        def qkv_proj(t):
                            pe.wait_ge(act_done, A["h1", "T", T - 1])
                            if t >= 1:
                                pe.wait_ge(act_done, A["qkv", t - 1])
                            project(ps[:, 5, :], aTB, t, kt("wqkv"), slice(0, 512))
                            project(ps[:, 6, 0:D], aTB, t, kt("wqkv"), slice(512, 768)).then_inc(pe_done, PE.step("qkv", t))
                        yield from norm("h1", hh, (5, 6), lambda: qkv_proj(0))
                        for i in range(T + 2):
                            for _ in range(4):
                                yield
                            if i + 1 < T:
                                qkv_proj(i + 1)
                            if i >= 2:
                                t = i - 2
                                pe.wait_ge(vec_done, V["l4", "o", t])
                                if t >= 1:
                                    pe.wait_ge(vec_done, V["conn", t - 1])
                                out_proj("l4", t, 7, ob, oTB, "wo2")
                            for _ in range(4):
                                yield

                        yield from norm("h2", hh, (5, 6))
                        yield from ffn("h2", "w1a", "w2a")

                        def sim(t):
                            pe.wait_ge(act_done, A["n5", "T", T - 1])
                            if t >= 1:
                                pe.wait_ge(vec_done, V["rep64", t - 1])
                            project(ps[:, 5, :], aTB, t, cmat, slice(0, 512))
                            project(ps[:, 6, :], aTB, t, cmat, slice(512, 1024)).then_inc(pe_done, PE.step("sim", t))
                        yield from norm("n5", xnB, (5, 6), lambda: sim(0))
                        for i in range(T + 1):
                            if i == 0:
                                pe.wait_ge(vec_done, V["h2", "f2", T - 2])
                                for t in range(T):
                                    ins = project(ps[:, 7, t * NP:(t + 1) * NP], aTB, t, kt("wd50"), slice(0, NP))
                                ins.then_inc(pe_done, PE.step("h50"))
                            if i >= 1:
                                t = i - 1
                                pe.wait_ge(vec_done, V["u50", t])
                                if t >= 1:
                                    pe.wait_ge(vec_done, V["x6", t - 1])
                                tr(ps[0:NP, 7, 256:384], u50[:, t % 2, :], ident).then_inc(pe_done, PE.step("uT", t))
                            for _ in range(3):
                                yield
                            if i >= 1:
                                t = i - 1
                                pe.wait_ge(act_done, A["uT", t])
                                mm(ps[:, 7, 0:D], pT[0:NP, t % 2, 0:P], w["wu50"][0:NP, :], start=True,
                                   stop=True).then_inc(pe_done, PE.step("up", t))
                            if i + 1 < T:
                                sim(i + 1)
                            for _ in range(4):
                                yield

                    run(front(), back())

                @block.scalar
                def _(act):
                    sa = nc.scalar.activation

                    def scale(tag, src, dst, small, turned=None):
                        mv, rstd, mr = small
                        act.wait_ge(vec_done, V[tag, "mr"])
                        for t in range(HALF, T):
                            if turned:
                                act.wait_ge(pe_done, PE[turned, "T", t])
                            sa(dst[:, t, :], src[:, t, :], ACT.Identity, bias=mr[:, t:t + 1],
                               scale=rstd[:, t:t + 1]).then_inc(act_done, A.step(tag, t))

                    smallA, smallB = (mvA, rstdA, mrA), (mvB, rstdB, mrB)

                    def norm(tag, aT, banks, reader, src, dst, small, turned=None, then=None, gain=None):
                        yield
                        scale(tag, src, dst, small, turned)
                        yield
                        if reader:
                            act.wait_ge(pe_done, PE[reader])
                        for t in range(T):
                            act.wait_ge(pe_done, PE[tag, "T", t])
                            if gain:
                                for k in range(KT):
                                    sa(aT[:, k, t * P:(t + 1) * P], ps[:, banks[t % 2], k * P:(k + 1) * P], ACT.Identity,
                                       scale=w[gain[0]][:, k:k + 1], bias=w[gain[1]][:, k:k + 1]).then_inc(
                                           act_done, A.step(*((tag, "T", t) if k == KT - 1 else ())))
                                continue
                            nc.scalar.copy(aT[:, :, t * P:(t + 1) * P], ps[:, banks[t % 2], 0:KT * P].rearrange(
                                "p (k n) -> p k n", k=KT)).then_inc(act_done, A.step(tag, "T", t))
                        if then:
                            then()
                        yield

                    def o_turn(tag, t, oT, bank):
                        act.wait_ge(pe_done, PE[tag, "oT", t])
                        if t >= 2:
                            act.wait_ge(pe_done, PE[tag, "wo", t - 2])
                        nc.scalar.copy(oT[:, t % 2].rearrange("p k n -> p (k n)"), ps[:, bank, 256:512]).then_inc(
                            act_done, A.step(tag, "oT", t))

                    def front():
                        yield from norm("n0", aTA, (0, 1), None, xA, xnA, smallA)
                        for f in range(2):
                            act.wait_ge(pe_done, PE["q0", f])
                            sa(qT[:, f, :], ps[:, 2 + f, :], ACT.Identity, bias=w["bq0"][:, f:f + 1]).then_inc(act_done, A.step("qT", f))
                        yield
                        for i in range(T + 2):
                            if 1 <= i <= T:
                                t = i - 1
                                act.wait_ge(pe_done, PE["pT0", t])
                                if t >= 2:
                                    act.wait_ge(pe_done, PE["pv0", t - 2])
                                nc.scalar.copy(pTA[:, t % 2, :], ps[:, 3, 0:256]).then_inc(act_done, A.step("pT0", t))
                            if i < T:
                                act.wait_ge(vec_done, V["sub0", i])
                                sa(pbA[:, i % 2, :], pbA[:, i % 2, :], ACT.Exp, scale=0.25).then_inc(act_done, A.step("exp0", i))
                            if i >= 2:
                                o_turn("l0", i - 2, oTA, 3)
                            yield
                        if streams == "f":
                            for k in range(KT):
                                act.wait_ge(pe_done, PE["cmat", k])
                                nc.scalar.copy(cmat[:, k, :], ps[:, 5:7, :]).then_inc(act_done, A.step("cmat", k))
                        yield from norm("n1", aTA, (0, 1), ("q0", 1), xA, xnA, smallA, "n0")
                        for i in range(T + 1):
                            if i < T:
                                act.wait_ge(pe_done, PE["v1", i])
                                nc.scalar.copy(valA[:, i, 0:D], ps[:, 2 + i % 2, 0:D]).then_inc(act_done, A.step("valA", i))
                            else:
                                act.wait_ge(vec_done, V["sq", T - 1])
                                sa(dist, dist, ACT.Sqrt).then_inc(act_done, A.step())
                                act.wait_ge(act_done, A.n)
                                sa(dist, dist, ACT.Exp, scale=-0.25).then_inc(act_done, A.step("dexp"))
                            yield
                        for i in range(T + 2):
                            if i >= 2:
                                o_turn("l1", i - 2, oTA, 2 + i % 2)
                            yield
                        yield from norm("n2", aTA, (0, 1), ("v1", T - 1), xA, xnA, smallA, "n1")
                        act.wait_ge(vec_done, V["lsub"])
                        sa(ex, ex, ACT.Exp).then_inc(act_done, A.step("lexp"))
                        yield
                        for e in range(NE + 2):
                            for f in range(4):
                                if e <= NE:
                                    n = e * 4 + f
                                    act.wait_ge(pe_done, PE["gu", n])
                                    if f == 0 and e >= 2:
                                        act.wait_ge(pe_done, PE["down", e - 2])
                                    sa(hE[:, e % 2, f, :], ps[:, 2 * (f % 2), :], ACT.Silu).then_inc(act_done, A.step("silu", n))
                                yield

                    def back():
                        yield from norm("y0", aTB, (5, 6), None, xB, xnB, smallB)
                        for i in range(T + 2):
                            if i < T:
                                t = i
                                act.wait_ge(vec_done, V["cmax", t])
                                sa(pb[:, t % 2, 0:P], pb[:, t % 2, 0:P], ACT.Exp, bias=nm[:, t:t + 1],
                                   accum_out=rs[:, t:t + 1]).then_inc(act_done, A.step("cexp", t))
                            if 1 <= i <= T:
                                t = i - 1
                                act.wait_ge(pe_done, PE["cpT", t])
                                if t >= 2:
                                    act.wait_ge(pe_done, PE["cpv", t - 2])
                                nc.scalar.copy(pT[:, t % 2, 0:P], ps[:, 6, 0:P]).then_inc(act_done, A.step("cpT", t))
                            yield
                        yield from norm("y1", aTB, (5, 6), ("cs", T - 1), xnB, xnB, smallB, gain=("g1c", "be1c"))
                        for i in range(T + 2):
                            if i < T:
                                t = i
                                act.wait_ge(vec_done, V["xmax", t])
                                if t >= 2:
                                    act.wait_ge(pe_done, PE["xpT", t - 2])
                                    act.wait_ge(vec_done, V["w4", t - 2])
                                sa(pb[:, t % 2, 0:NK], ps[:, 5, 0:NK], ACT.Exp, bias=nm[:, t:t + 1], scale=1.0 / 16,
                                   accum_out=rs[:, t:t + 1]).then_inc(act_done, A.step("xexp", t))
                            if 1 <= i <= T:
                                t = i - 1
                                act.wait_ge(pe_done, PE["xpT", t])
                                if t >= 2:
                                    act.wait_ge(pe_done, PE["xpv", t - 2])
                                nc.scalar.copy(pT[:, t % 2, 0:256], ps[:, 6, 0:256]).then_inc(act_done, A.step())
                                nc.scalar.copy(pT[0:BT, t % 2, 256:384], ps[0:BT, 6, 256:384]).then_inc(act_done, A.step("xpT", t))
                            yield

                        def ffn(tag, b1):
                            for f in range(FF // P):
                                act.wait_ge(pe_done, PE[tag, "f1", f])
                                sa(hF[:, f, :], ps[:, 5 + f % 2, :], ACT.Relu, bias=w[b1][:, f:f + 1]).then_inc(act_done, A.step(tag, "relu", f))
                                yield
                            for _ in range(T + 1):
                                yield

                        yield from norm("y2", aTB, (5, 6), ("xs", T - 1), xnB, xnB, smallB, gain=("g2c", "be2c"))
                        yield from ffn("y2", "b1x")
                        yield
                        scale("y3", xnB, xnB, smallB)
                        yield
                        yield
                        yield
                        scale("z", xB, xnB, smallB)
                        yield

                        def qkv_copy(t):
                            act.wait_ge(pe_done, PE["qkv", t])
                            if t >= 2:
                                act.wait_ge(vec_done, V["pprod", t - 2])
                                act.wait_ge(pool_done, O["pprod", t - 2])
                            nc.scalar.copy(qkv[:, t % 2, 0:512], ps[:, 5, :]).then_inc(act_done, A.step())
                            nc.scalar.copy(qkv[:, t % 2, 512:768], ps[:, 6, 0:256]).then_inc(act_done, A.step("qkv", t))
                        yield from norm("h1", aTB, (5, 6), ("y2", "f1", FF // P - 1), xnB, hh, smallB, None, lambda: qkv_copy(0), ("lg1", "lb1"))
                        for i in range(T + 2):
                            for _ in range(4):
                                yield
                            if i + 1 < T:
                                qkv_copy(i + 1)
                            if i >= 2:
                                o_turn("l4", i - 2, oTB, 7)
                            for _ in range(3):
                                yield
                            if i < T:
                                act.wait_ge(vec_done, V["dsub", i])
                                sa(sc[:, i % 2, :], sc[:, i % 2, :], ACT.Exp, scale=8.0 ** -0.5).then_inc(act_done, A.step("dexp2", i))
                            yield
                        yield from norm("h2", aTB, (5, 6), ("qkv", T - 1), xnB, hh, smallB, gain=("lg2", "lb2"))
                        yield from ffn("h2", "b1a")
                        yield from norm("n5", aTB, (5, 6), ("h2", "f1", FF // P - 1), xB, xnB, smallB)
                        for i in range(T + 1):
                            if i == 0:
                                act.wait_ge(pe_done, PE["h50"])
                                sa(g50, ps[:, 7, 0:T * NP], ACT.Gelu).then_inc(act_done, A.step("g50"))
                            if i >= 1:
                                t = i - 1
                                act.wait_ge(pe_done, PE["uT", t])
                                if t >= 2:
                                    act.wait_ge(pe_done, PE["up", t - 2])
                                nc.scalar.copy(pT[0:NP, t % 2, 0:P], ps[0:NP, 7, 256:384]).then_inc(act_done, A.step("uT", t))
                            for _ in range(4):
                                yield
                            if i < T:
                                act.wait_ge(vec_done, V["csub", i])
                                sa(cexp[:, i % 2], cexp[:, i % 2], ACT.Exp).then_inc(act_done, A.step("cexp2", i))
                            for _ in range(3):
                                yield

                    run(front(), back())

                @block.vector
                def _(v):
                    vv = nc.vector

                    def own_steps():
                        v.wait_ge(vec_done, V.n)

                    def norm(tag, src, dst, small, gain=None, before=None, turned=None, slots=3, after=None, early=False):
                        st, mv, ve, rstd, mr = small
                        if before:
                            before()
                        for t in range(0 if early else T):
                            if t == 0 and V.n:
                                own_steps()
                            vv.bn_stats(st[:, t, :], src[:, t, :]).then_inc(vec_done, V.step(tag, "st", t))
                        for t in range(T):
                            v.wait_ge(vec_done, V[tag, "st", t])
                            vv.bn_aggr(mv[:, t, :], st[:, t, :]).then_inc(vec_done, V.step())
                        own_steps()
                        vv.tensor_scalar(ve, mv[:, :, 1], EPS, None, ALU.add).then_inc(vec_done, V.step(tag, "var"))
                        yield
                        v.wait_ge(pool_done, O[tag, "rstd"])
                        vv.scalar_tensor_tensor(mr, mv[:, :, 0], -1.0, rstd, ALU.mult, ALU.mult).then_inc(vec_done, V.step(tag, "mr"))
                        for t in range(HALF):
                            if turned:
                                v.wait_ge(pe_done, PE[turned, "T", t])
                            vv.tensor_scalar(dst[:, t, :], src[:, t, :], mv[:, t, 0:1], rstd[:, t:t + 1], ALU.subtract,
                                             ALU.mult).then_inc(vec_done, V.step(tag, t))
                        if gain:
                            for t in range(T):
                                wait_scaled(v, tag, t)
                                vv.tensor_tensor(dst[:, t, :], dst[:, t, :], w[gain], ALU.mult).then_inc(vec_done, V.step(tag, "g", t))
                        yield
                        if after:
                            after()
                        if slots == 3:
                            yield

                    def stats(tag, src, small, t):
                        own_steps()
                        vv.bn_stats(small[0][:, t, :], src[:, t, :]).then_inc(vec_done, V.step(tag, "st", t))

                    def late_gain(tag, name):
                        def after():
                            for t in range(T):
                                v.wait_ge(pe_done, PE[tag, "T", t])
                                vv.tensor_tensor(xnB[:, t, :], xnB[:, t, :], w[name], ALU.mult).then_inc(vec_done, V.step(tag, "g", t))
                        return after

                    smallA, smallB = (stA, mvA, veA, rstdA, mrA), (stB, mvB, veB, rstdB, mrB)

                    def front():
                        yield from norm("n0", xA, xnA, smallA, before=lambda: v.wait_ge(x_in, 16))
                        yield
                        hm = w["headmask"].unsqueeze(1)
                        for i in range(T + 2):
                            if i < T:
                                t = i
                                if t >= 2:
                                    v.wait_ge(pe_done, PE["s0", t - 2])
                                for f in range(2):
                                    v.wait_ge(pe_done, PE["k0", t, f])
                                    vv.scalar_tensor_tensor(keyT[:, t % 2, f, :].rearrange("p (b n) -> p b n", b=BT),
                                                            ps[:, f, :].rearrange("p (b n) -> p b n", b=BT), w["bk0"][:, f:f + 1],
                                                            hm.broadcast_to([P, BT, P]), ALU.add,
                                                            ALU.mult).then_inc(vec_done, V.step("keyT", t, f))
                            if 1 <= i <= T:
                                t = i - 1
                                v.wait_ge(act_done, A["exp0", t])
                                own_steps()
                                vv.tensor_reduce(smA, pbA[:, t % 2, :].rearrange("p (h l) -> p h l", h=H), AX.X,
                                                 ALU.add).then_inc(vec_done, V.step())
                                own_steps()
                                vv.reciprocal(riA, smA).then_inc(vec_done, V.step())
                                own_steps()
                                v.wait_ge(pe_done, PE["pv0", t])
                                if t >= 2:
                                    v.wait_ge(pe_done, PE["l0", "oT", t - 2])
                                vv.tensor_tensor(obA[:, t % 2, :].rearrange("p (h l) -> p h l", h=H),
                                                 ps[:, 4, 0:256].rearrange("p (h l) -> p h l", h=H), b16(riA, 16),
                                                 ALU.mult).then_inc(vec_done, V.step("l0", "o", t))
                            if i < T:
                                t = i
                                v.wait_ge(pe_done, PE["v0", t])
                                if t >= 2:
                                    v.wait_ge(pe_done, PE["pv0", t - 2])
                                vv.tensor_tensor(valM[:, t % 2].rearrange("p f b n -> p (f b) n"),
                                                 ps[:, 0:2, :].rearrange("p f (b n) -> p (f b) n", b=BT),
                                                 hm.broadcast_to([P, 2 * BT, P]), ALU.mult).then_inc(vec_done, V.step("valM", t))
                                v.wait_ge(pe_done, PE["s0", t])
                                if t >= 2:
                                    v.wait_ge(pe_done, PE["pT0", t - 2])
                                sv = ps[:, 2, 0:256].rearrange("p (h l) -> p h l", h=H)
                                own_steps()
                                vv.tensor_reduce(mxA, sv, AX.X, ALU.max).then_inc(vec_done, V.step())
                                own_steps()
                                vv.tensor_tensor(pbA[:, t % 2, :].rearrange("p (h l) -> p h l", h=H), sv, b16(mxA, 16),
                                                 ALU.subtract).then_inc(vec_done, V.step("sub0", t))
                            if i >= 2:
                                t = i - 2
                                v.wait_ge(pe_done, PE["l0", "wo", t])
                                v.wait_ge(pool_done, O["xbn0", t])
                                vv.tensor_tensor(xA[:, t, :], ps[:, 3, 0:D], xA[:, t, :], ALU.add).then_inc(vec_done, V.step("x1", t))
                                stats("n1", xA, smallA, t)
                            yield

                        yield from norm("n1", xA, xnA, smallA, turned="n0", early=True)
                        if streams == "f":
                            v.wait_ge(late_in, n_late)
                        e3 = w["eye32"].unsqueeze(1).broadcast_to([P, 3, S])
                        for i in range(T + 1):
                            if i == 0:
                                own_steps()
                                v.wait_ge(pe_done, PE["pv0", T - 1])
                                vv.memset(valA[:, :, D:D + 1], 1.0).then_inc(vec_done, V.step())
                            if i < T:
                                t = i
                                v.wait_ge(act_done, A["valA", t])
                                vv.tensor_tensor(pos[:, t, :], ps[:, 2 + t % 2, D:D + 3], w["b3d"], ALU.add).then_inc(vec_done, V.step())
                                own_steps()
                                if t >= 2:
                                    v.wait_ge(pe_done, PE["pos", t - 2])
                                vv.tensor_tensor(dg[:, t % 2, :].rearrange("p (c j) -> p c j", c=3), b16(pos[:, t, :], S), e3,
                                                 ALU.mult).then_inc(vec_done, V.step("dg", t))
                            if i >= 1:
                                t = i - 1
                                v.wait_ge(pe_done, PE["pos", t])
                                pv = ps[:, 4, 0:96].rearrange("p (c j) -> p c j", c=3)
                                d3 = df.rearrange("p (c j) -> p c j", c=3)
                                own_steps()
                                vv.tensor_tensor(d3, pv, e3, ALU.mult).then_inc(vec_done, V.step())
                                own_steps()
                                vv.tensor_reduce(own, d3, AX.X, ALU.add).then_inc(vec_done, V.step())
                                own_steps()
                                vv.tensor_tensor(d3, pv, b16(own, S), ALU.subtract).then_inc(vec_done, V.step())
                                own_steps()
                                vv.tensor_tensor(df, df, df, ALU.mult).then_inc(vec_done, V.step())
                                own_steps()
                                vv.tensor_reduce(dist[:, t, :], df.rearrange("p (c j) -> p j c", c=3), AX.X, ALU.add).then_inc(vec_done, V.step("sq", t))
                            yield
                        for i in range(T + 2):
                            if i == 0:
                                v.wait_ge(act_done, A["dexp"])
                                own_steps()
                            if i < T:
                                t = i
                                if t >= 2:
                                    v.wait_ge(pe_done, PE["av1", t - 2])
                                vv.tensor_tensor(attT[:, t % 2, :].rearrange("p (b j) -> p b j", b=BT),
                                                 dist[:, t, :].unsqueeze(1).broadcast_to([P, BT, S]),
                                                 w["causalT"].rearrange("p (b j) -> p b j", b=BT), ALU.mult).then_inc(vec_done, V.step("attT", t))
                            if 1 <= i <= T:
                                t = i - 1
                                v.wait_ge(pe_done, PE["av1", t])
                                own_steps()
                                vv.reciprocal(riA[:, 0:1], ps[:, t % 2, D:D + 1]).then_inc(vec_done, V.step())
                                own_steps()
                                if t >= 2:
                                    v.wait_ge(pe_done, PE["l1", "oT", t - 2])
                                vv.tensor_scalar(obA[:, t % 2, :], ps[:, t % 2, 0:D], riA[:, 0:1], None,
                                                 ALU.mult).then_inc(vec_done, V.step("l1", "o", t))
                            if i >= 2:
                                t = i - 2
                                v.wait_ge(pe_done, PE["l1", "wo", t])
                                v.wait_ge(pool_done, O["xbn1", t])
                                vv.tensor_tensor(xA[:, t, :], ps[:, 2 + t % 2, 0:D], xA[:, t, :], ALU.add).then_inc(vec_done, V.step("x2", t))
                                stats("n2", xA, smallA, t)
                            yield

                        yield from norm("n2", xA, xnA, smallA, turned="n1", early=True)
                        v.wait_ge(pe_done, PE["router"])
                        vv.tensor_copy(lg[:, :, 0:NE], ps[:, 4, 0:T * NE].rearrange("p (t n) -> p t n", t=T)).then_inc(vec_done, V.step("logits"))
                        own_steps()
                        for t in range(T):
                            vv.max(m8[:, t, :], lg[:, t, :]).then_inc(vec_done, V.step())
                        own_steps()
                        for t in range(T):
                            vv.match_replace(lrep[:, t, :], m8[:, t, :], lg[:, t, :], NEG).then_inc(vec_done, V.step())
                        vv.tensor_tensor(ex, lg[:, :, 0:NE], m8[:, :, 6:7].broadcast_to([P, T, NE]), ALU.subtract).then_inc(vec_done, V.step("lsub"))
                        v.wait_ge(act_done, A["lexp"])
                        own_steps()
                        vv.scalar_tensor_tensor(comb, lrep[:, :, 0:NE], NEG, ex, ALU.is_equal, ALU.mult).then_inc(vec_done, V.step())
                        own_steps()
                        vv.tensor_reduce(smA[:, 0:T], comb, AX.X, ALU.add).then_inc(vec_done, V.step())
                        own_steps()
                        vv.reciprocal(riA[:, 0:T], smA[:, 0:T]).then_inc(vec_done, V.step())
                        own_steps()
                        vv.tensor_tensor(comb, comb, b16(riA[:, 0:T], NE), ALU.mult).then_inc(vec_done, V.step("comb"))
                        yield
                        def accumulate(e, half):
                            for t in (2 * half, 2 * half + 1):
                                c = (t % 2) * D
                                v.wait_ge(pe_done, PE["down", e] if half else PE["down", e, 1])
                                v.wait_ge(vec_done, V["acc", e - 1, t] if e >= 1 else V["comb"])
                                if e < NE:
                                    vv.scalar_tensor_tensor(xA[:, t, :], ps[:, 4, c:c + D], comb[:, t, e:e + 1], xA[:, t, :],
                                                            ALU.mult, ALU.add).then_inc(vec_done, V.step("acc", e, t))
                                else:
                                    vv.tensor_tensor(xA[:, t, :], ps[:, 4, c:c + D], xA[:, t, :], ALU.add).then_inc(vec_done, V.step("acc", e, t))
                        for e in range(NE + 2):
                            for f in range(4):
                                if f == 2 and e >= 1:
                                    accumulate(e - 1, 0)
                                if f == 0 and e >= 2:
                                    accumulate(e - 2, 1)
                                if f == 3 and e == NE + 1:
                                    accumulate(e - 1, 1)
                                if e <= NE:
                                    n = e * 4 + f
                                    v.wait_ge(act_done, A["silu", n])
                                    vv.tensor_tensor(hE[:, e % 2, f, :], ps[:, 2 * (f % 2) + 1, :], hE[:, e % 2, f, :], ALU.mult).then_inc(vec_done, V.step("hid", n))
                                yield

                    def back():
                        yield from norm("y0", xB, xnB, smallB)
                        for i in range(T + 2):
                            if i < T:
                                t = i
                                v.wait_ge(pe_done, PE["cs", t])
                                if t >= 2:
                                    v.wait_ge(pe_done, PE["cpT", t - 2])
                                vv.scalar_tensor_tensor(pb[:, t % 2, 0:P], ps[:, 5, 0:P], 1.0 / 16, w["causal"], ALU.mult,
                                                        ALU.add).then_inc(vec_done, V.step("cs", t))
                                own_steps()
                                vv.tensor_reduce(nm[:, t:t + 1], pb[:, t % 2, 0:P], AX.X, ALU.max, negate=True).then_inc(vec_done, V.step("cmax", t))
                            if i >= 2:
                                t = i - 2
                                v.wait_ge(act_done, A["cexp", t])
                                vv.reciprocal(ri[:, 0, t:t + 1], rs[:, t:t + 1]).then_inc(vec_done, V.step())
                                own_steps()
                                v.wait_ge(pe_done, PE["cpv", t])
                                vv.scalar_tensor_tensor(xnB[:, t, :], ps[:, 7, 0:D], ri[:, 0, t:t + 1], xnB[:, t, :], ALU.mult,
                                                        ALU.add).then_inc(vec_done, V.step("y1p", t))
                                stats("y1", xnB, smallB, t)
                            yield

                        yield from norm("y1", xnB, xnB, smallB, after=late_gain("y1", "g1"), early=True)
                        for i in range(T + 2):
                            if 1 <= i <= T:
                                t = i - 1
                                v.wait_ge(act_done, A["xexp", t])
                                if t >= 2:
                                    v.wait_ge(pe_done, PE["xpT", t - 2])
                                vv.tensor_scalar(w4[:, t % 2, :], w["blkind"], pb[:, t % 2, NK - 1:NK], None, ALU.mult).then_inc(vec_done, V.step("w4", t))
                            if i < T:
                                t = i
                                v.wait_ge(pe_done, PE["xs", t])
                                vv.tensor_reduce(nm2[:, t:t + 1], ps[:, 5, 0:NK], AX.X, ALU.max, negate=True).then_inc(vec_done, V.step())
                                own_steps()
                                vv.tensor_scalar(nm[:, t:t + 1], nm2[:, t:t + 1], 1.0 / 16, None, ALU.mult).then_inc(vec_done, V.step("xmax", t))
                            if i >= 2:
                                t = i - 2
                                if t == 0:
                                    own_steps()
                                vv.reciprocal(ri[:, 1, t:t + 1], rs[:, t:t + 1]).then_inc(vec_done, V.step())
                                own_steps()
                                v.wait_ge(pe_done, PE["xpv", t])
                                v.wait_ge(pool_done, O["y1", t])
                                vv.scalar_tensor_tensor(xnB[:, t, :], ps[:, 7, 0:D], ri[:, 1, t:t + 1], xnB[:, t, :], ALU.mult,
                                                        ALU.add).then_inc(vec_done, V.step("y2p", t))
                                stats("y2", xnB, smallB, t)
                            yield

                        def ffn(tag, ready, dst, key):
                            for _ in range(FF // P):
                                yield
                            for i in range(T + 1):
                                if i >= 1:
                                    t = i - 1
                                    v.wait_ge(pe_done, PE[tag, "f2", t])
                                    v.wait_ge(pool_done, O[ready, t])
                                    vv.tensor_tensor(dst[:, t, :], ps[:, (7, 5)[t % 2], 0:D], dst[:, t, :], ALU.add).then_inc(vec_done, V.step(tag, "f2", t))
                                    stats("y3" if tag == "y2" else "n5", dst, smallB, t)
                                yield

                        yield from norm("y2", xnB, xnB, smallB, after=late_gain("y2", "g2"), early=True)
                        yield from ffn("y2", "y2b", xnB, None)
                        yield from norm("y3", xnB, xnB, smallB, gain="g3", slots=2, early=True)
                        for t in range(T):
                            v.wait_ge(pool_done, O["xbe3", t])
                            v.wait_ge(vec_done, V["y3", "g", t])
                            vv.tensor_tensor(xB[:, t, :], xB[:, t, :], xnB[:, t, :], ALU.add).then_inc(vec_done, V.step("x4", t))
                        yield

                        yield from norm("z", xB, xnB, smallB, slots=2)
                        def before_h1():
                            v.wait_ge(pe_done, PE["xpv", T - 1])
                            wait_scaled(v, "z", T - 1)
                        yield from norm("h1", xnB, hh, smallB, before=before_h1)
                        def scores(t, c):
                            v.wait_ge(act_done, A["qkv", t])
                            if c == 0:
                                v.wait_ge(pe_done, PE["h1", "T", T - 1])
                            if c % 2 == 0:
                                own_steps()
                                qk_product(vv, t, c).then_inc(vec_done, V.step())
                                own_steps()
                            else:
                                v.wait_ge(pool_done, O["dprod", t, c])
                            vv.tensor_reduce(sc[:, t % 2, c * 256:(c + 1) * 256],
                                             prod[:, c % 2, :].rearrange("p (n d) -> p n d", d=8), AX.X,
                                             ALU.add).then_inc(vec_done, V.step("dred", t, c))

                        def less_maximum(t):
                            s2 = sc[:, t % 2, :]
                            s3 = s2.rearrange("p (q k) -> p q k", q=32)
                            own_steps()
                            vv.tensor_scalar(s2, s2, FMAX, -FMAX, ALU.min, ALU.max).then_inc(vec_done, V.step())
                            own_steps()
                            vv.tensor_reduce(sm[:, t % 2, :], s3, AX.X, ALU.max).then_inc(vec_done, V.step())
                            own_steps()
                            vv.tensor_tensor(s3, s3, b16(sm[:, t % 2, :], 32), ALU.subtract).then_inc(vec_done, V.step("dsub", t))

                        def weights(t):
                            aa = a2[:, t % 2, :].rearrange("p (a h) -> p a h", a=16)
                            v.wait_ge(act_done, A["dexp2", t])
                            s3 = sc[:, t % 2, :].rearrange("p (q k) -> p q k", q=32)
                            vv.tensor_reduce(sm[:, t % 2, :], s3, AX.X, ALU.add).then_inc(vec_done, V.step())
                            own_steps()
                            vv.reciprocal(ri[:, t % 2, :], sm[:, t % 2, :]).then_inc(vec_done, V.step())
                            own_steps()
                            vv.tensor_scalar(ri[:, t % 2, 16:32], ri[:, t % 2, 16:32], neglam, None, ALU.mult).then_inc(vec_done, V.step())
                            if t >= 2:
                                v.wait_ge(pool_done, O["pprod", t - 2])
                            vv.tensor_tensor(aa, s3[:, 0:16, 0:16], b16(ri[:, t % 2, 0:16], 16), ALU.mult).then_inc(vec_done, V.step())
                            own_steps()
                            e1 = s3[:, 16:32, 16:32]
                            vv.tensor_tensor(e1, e1, b16(ri[:, t % 2, 16:32], 16), ALU.mult).then_inc(vec_done, V.step())
                            own_steps()
                            vv.tensor_tensor(aa, aa, e1, ALU.add).then_inc(vec_done, V.step("datt", t))

                        def values(t):
                            own_steps()
                            pv_product(vv, t, 0).then_inc(vec_done, V.step("pprod", t))
                            own_steps()
                            if t >= 2:
                                v.wait_ge(pe_done, PE["l4", "oT", t - 2])
                            output(t, 0, prod[:, 0, :])

                        def output(t, j, products):
                            vv.tensor_reduce(ob[:, t % 2, j * 128:(j + 1) * 128], products.rearrange("p (n h) -> p n h", h=16),
                                             AX.X, ALU.add).then_inc(vec_done, V.step("pred", t, j))

                        def mean_squares(t):
                            v.wait_ge(pool_done, O["pprod", t])
                            output(t, 1, prodV)
                            own_steps()
                            vv.tensor_tensor(a2[:, t % 2, :], ob[:, t % 2, :], ob[:, t % 2, :], ALU.mult).then_inc(vec_done, V.step())
                            own_steps()
                            vv.tensor_reduce(mx[:, t % 2, 0:16], a2[:, t % 2, :].rearrange("p (a d) -> p a d", a=16), AX.X,
                                             ALU.add).then_inc(vec_done, V.step())
                            own_steps()
                            vv.tensor_scalar(mx[:, t % 2, 16:32], mx[:, t % 2, 0:16], RMS / 16, EPS * RMS, ALU.mult,
                                             ALU.add).then_inc(vec_done, V.step("rms", t))

                        for i in range(T + 2):
                            tile, before = i < T, 1 <= i <= T
                            if tile:
                                scores(i, 0)
                            yield
                            if before:
                                weights(i - 1)
                            yield
                            if tile:
                                scores(i, 1)
                            yield
                            if before:
                                values(i - 1)
                            yield
                            if tile:
                                scores(i, 2)
                            yield
                            if before:
                                mean_squares(i - 1)
                            yield
                            if tile:
                                scores(i, 3)
                                less_maximum(i)
                            yield
                            if before:
                                t = i - 1
                                v.wait_ge(pool_done, O["rms", t])
                                o3 = ob[:, t % 2, :].rearrange("p (a d) -> p a d", a=16)
                                vv.tensor_tensor(o3, o3, b16(mx[:, t % 2, 0:16], 16), ALU.mult).then_inc(vec_done, V.step("l4", "o", t))
                            if i >= 2:
                                t = i - 2
                                v.wait_ge(pe_done, PE["l4", "wo", t])
                                v.wait_ge(pool_done, O["zb", t])
                                vv.tensor_tensor(xnB[:, t, :], ps[:, 7, 0:D], xnB[:, t, :], ALU.add).then_inc(vec_done, V.step("conn", t))
                                stats("h2", xnB, smallB, t)
                            yield
                        yield from norm("h2", xnB, hh, smallB, early=True)
                        yield from ffn("h2", "xc", xB, None)

                        yield from norm("n5", xB, xnB, smallB, early=True)
                        for i in range(T + 1):
                            if i < T:
                                t = i
                                v.wait_ge(pe_done, PE["sim", t])
                                own_steps()
                                sim = ps[:, 5:7, :].rearrange("p s (a k) -> p (s a) k", a=8)
                                for a in range(NPH):
                                    vv.max(s16[:, a, 0:8], sim[:, a, :]).then_inc(vec_done, V.step())
                            yield
                            if i < T:
                                for a in range(NPH):
                                    v.wait_ge(vec_done, V.n - NPH + 1)
                                    vv.match_replace(rep64[:, a, :], s16[:, a, 0:8], sim[:, a, :], NEG).then_inc(
                                        vec_done, V.step(*(("rep64", t) if a == NPH - 1 else ())))
                            yield
                            if i < T:
                                for a in range(NPH):
                                    v.wait_ge(vec_done, V.n - NPH + 1)
                                    vv.max(s16[:, a, 8:16], rep64[:, a, :]).then_inc(vec_done, V.step())
                            yield
                            if i >= 1:
                                t = i - 1
                                v.wait_ge(pe_done, PE["up", t])
                                vv.tensor_tensor(xnB[:, t, :], ps[:, 7, 0:D], xB[:, t, :], ALU.add).then_inc(vec_done, V.step("x6", t))
                            if i < T:
                                t = i
                                own_steps()
                                sx, sy = s16[:, 0:8, :], s16[:, 8:16, :]
                                off = 0
                                for a0, a1 in ((0, 1), (1, 2), (2, 3), (3, 4), (4, 5), (5, 8), (8, 16)):
                                    na, nb = a1 - a0, TOP // a1
                                    c4 = cand[:, :, off:off + na * nb].rearrange("p h (a b) -> p h a b", a=na)
                                    vv.tensor_tensor(c4, sx[:, :, a0:a1].unsqueeze(3).broadcast_to([P, 8, na, nb]),
                                                     sy[:, :, 0:nb].unsqueeze(2).broadcast_to([P, 8, na, nb]),
                                                     ALU.add).then_inc(vec_done, V.step())
                                    off += na * nb
                                assert off == NP
                            yield
                            if i < T:
                                own_steps()
                                for h in range(8):
                                    vv.max(cm[:, h, :], cand[:, h, :]).then_inc(vec_done, V.step())
                                own_steps()
                                vv.tensor_tensor(cexp[:, t % 2], cand, cm[:, :, 0:1].broadcast_to([P, 8, NP]), ALU.subtract).then_inc(vec_done, V.step("csub", t))
                                for h in range(8):
                                    vv.match_replace(rep1[:, h, :], cm[:, h, :], cand[:, h, :], NEG).then_inc(vec_done, V.step())
                            yield
                            if i < T:
                                t = i
                                for h in range(8):
                                    v.wait_ge(vec_done, V.n - 7)
                                    vv.max(cm2[:, h, :], rep1[:, h, :]).then_inc(vec_done, V.step())
                                for h in range(8):
                                    v.wait_ge(vec_done, V.n - 7)
                                    vv.match_replace(rep2[:, h, :], cm2[:, h, :], rep1[:, h, :], NEG).then_inc(vec_done, V.step())
                            yield
                            if i < T:
                                own_steps()
                                v.wait_ge(act_done, A["cexp2", t])
                                cflat = cexp[:, t % 2].rearrange("p h n -> p (h n)")
                                vv.scalar_tensor_tensor(cflat, rep2.rearrange("p h n -> p (h n)"), NEG, cflat, ALU.is_equal, ALU.mult).then_inc(vec_done, V.step())
                                own_steps()
                                vv.tensor_reduce(sm[:, 0, 0:8], cexp[:, t % 2], AX.X, ALU.add).then_inc(vec_done, V.step())
                                own_steps()
                                vv.reciprocal(ri[:, 0, 0:8], sm[:, 0, 0:8]).then_inc(vec_done, V.step())
                                own_steps()
                                vv.tensor_tensor(cexp[:, t % 2], cexp[:, t % 2], b16(ri[:, 0, 0:8], NP), ALU.mult).then_inc(vec_done, V.step())
                                own_steps()
                                vv.tensor_reduce(phd[:, t % 2, :], cexp[:, t % 2].rearrange("p h n -> p n h"), AX.X, ALU.add).then_inc(vec_done, V.step())
                                own_steps()
                                if t >= 2:
                                    v.wait_ge(pe_done, PE["uT", t - 2])
                                v.wait_ge(act_done, A["g50"])
                                vv.tensor_tensor(u50[:, t % 2, :], phd[:, t % 2, :], g50[:, t * NP:(t + 1) * NP], ALU.mult).then_inc(vec_done, V.step("u50", t))
                            yield

                    run(front(), back())
                    if "f" in streams:
                        own_steps()
                        vv.tensor_copy(xB, xA).then_inc(vec_done, V.step())

            nc.gpsimd.sem_clear(range(first, last + 1))
            nc.all_engine_barrier()

        group(0, "f")
        with nc.Fori(1, G) as g:
            group(g, "fb")
        group(G, "b")


def lay_out(a):
    def kmaj(wt):
        k, n = wt.shape
        return wt.reshape(k // P, P, n).transpose(1, 0, 2).reshape(P, -1)

    def row(b):
        return np.broadcast_to(b.reshape(1, -1), (P, b.size))

    def col(b):
        return b.reshape(-1, P).T

    i = np.arange(P)
    blk = (i[:, None] // S) == (i[None, :] // S)
    out = {
        "wq0": kmaj(a["L0_xattn_Wq"].T), "wk0": kmaj(a["L0_xattn_Wk"].T), "wv0": kmaj(a["L0_xattn_Wv"].T),
        "wo0": kmaj(a["L0_xattn_Wo"].T), "bq0": col(a["L0_xattn_bq"]), "bk0": col(a["L0_xattn_bk"]),
        "bv0": col(a["L0_xattn_bv"]),
        "bo01": row(np.concatenate([a["L0_xattn_bo"], a["L0_attn_bo"]])),
        "wv1": kmaj(np.concatenate([a["L0_attn_wv"], a["L0_attn_w3d"]]).T), "wo1": kmaj(a["L0_attn_wo"].T),
        "bv1": col(a["L0_attn_bv"]), "b3d": row(a["L0_attn_b3d"]),
        "router": kmaj(a["L0_ffn_router_w"].T),
        "w1x": kmaj(a["L1_xattn_w1"]), "b1x": col(a["L1_xattn_b1"]), "w2x": kmaj(a["L1_xattn_w2"]),
        "b2x": row(a["L1_xattn_b2"]), "g1": row(a["L1_xattn_g1"]), "be1": row(a["L1_xattn_beta1"]),
        "g2": row(a["L1_xattn_g2"]), "be2": row(a["L1_xattn_beta2"]), "g3": row(a["L1_xattn_g3"]),
        "be3": row(a["L1_xattn_beta3"]),
        "wqkv": kmaj(np.concatenate([a["L1_attn_Wq"].reshape(16, 8, 2, D).transpose(2, 0, 1, 3).reshape(D, D),
                                     a["L1_attn_Wk"].reshape(16, 8, 2, D).transpose(2, 0, 1, 3).reshape(D, D),
                                     a["L1_attn_Wv"].reshape(16, 16, D).transpose(1, 0, 2).reshape(D, D)]).T),
        "wo2": kmaj(a["L1_attn_Wo"].T), "bo2": row(a["L1_attn_bo"]),
        "lg1": col(a["L1_attn_ln1_g"]), "lb1": col(a["L1_attn_ln1_b"]), "lg2": col(a["L1_attn_ln2_g"]),
        "lb2": col(a["L1_attn_ln2_b"]), "g1c": col(a["L1_xattn_g1"]), "be1c": col(a["L1_xattn_beta1"]),
        "g2c": col(a["L1_xattn_g2"]), "be2c": col(a["L1_xattn_beta2"]), "w1a": kmaj(a["L1_attn_W1"].T), "b1a": col(a["L1_attn_b1"]),
        "w2a": kmaj(a["L1_attn_W2"].T), "b2a": row(a["L1_attn_b2"]),
        "lqk": row(np.concatenate([a["L1_attn_" + n] for n in ("lq1", "lq2", "lk1", "lk2")])),
        "ident": np.eye(P), "headmask": (i[:, None] // H) == (i[None, :] // H), "blockones": blk,
        "causalT": blk & (i[None, :] >= i[:, None]), "causal": np.where(blk & (i[None, :] <= i[:, None]), 0.0, -1e30),
        "eye32": (i[:, None] % S) == np.arange(S)[None, :], "blkind": (i[:, None] // S) == np.arange(BT)[None, :],
        "wqp": a["L1_ffn_Wq"].reshape(NPH, P, D).transpose(1, 0, 2).reshape(P, -1),
        "keysp": a["L1_ffn_keys"].transpose(3, 2, 0, 1).reshape(P, -1),
    }
    rows = [p * TOP + q for p, q in PAIRS]
    out["wd50"] = kmaj(a["L1_ffn_W_down"][rows].T)
    wu = np.zeros((P, D), np.float32)
    wu[:NP] = a["L1_ffn_W_up"][rows]
    out["wu50"] = wu
    gate = [*a["L0_ffn_eg"], a["L0_ffn_sg"]]
    up = [*a["L0_ffn_eu"], a["L0_ffn_su"]]
    down = [*a["L0_ffn_ed"], a["L0_ffn_sd"]]
    out["experts"] = np.concatenate([np.concatenate([kmaj(x.T), kmaj(y.T), kmaj(z.T)], 1) for x, y, z in zip(gate, up, down)])
    out["x"] = a["x"].reshape(G, T, P, D).transpose(0, 2, 1, 3).reshape(G * P, T * D)
    order = [h + H * l for h in range(H) for l in range(NK // H)]
    c = a["ctx_1024"].reshape(G, T, BT, NK, D)
    cp = c[:, :, :, order + [NK - 1], :]
    out["ctxT"] = cp.reshape(G, T, BT, NK, KT, P).transpose(0, 5, 1, 4, 2, 3).reshape(G * P, -1)
    out["ctxN"] = c[:, :, :, order, :].reshape(G, T, BT, 2, P, D).transpose(0, 4, 1, 3, 2, 5).reshape(G * P, -1)
    out["ctxL"] = c[:, :, :, NK - 1, :].transpose(0, 2, 1, 3).reshape(G * BT, -1)
    return {k: np.ascontiguousarray(x, dtype=np.float32) for k, x in out.items()}


def kernel(**inputs):
    import concourse.bacc as bacc
    from concourse.bass_utils import run_bass_kernel_spmd

    arrays = lay_out({k: np.asarray(x) for k, x in inputs.items()})
    marks = {}
    for _ in range(2):
        nc = bacc.Bacc("TRN2", target_bir_lowering=False, num_devices=1)
        dram = {k: nc.dram_tensor("in_" + k, x.shape, F32, kind="ExternalInput").ap() for k, x in arrays.items()}
        dram["out"] = nc.dram_tensor("out_0", (G * P, T * D), F32, kind="ExternalOutput").ap()
        build(nc, marks, dram)
    r = run_bass_kernel_spmd(nc, [{"in_" + k: x for k, x in arrays.items()}], core_ids=[0])
    y = r.results[0]["out_0"]
    return y.reshape(G, P, T, D).transpose(0, 2, 1, 3).reshape(NB, S, D)
```
